# Optimizing a Trainium2 kernel written in Bass

```python
import numpy as np
import jax
import jax.numpy as jnp

def _softmax(x, axis=-1):
    return jax.nn.softmax(x, axis=axis)

def _gelu(x):
    return jax.nn.gelu(x, approximate=True)

def _silu(x):
    return jax.nn.silu(x)

def _sigmoid(x):
    return jax.nn.sigmoid(x)

def _layernorm(x, axis=-1, eps=1e-05):
    m = jnp.mean(x, axis=axis, keepdims=True)
    v = jnp.var(x, axis=axis, keepdims=True)
    return (x - m) / jnp.sqrt(v + eps)

def _scatter_add(tgt, idx, src, axis=0):
    return tgt.at[idx].add(src)

def _segment_sum(src, seg, n):
    return jax.ops.segment_sum(src, seg, n)
kernel_name = 'mk_seq_postln_d1_jaxref_r4_d54b74'

def setup_inputs(seed: int=0):
    np.random.seed(seed)
    _w = jnp.asarray

    def _L0_attn_setup():
        import jax, jax.numpy as jnp
        import numpy as np
        DIM = 256
        B, N = (8, 1024)
        EPS = 1e-06
        key = jax.random.key(seed)
        k1, k2, k3, k4 = jax.random.split(key, 4)
        x = jax.random.normal(k1, (B, N, DIM), dtype=jnp.float32)
        s = 1.0 / np.sqrt(DIM)
        W_qkv = jax.random.uniform(k2, (3 * DIM, DIM), jnp.float32, -s, s)
        W_out = jax.random.uniform(k3, (DIM, DIM), jnp.float32, -s, s)
        b_out = jax.random.uniform(k4, (DIM,), jnp.float32, -s, s)
        return {'x': x, 'W_qkv': W_qkv, 'W_out': W_out, 'b_out': b_out}
    _L0_attn_in = _L0_attn_setup()

    def _L0_ffn_setup():
        import jax, jax.numpy as jnp
        import numpy as np
        B, T, D, E, H, K = (4, 512, 256, 8, 512, 2)
        key = jax.random.key(seed)
        k0, k1, k2, k3 = jax.random.split(key, 4)
        x = jax.random.normal(k0, (B, T, D), dtype=jnp.float32)
        router_w = jax.random.normal(k1, (E, D), dtype=jnp.float32) * D ** (-0.5)
        w1 = jax.random.normal(k2, (E, D, H), dtype=jnp.float32) * D ** (-0.5)
        w2 = jax.random.normal(k3, (E, H, D), dtype=jnp.float32) * H ** (-0.5)
        return {'x': x, 'router_w': router_w, 'w1': w1, 'w2': w2}
    _L0_ffn_in = _L0_ffn_setup()
    _d = {'L0_attn_x': _L0_attn_in['x'], 'L0_attn_W_qkv': _L0_attn_in['W_qkv'], 'L0_attn_W_out': _L0_attn_in['W_out'], 'L0_attn_b_out': _L0_attn_in['b_out'], 'L0_ffn_router_w': _L0_ffn_in['router_w'], 'L0_ffn_w1': _L0_ffn_in['w1'], 'L0_ffn_w2': _L0_ffn_in['w2']}
    _x0 = _d['L0_attn_x']
    _d['L0_attn_x'] = jax.random.normal(jax.random.fold_in(jax.random.key(seed), 1), (2, 4096, 256), dtype=_x0.dtype)
    del _x0
    return _d

def reference(L0_attn_x, L0_attn_W_qkv, L0_attn_W_out, L0_attn_b_out, L0_ffn_router_w, L0_ffn_w1, L0_ffn_w2):

    def _L0_attn_ref(x, W_qkv, W_out, b_out):
        import jax, jax.numpy as jnp
        import numpy as np
        DIM = 256
        B, N = (8, 1024)
        EPS = 1e-06
        qkv = jnp.einsum('bnd,ed->bne', x, W_qkv)
        q, k, v = jnp.split(qkv, 3, axis=-1)
        q = jax.nn.relu(q) + EPS
        k = jax.nn.relu(k) + EPS
        kv = jnp.einsum('bnd,bne->bde', k, v)
        z = 1.0 / (jnp.einsum('bnd,bd->bn', q, k.sum(axis=1)) + EPS)
        attn = jnp.einsum('bnd,bde,bn->bne', q, kv, z)
        return jnp.einsum('bne,fe->bnf', attn, W_out) + b_out

    def _L0_ffn_ref(x, router_w, w1, w2):
        import jax, jax.numpy as jnp
        import numpy as np
        B, T, D, E, H, K = (4, 512, 256, 8, 512, 2)
        Bb, Tt, Dd = x.shape
        N = Bb * Tt
        logits = jnp.einsum('btd,ed->bte', x, router_w)
        top_vals, top_idx = jax.lax.top_k(logits, K)
        top_w = jax.nn.softmax(top_vals, axis=-1)
        xf = x.reshape(N, Dd)
        h = jnp.einsum('nd,edh->enh', xf, w1)
        h = jnp.square(jax.nn.relu(h))
        y = jnp.einsum('enh,ehd->end', h, w2)
        idx_f = top_idx.reshape(N, K)
        w_f = top_w.reshape(N, K)
        y_sel = y[idx_f, jnp.arange(N)[:, None]]
        out = jnp.einsum('nk,nkd->nd', w_f, y_sel)
        return out.reshape(Bb, Tt, Dd)
    x = L0_attn_x
    x = _layernorm(x + _L0_attn_ref(x, L0_attn_W_qkv, L0_attn_W_out, L0_attn_b_out), axis=-1)
    x = _layernorm(x + _L0_ffn_ref(x, L0_ffn_router_w, L0_ffn_w1, L0_ffn_w2), axis=-1)
    return x

_drawn_inputs = setup_inputs


def setup_inputs(seed=0):
    import zlib

    import numpy as np

    out = dict(_drawn_inputs(seed))
    spreads = {}
    factors = {}
    for name, (base, spread) in spreads.items():
        noise = np.random.default_rng([zlib.crc32(name.encode()), seed]).standard_normal(out[name].shape)
        drawn = base * np.exp(spread * noise) if base else spread * noise
        out[name] = jnp.asarray(drawn.astype(out[name].dtype))
    for name, factor in factors.items():
        out[name] = (out[name] * factor).astype(out[name].dtype)
    return out
```

```python
import concourse.bass as bass
from concourse import mybir
from contextlib import ExitStack


def linear_attention_then_top2_experts(nc, x_in, w_qkv, w_out, b_out, router_w, w1_in, w2_in, out):
    f32, f16, bf16, i32 = mybir.dt.float32, mybir.dt.float16, mybir.dt.bfloat16, mybir.dt.int32
    ALU = mybir.AluOpType
    ACT = mybir.ActivationFunctionType
    AX = mybir.AxisListType
    ds = bass.ds

    P = 128
    B, T, D = x_in.shape
    E, _, H = w1_in.shape
    DC, HC = D // P, H // P
    NT = T // P
    GT = 4
    NG = NT // GT
    ST = 2 * NT + E
    NS = B * ST
    DR = D + E
    DEN = DR
    ROW = D + 4
    EPS, EPS_LN = 1e-6, 1e-5
    XS = 2048.0
    R_SCALE = 2.0 ** -27
    TINY = 2.0 ** -100
    FAR = float(1 << 20)

    xf = x_in.rearrange("b (n p) d -> p (b n) d", p=P)
    of = out.rearrange("b (n p) d -> p (b n) d", p=P)
    x_slots = nc.dram_tensor("x_slots", (NS * P, ROW), f32, kind="Internal").ap()
    y_rows = nc.dram_tensor("y_rows", (2 * B * T, D), f32, kind="Internal").ap()
    xs_v = x_slots.rearrange("(j p) c -> p j c", p=P)
    yr_v = y_rows.rearrange("(k n p) d -> p k n d", k=2, p=P)

    ctx = ExitStack()
    with ctx:
        def sb(name, shape, dt):
            return ctx.enter_context(nc.sbuf_tensor(name, shape, dt))

        def sem(name):
            return ctx.enter_context(nc.semaphore(name))

        X = sb("X", [P, B * NT, ROW], f32)
        XH = X[:, :, :].bitcast(f16)
        W1 = sb("W1", [P, E, DC, 2, H], f16)
        W2 = sb("W2", [P, E, HC, 2, D], f16)
        W1f = W1[:, :, :, :, :].rearrange("p e c s h -> p (e c s h)")
        W2f = W2[:, :, :, :, :].rearrange("p e c s h -> p (e c s h)")
        STG = sb("STG", [P, 2, 1024], f32)
        Qb = sb("Qb", [P, DC * T], f32)
        Q = Qb[:, :].rearrange("p (c t) -> p c t", c=DC)
        RAW = Qb[:, 0:8 * D].rearrange("p (a d) -> p a d", a=8)
        XT = sb("XT", [P, 2, DC, GT * P], f32)
        KS = sb("KS", [P, 2, GT, D], f32)
        WKR = sb("WKR", [P, DC, DR], f32)
        WQT = sb("WQT", [P, DC, D], f32)
        WOT = Qb[:, 2048:2048 + DC * DR].rearrange("p (c d) -> p c d", c=DC)
        G = sb("G", [P, DC, DR], f32)
        RT = sb("RT", [P, DC, E], f32)
        RR = Qb[0:E, 2624:2624 + D]
        MQ = sb("MQ", [P, DC, DR + 2], f32)
        KXS = sb("KXS", [P, DC, D + 2], f32)
        KXT = KS[:, 0, 0:DC, :]
        ID = sb("ID", [P, P], f32)
        ID16 = sb("ID16", [P, P], f16)
        UPPER = sb("UPPER", [P, P], bf16)
        ONESB = sb("ONESB", [P, P], bf16)
        ZERO = sb("ZERO", [P, D + 2], f32)
        BB = sb("BB", [P, D], f32)
        BCOL = sb("BCOL", [P, DC], f32)
        LB = Qb[:, 3072:3072 + 2 * D].rearrange("p (n c k) -> p n c k", n=2, c=DC)
        SRBR = sb("SRBR", [P, 2, E], f32)
        PADROW = sb("PADROW", [P, ROW], f32)
        XR = sb("XR", [P, NT, E], f32)
        LG = sb("LG", [P, NT, E], f32)
        MEAN = sb("MEAN", [P, NT], f32)
        VAR = sb("VAR", [P, NT], f32)
        SD = sb("SD", [P, NT], f32)
        RSTD = sb("RSTD", [P, NT], f32)
        ZT = sb("ZT", [P, 2, GT], f32)
        ZR = sb("ZR", [P, 2, GT], f32)
        ST6 = sb("ST6", [P, 2, GT, 6], f32)
        MV = sb("MV", [P, 2, GT, 2], f32)
        NW = sb("NW", [P, 4, GT], f32)
        RS2 = sb("RS2", [P, 2, GT], f32)
        NB = sb("NB", [P, 2, GT], f32)
        AM = sb("AM", [P, 2], f32)
        AMX = sb("AMX", [P, 2], f32)
        P2 = sb("P2", [P, E, 2], f32)
        PW = sb("PW", [P, 2], f32)
        SG = sb("SG", [P, 2, 2], f32)
        KAP = sb("KAP", [P, E], f32)
        XTW = XT[:, :, :, :].rearrange("p u c t -> p (u c t)")
        TN = NT * E
        TA = XTW[:, 0:TN].rearrange("p (t e) -> p t e", e=E)
        TB = XTW[:, TN:2 * TN].rearrange("p (t e) -> p t e", e=E)
        OH = XTW[:, 2 * TN:4 * TN].rearrange("p (k t e) -> p k t e", k=2, e=E)
        MK = sb("MK", [P, E, NT], bf16)
        ONES = sb("ONES", [P, E * NT], f32)
        SI = XTW[:, 4 * TN:5 * TN].rearrange("p (e t) -> p e t", e=E)
        SX = XTW[:, 5 * TN:6 * TN].rearrange("p (e t) -> p e t", e=E)
        SMALL = XTW[:, 6 * TN:6 * TN + 12 * NT].rearrange("p (k t) -> p k t", t=NT)
        MX, CM, SL, GA = SMALL[:, 0:2, :], SMALL[:, 2:4, :], SMALL[:, 4:6, :], SMALL[:, 6:12, :]
        IDX = sb("IDX", [P, B, 2, NT], i32)
        CNT = sb("CNT", [P, E], f32)
        CI = sb("CI", [P, E], i32)
        NTL = sb("NTL", [P, E], f32)
        TBI = sb("TBI", [P, E], f32)
        TBX = sb("TBX", [P, E], f32)
        OFF = sb("OFF", [P, E], f32)
        PD = sb("PD", [P, 3, E], f32)
        PIDX = sb("PIDX", [P, B, E], i32)
        CMP = KS[:, :, :, :].rearrange("p u t d -> p (u t d)")[:, 0:ST * E].rearrange("p (j e) -> p j e", e=E)
        EIDF = sb("EIDF", [P, NS], f32)
        EID = sb("EID", [P, NS], i32)
        REV = sb("REV", [P, E], f32)
        TOK = sb("TOK", [P, B * NT], f32)
        JROW = sb("JROW", [P, ST], f32)
        PCOL = sb("PCOL", [P, 1], f32)
        MT = sb("MT", [P, 2, 2], f32)
        YID = sb("YID", [P, 4, 1], i32)
        GATE = sb("GATE", [P, 4], f32)
        cut = [0]

        def region(words):
            a = cut[0]
            cut[0] += words
            return Qb[:, a:a + words]

        XG = region(4 * ROW).rearrange("p (j c) -> p j c", j=4)
        XGH = XG.bitcast(f16)
        XTF = region(2 * DC * P).bitcast(f16).rearrange("p (u s) -> p u s", u=2)
        RL = region(2 * H).rearrange("p (u h) -> p u h", u=2)
        H32 = region(2 * H).rearrange("p (u h) -> p u h", u=2)
        HHL = region(2 * H).bitcast(f16).rearrange("p (u s h) -> p u s h", u=2, s=2)
        YS = region(4 * D).rearrange("p (j d) -> p j d", j=4)
        C6 = region(4 * 6).rearrange("p (u d) -> p u d", u=4)
        CV = region(4 * 2).rearrange("p (u d) -> p u d", u=4)
        CW = region(4 * 8).rearrange("p (u d) -> p u d", u=4)
        YG = KS[:, :, :, :].rearrange("p u t d -> p (u t d)").rearrange("p (u k d) -> p u k d", u=4, k=2)
        SF = XTW[:, 0:4 * D].rearrange("p (u d) -> p u d", u=4)
        OF = XTW[:, 4 * D:8 * D].rearrange("p (u d) -> p u d", u=4)
        assert cut[0] <= DC * T

        PS = ctx.enter_context(nc.psum_tensor("PS", [P, 8, 512], f32))
        PS16 = PS[:, :, :].bitcast(f16)

        s_raw, s_bias = sem("s_raw"), sem("s_bias")
        s_x = [sem(f"s_x{i}") for i in range(4)]
        s_w = [sem(f"s_w{i}") for i in range(2)]
        s_tail = sem("s_tail")
        const_done, pool_chain, setup_chain = sem("const_done"), sem("pool_chain"), sem("setup_chain")
        set_mm, set_ev = sem("set_mm"), sem("set_ev")
        xt_mm, xt_ev, k_mm, k_ev, q_mm, q_ev, kx_mm, b_add = (sem(n) for n in (
            "xt_mm", "xt_ev", "k_mm", "k_ev", "q_mm", "q_ev", "kx_mm", "b_add"))
        m_mm, m_ev = sem("m_mm"), sem("m_ev")
        w_max, w_all, w_scale, w_hi, w_lo, w_step = (sem(n) for n in ("w_max", "w_all", "w_scale", "w_hi", "w_lo", "w_step"))
        u_mm, z_step, x2_done, st_step, var_rdy, sd_rdy, nw_step, rs_rdy, x1_rdy, hi_rdy, lo_rdy = (sem(n) for n in (
            "u_mm", "z_step", "x2_done", "st_step", "var_rdy", "sd_rdy", "nw_step", "rs_rdy", "x1_rdy", "hi_rdy", "lo_rdy"))
        r_step, ex_in, ex_out, mask_rdy, cnt_mm, r_done = (sem(n) for n in (
            "r_step", "ex_in", "ex_out", "mask_rdy", "cnt_mm", "r_done"))
        s_scat = [sem(f"s_scat{b}") for b in range(B)]
        s_g = [sem(f"s_g{i}") for i in range(2)]
        t_mm, t_ev, z_mm, z_ev, rt_mm, sq_ev, h_cp, h_ev, y_mm, y_ev, meta, meta_step = (sem(n) for n in (
            "t_mm", "t_ev", "z_mm", "z_ev", "rt_mm", "sq_ev", "h_cp", "h_ev", "y_mm", "y_ev", "meta", "meta_step"))
        s_y = [sem(f"s_y{i}") for i in range(4)]
        s_yg = [sem(f"s_yg{i}") for i in range(4)]
        s_o = [sem(f"s_o{i}") for i in range(4)]
        c_step, c_var, c_sd, cn_step, c_rs, c_out = (sem(n) for n in ("c_step", "c_var", "c_sd", "cn_step", "c_rs", "c_out"))
        kap_step = sem("kap_step")

        block = ctx.enter_context(nc.Block())

        def each_group(eng, b, body):
            first = 0
            if b == 0:
                body(0, 0)
                body(1, 1)
                first = 1
            with eng.Fori(first, NG // 2) as i:
                for u in range(2):
                    body(i * 2 + (b * NG + u), u)

        @block.sync
        def _(sp):
            sp.dma_start(RAW[:, 0:6, :], w_qkv.rearrange("(a p) d -> p a d", p=P)).then_inc(s_raw, 16)
            sp.dma_start(RAW[:, 6:8, :], w_out.rearrange("(a p) d -> p a d", p=P)).then_inc(s_raw, 16)
            sp.dma_start(RR[:, :], router_w).then_inc(s_raw, 16)
            for g in range(4):
                sp.dma_start(X[:, g * GT:(g + 1) * GT, 0:D], xf[:, g * GT:(g + 1) * GT, :]).then_inc(s_x[g], 16)
            sp.dma_start(BCOL[:, :], b_out.rearrange("(c p) -> p c", p=P), allow_slow_non_contiguous=True).then_inc(s_bias, 16)
            sp.dma_start(BB[:, :], b_out.rearrange("(o d) -> o d", o=1).broadcast_to([P, D])).then_inc(s_bias, 16)

            sp.wait_ge(const_done, 1)
            for b in range(B):
                for j in range(E):
                    sp.dma_start(xs_v[:, b * ST + 2 * NT + j, :], PADROW[:, :]).then_inc(s_tail, 16)

            def load_expert(e, first):
                if not first:
                    sp.wait_ge(w_lo, 2 * e - 1)
                    sp.wait_ge(w_hi, 2 * e - 1)
                sp.dma_start(STG[:, 0, :].rearrange("p (c h) -> p c h", c=DC),
                             w1_in[ds(e, 1), :, :].rearrange("o (c p) h -> p (o c) h", p=P)).then_inc(s_w[0], 16)
                if not first:
                    sp.wait_ge(w_lo, 2 * e)
                    sp.wait_ge(w_hi, 2 * e)
                sp.dma_start(STG[:, 1, :].rearrange("p (c h) -> p c h", c=HC),
                             w2_in[ds(e, 1), :, :].rearrange("o (c p) h -> p (o c) h", p=P)).then_inc(s_w[1], 16)

            load_expert(0, True)
            with sp.Fori(1, 4) as i:
                for k in range(4):
                    sp.wait_ge(s_x[k], i * 16)
                    gi = i * 4 + k
                    sp.dma_start(X[:, ds(gi * GT, GT), 0:D], xf[:, ds(gi * GT, GT), :]).then_inc(s_x[k], 16)
            with sp.Fori(1, E) as e:
                load_expert(e, False)

            sp.wait_ge(s_scat[0], 16 * (2 * NT + E))
            sp.wait_ge(u_mm, B * NT)

            def load_pair(j, v, wait=True):
                if wait:
                    sp.wait_ge(meta, j - 1)
                sp.dma_start(XG[:, 2 * v:2 * v + 2, :], xs_v[:, ds(j * 2, 2), :]).then_inc(s_g[v], 16)

            load_pair(0, 0, False)
            load_pair(1, 1, False)
            with sp.Fori(1, ST // 4) as i:
                for v in range(2):
                    load_pair(i * 2 + v, v)
            sp.wait_ge(s_scat[1], 16 * (2 * NT + E))

            def load_rows(n, u, wait=True):
                if wait:
                    sp.wait_ge(c_step, n * 5 - 17)
                sp.dma_start(YG[:, u, :, :], yr_v[:, :, ds(n, 1), :].rearrange("p k o d -> p k (o d)")).then_inc(s_yg[u], 16)

            def store_rows(n, u):
                sp.wait_ge(c_out, n + 1)
                sp.dma_start(of[:, ds(n, 1), :].rearrange("p o d -> p (o d)"), OF[:, u, :]).then_inc(s_o[u], 16)

            Q1 = ST // 2
            load_pair(Q1, 0)
            load_pair(Q1 + 1, 1)
            load_pair(Q1 + 2, 0)
            load_pair(Q1 + 3, 1)
            for v in range(4):
                sp.wait_ge(s_y[v], 16 * ST // 4)
            for n in range(4):
                load_rows(n, n, False)
            load_pair(Q1 + 4, 0)
            load_pair(Q1 + 5, 1)
            with sp.Fori(1, NT // 4) as i:
                for h in range(2):
                    for v in range(2):
                        load_pair(i * 4 + (Q1 + 2 + 2 * h + v), v)
                    for v in range(2):
                        store_rows(i * 4 + (2 * h + v - 4), 2 * h + v)
                    for v in range(2):
                        load_rows(i * 4 + (2 * h + v), 2 * h + v)
            for v in range(2):
                load_pair(NS // 2 - 2 + v, v)
            for v in range(4):
                store_rows(NT - 4 + v, v)
            for v in range(4):
                sp.wait_ge(s_y[v], B * 16 * ST // 4)
            for v in range(4):
                load_rows(NT + v, v)
            with sp.Fori(NT // 4 + 1, 2 * NT // 4) as i:
                for v in range(4):
                    store_rows(i * 4 + (v - 4), v)
                    load_rows(i * 4 + v, v)
            for v in range(4):
                store_rows(2 * NT - 4 + v, v)
            for v in range(4):
                sp.wait_ge(s_o[v], 16 * 2 * NT // 4)

        @block.gpsimd
        def _(pool):
            nc.gpsimd.memset(ID[:], 0.0)
            nc.gpsimd.memset(ZERO[:], 0.0)
            nc.gpsimd.memset(UPPER[:], 1.0)
            nc.gpsimd.memset(PADROW[:], 0.0).then_inc(pool_chain, 1)
            pool.wait_ge(pool_chain, 1)
            nc.gpsimd.affine_select(out=ID[:], in_=ID[:], compare_op=ALU.not_equal, fill=1.0, base=0,
                                    pattern=[[-1, P]], channel_multiplier=1)
            nc.gpsimd.affine_select(out=UPPER[:], in_=UPPER[:], compare_op=ALU.is_gt, fill=0.0, base=0,
                                    pattern=[[1, P]], channel_multiplier=-1)
            nc.gpsimd.memset(PADROW[:, D:D + 1], FAR)
            nc.gpsimd.memset(PADROW[:, D + 1:D + 2], -1.0)
            nc.gpsimd.iota(REV[:], [[-1, E]], base=E, channel_multiplier=0, allow_small_or_imprecise_dtypes=True)
            nc.gpsimd.iota(TOK[:], [[P, B * NT]], base=0, channel_multiplier=1, allow_small_or_imprecise_dtypes=True)
            nc.gpsimd.iota(JROW[:], [[1, ST]], base=0, channel_multiplier=0, allow_small_or_imprecise_dtypes=True)
            nc.gpsimd.iota(PCOL[:], [[0, 1]], base=0, channel_multiplier=1,
                           allow_small_or_imprecise_dtypes=True).then_inc(const_done, 1)

            for e in range(E):
                pool.wait_ge(w_max, e * 2 + 2)
                nc.gpsimd.partition_all_reduce(AMX[:, :], AM[:, :], P, bass.bass_isa.ReduceOp.absmax).then_inc(w_all, 1)

            def scatter_tile(b, t, k):
                nc.gpsimd.indirect_dma_start(
                    out=x_slots, out_offset=bass.IndirectOffsetOnAxis(ap=IDX[:, b, k, t:t + 1], axis=0),
                    in_=X[:, t + b * NT, :], in_offset=None).then_inc(s_scat[b], 16)

            def scatter_padding(b):
                for e in range(E):
                    nc.gpsimd.indirect_dma_start(
                        out=x_slots, out_offset=bass.IndirectOffsetOnAxis(ap=PIDX[:, b, e:e + 1], axis=0),
                        in_=PADROW[:, :], in_offset=None, bounds_check=NS * P - 1, oob_is_err=False).then_inc(s_scat[b], 16)

            def scatter_result(j, v):
                pool.wait_ge(y_ev, j + 1)
                nc.gpsimd.indirect_dma_start(
                    out=y_rows, out_offset=bass.IndirectOffsetOnAxis(ap=YID[:, v, :], axis=0),
                    in_=YS[:, v, :], in_offset=None, bounds_check=last_row, oob_is_err=False).then_inc(s_y[v], 16)

            last_row = pool.to_reg(2 * B * T - 1)
            pool.wait_ge(s_tail, B * E * 16)
            pool.wait_ge(r_done, 1)
            scatter_padding(0)
            for t in range(NT):
                for k in range(2):
                    scatter_tile(0, t, k)
            pool.wait_ge(r_done, 2)
            scatter_padding(1)
            for t in range(NT):
                for k in range(2):
                    scatter_tile(1, t, k)
                for k in range(2):
                    scatter_result(t * 2 + k, (t * 2 + k) % 4)
            for j in range(2 * NT, NS):
                scatter_result(j, j % 4)

        @block.tensor
        def _(pe):
            pe.wait_ge(const_done, 1)
            pe.wait_ge(s_raw, 48)
            for n, a0 in enumerate((0, 2, 6)):
                for a in range(2):
                    for c in range(DC):
                        last = nc.tensor.transpose(PS[:, n, c * D + a * P:c * D + (a + 1) * P],
                                                   RAW[:, a0 + a, c * P:(c + 1) * P], ID[:])
                last.then_inc(set_mm, 1)
            for c in range(DC):
                last = nc.tensor.transpose(PS[:, 3, c * E:(c + 1) * E], RR[:, c * P:(c + 1) * P], ID[0:E, 0:E])
            last.then_inc(set_mm, 1)
            pe.wait_ge(set_ev, 4)
            for e in range(DC):
                for f in range(DC):
                    last = nc.tensor.matmul(PS[:, 4, e * E:(e + 1) * E], RAW[:, 6 + f, e * P:(e + 1) * P], RT[:, f, :],
                                            start=(f == 0), stop=(f == DC - 1))
            last.then_inc(set_mm, 1)
            pe.wait_ge(set_ev, 6)
            for c in range(DC):
                for e in range(DC):
                    last = nc.tensor.matmul(PS[:, 5 + c, 0:DR], RAW[:, 4 + e, c * P:(c + 1) * P], WOT[:, e, :],
                                            start=(e == 0), stop=(e == DC - 1))
            last.then_inc(set_mm, 1)
            for n in range(2):
                for f in range(DC):
                    last = nc.tensor.matmul(PS[:, 7, n * E:(n + 1) * E], LB[:, n, f, :], RT[:, f, :],
                                            start=(f == 0), stop=(f == DC - 1))
            last.then_inc(set_mm, 1)
            pe.wait_ge(set_ev, 8)

            def transpose_x(gi, k, first=False):
                pe.wait_ge(s_x[k], 16 * (gi // 4 + 1) if isinstance(gi, int) else (gi - k) * 4 + 16)
                for c in range(DC):
                    if not first:
                        pe.wait_ge(xt_ev, gi * 2 - 1 + c)
                    for t in range(GT):
                        last = nc.tensor.transpose(PS[:, c, t * P:(t + 1) * P],
                                                   X[:, ds(gi * GT + t, 1), c * P:(c + 1) * P].rearrange("p o c -> p (o c)"), ID[:])
                    last.then_inc(xt_mm, 1)

            def project(gi, u, first=False):
                pe.wait_ge(xt_ev, gi * 2 + 2)
                for t in range(GT):
                    if not (first and t < 2):
                        pe.wait_ge(k_ev, gi * GT + (t - 1))
                    for c in range(DC):
                        last = nc.tensor.matmul(PS[:, 2 + t % 2, 0:DR], XT[:, u, c, t * P:(t + 1) * P], WKR[:, c, :],
                                                start=(c == 0), stop=(c == DC - 1))
                    last.then_inc(k_mm, 1)
                for m in range(DC):
                    if not first:
                        pe.wait_ge(q_ev, gi * 2 + (m - 1))
                    for c in range(DC):
                        last = nc.tensor.matmul(PS[:, 4 + m, :], WQT[:, c, m * P:(m + 1) * P], XT[:, u, c, :],
                                                start=(c == 0), stop=(c == DC - 1))
                    last.then_inc(q_mm, 1)
                for t in range(GT):
                    pe.wait_ge(k_ev, gi * GT + (t + 1))
                    for m in range(DC):
                        last = nc.tensor.matmul(PS[:, 6 + m, 0:D + 2], KS[:, u, t, m * P:(m + 1) * P],
                                                X[:, ds(gi * GT + t, 1), 0:D + 2].rearrange("p o c -> p (o c)"),
                                                start=False, stop=False, skip_group_check=True)
                last.then_inc(kx_mm, 1)

            def attention_sums(b):
                g0 = b * NG
                if b > 0:
                    pe.wait_ge(r_done, b)
                for m in range(DC):
                    nc.tensor.matmul(PS[:, 6 + m, 0:D + 2], ZERO[:, 0:P], ZERO[:, :], start=True, stop=False, skip_group_check=True)
                transpose_x(g0, 0, first=(b == 0))
                for g in range(g0, g0 + NG):
                    if g + 1 < g0 + NG:
                        transpose_x(g + 1, (g + 1) % 4)
                    project(g, g % 2, first=(g == 0))
                for m in range(DC):
                    last = nc.tensor.matmul(PS[:, 6 + m, 0:D + 2], ZERO[:, 0:P], ZERO[:, :], start=False, stop=True, skip_group_check=True)
                last.then_inc(m_mm, 1)
                pe.wait_ge(m_ev, 3 * b + 1)
                for m in range(DC):
                    for c in range(DC):
                        last = nc.tensor.transpose(PS[:, 0, c * D + m * P:c * D + (m + 1) * P], KXS[:, m, c * P:(c + 1) * P], ID[:])
                last.then_inc(m_mm, 1)
                pe.wait_ge(m_ev, 3 * b + 2)
                for m in range(DC):
                    for c in range(DC):
                        last = nc.tensor.matmul(PS[:, 1 + m, 0:DR], KXT[:, c, m * P:(m + 1) * P], G[:, c, :],
                                                start=(c == 0), stop=(c == DC - 1))
                last.then_inc(m_mm, 1)
                pe.wait_ge(m_ev, 3 * b + 3)

            def apply_m(b):
                for g in range(NG):
                    if g >= 2:
                        pe.wait_ge(x2_done, b * NG + g - 1)
                    for t in range(GT):
                        for m in range(DC):
                            last = nc.tensor.matmul(PS[:, 4 * (g % 2) + t, 0:DR + 1], Q[:, m, (g * GT + t) * P:(g * GT + t + 1) * P],
                                                    MQ[:, m, 0:DR + 1], start=(m == 0), stop=(m == DC - 1))
                        last.then_inc(u_mm, 1)

            def count_slots(b):
                pe.wait_ge(mask_rdy, b + 1)
                nc.tensor.matmul(PS[:, 0, 0:E * NT], UPPER[:], MK[:, :, :].rearrange("p e t -> p (e t)"), start=True, stop=True)
                nc.tensor.matmul(PS[:, 1, 0:E * NT], ONESB[:], MK[:, :, :].rearrange("p e t -> p (e t)"),
                                 start=True, stop=True).then_inc(cnt_mm, 1)

            attention_sums(0)
            apply_m(0)
            count_slots(0)
            attention_sums(1)
            apply_m(1)
            count_slots(1)
            pe.wait_ge(r_done, 2)

            def slots_transpose(j, v, first=False):
                if v % 2 == 0:
                    pe.wait_ge(s_g[v // 2], 16 * (j // 4 + 1) if isinstance(j, int) else (j - v) * 4 + 16)
                if not first:
                    pe.wait_ge(t_ev, j - 1)
                for c in range(DC):
                    for s in range(2):
                        last = nc.tensor.transpose(PS16[:, v % 2, (2 * c + s) * P:(2 * c + s + 1) * P],
                                                   XGH[:, v, s * D + c * P:s * D + (c + 1) * P], ID16[:])
                last.then_inc(t_mm, 1)

            THREE = ((0, 0), (0, 1), (1, 0))

            def first_product(j, v, first=False):
                e = pe.value_load(EID[0:1, ds(j, 1)], min_val=0, max_val=E - 1)
                pe.wait_ge(t_ev, j + 1)
                if not first:
                    pe.wait_ge(z_ev, j - 1)
                n = 0
                for c in range(DC):
                    for xp, wp in THREE:
                        last = nc.tensor.matmul(PS[:, 2 + v % 2, :], XTF[:, v % 2, (2 * c + xp) * P:(2 * c + xp + 1) * P],
                                                W1f[:, ds(e * (DC * 2 * H) + (2 * c + wp) * H, H)],
                                                start=(n == 0), stop=(n == 3 * DC - 1))
                        n += 1
                last.then_inc(z_mm, 1)

            def relu_transpose(j, v, first=False):
                pe.wait_ge(z_ev, j + 1)
                if not first:
                    pe.wait_ge(sq_ev, j - 1)
                for c in range(HC):
                    last = nc.tensor.transpose(PS[:, 4 + v % 2, c * P:(c + 1) * P], RL[:, v % 2, c * P:(c + 1) * P], ID[:])
                last.then_inc(rt_mm, 1)

            def second_product(j, v, first=False):
                e = pe.value_load(EID[0:1, ds(j, 1)], min_val=0, max_val=E - 1)
                pe.wait_ge(h_ev, j + 1)
                if not first:
                    pe.wait_ge(y_ev, j - 1)
                n = 0
                for c in range(HC):
                    for hp, wp in THREE:
                        last = nc.tensor.matmul(PS[:, 6 + v % 2, 0:D], HHL[:, v % 2, hp, c * P:(c + 1) * P],
                                                W2f[:, ds(e * (HC * 2 * D) + (2 * c + wp) * D, D)],
                                                start=(n == 0), stop=(n == 3 * HC - 1))
                        n += 1
                last.then_inc(y_mm, 1)

            def step(s, k):
                known = isinstance(s, int)
                if not known or s < NS:
                    slots_transpose(s, k, first=known and s < 2)
                if not known or 0 <= s - 1 < NS:
                    first_product(s - 1, (k - 1) % 4, first=known and s - 1 < 2)
                if not known or 0 <= s - 2 < NS:
                    relu_transpose(s - 2, (k - 2) % 4, first=known and s - 2 < 2)
                if not known or 0 <= s - 3 < NS:
                    second_product(s - 3, (k - 3) % 4, first=known and s - 3 < 2)

            for s in range(8):
                step(s, s % 4)
            with pe.Fori(2, NS // 4) as i:
                for k in range(4):
                    step(i * 4 + k, k)
            for s in range(NS, NS + 3):
                step(s, s % 4)

        @block.scalar
        def _(act):
            def sums_part(gi, u):
                first = isinstance(gi, int) and gi < 2
                for c in range(DC):
                    act.wait_ge(xt_mm, gi * 2 + (c + 1))
                    if not first and c == 0:
                        act.wait_ge(q_mm, gi * 2 - 2)
                    nc.scalar.copy(XT[:, u, c, :], PS[:, c, :]).then_inc(xt_ev, 1)

            def expert_part(e):
                act.wait_ge(w_scale, e + 1)
                nc.scalar.activation(W1[:, ds(e, 1), :, 0, :].rearrange("p o c h -> p (o c) h"),
                                     STG[:, 0, :].rearrange("p (c h) -> p c h", c=DC), ACT.Copy,
                                     scale=SG[:, 0, 0:1]).then_inc(w_hi, 1)
                nc.scalar.activation(W2[:, ds(e, 1), :, 0, :].rearrange("p o c h -> p (o c) h"),
                                     STG[:, 1, :].rearrange("p (c h) -> p c h", c=HC), ACT.Copy,
                                     scale=SG[:, 0, 1:2]).then_inc(w_hi, 1)

            def both(gi, u):
                sums_part(gi, u)
                expert_part(gi)

            def norm_sqrt(gi, b):
                act.wait_ge(var_rdy, gi + 1)
                nc.scalar.activation(SD[:, ds((gi - b * NG) * GT, GT)], VAR[:, ds((gi - b * NG) * GT, GT)],
                                     ACT.Sqrt).then_inc(sd_rdy, 1)

            def norm_apply(gi, u, b):
                act.wait_ge(rs_rdy, gi + 1)
                for t in range(GT):
                    last = nc.scalar.activation(KS[:, u, t, :], X[:, ds(gi * GT + t, 1), 0:D].rearrange("p o c -> p (o c)"),
                                                ACT.Identity, bias=NB[:, u, t:t + 1], scale=RS2[:, u, t:t + 1])
                last.then_inc(x1_rdy, 1)
                act.wait_ge(x1_rdy, gi + 1)
                nc.scalar.copy(XH[:, ds(gi * GT, GT), 0:D], KS[:, u, :, :]).then_inc(hi_rdy, 1)

            def norm_part(b):
                g0 = b * NG
                norm_sqrt(g0, b)
                for g in range(1, NG):
                    norm_sqrt(g0 + g, b)
                    norm_apply(g0 + g - 1, (g - 1) % 2, b)
                norm_apply(g0 + NG - 1, (NG - 1) % 2, b)
                act.wait_ge(ex_in, b + 1)
                nc.scalar.activation(GA[:, 1, :], GA[:, 0, :], ACT.Exp).then_inc(ex_out, 1)

            each_group(act, 0, both)
            norm_part(0)
            each_group(act, 1, sums_part)
            norm_part(1)

            def act_relu(j, v):
                act.wait_ge(z_mm, j + 1)
                if not (isinstance(j, int) and j < 2):
                    act.wait_ge(rt_mm, j - 1)
                nc.scalar.activation(RL[:, v % 2, :], PS[:, 2 + v % 2, :], ACT.Relu, scale=R_SCALE).then_inc(z_ev, 1)

            def act_square(j, v):
                act.wait_ge(rt_mm, j + 1)
                if not (isinstance(j, int) and j < 2):
                    act.wait_ge(h_ev, j - 1)
                nc.scalar.activation(H32[:, v % 2, :], PS[:, 4 + v % 2, :], ACT.Square).then_inc(sq_ev, 1)

            def act_step(s, k, pair=None):
                known = isinstance(s, int)
                if not known or 0 <= s - 1 < NS:
                    act_relu(s - 1, (k - 1) % 4)
                if not known or 0 <= s - 2 < NS:
                    act_square(s - 2, (k - 2) % 4)
                if not known or 0 <= s - 3 < NS:
                    j, v = s - 3, (k - 3) % 4
                    act.wait_ge(y_mm, j + 1)
                    if v % 2 == 0:
                        act.wait_ge(meta, j // 2 + 1 if known else pair)
                    if not (known and j < 4):
                        act.wait_ge(s_y[v], 16 * (j // 4) if known else (j - v) * 4)
                    nc.scalar.activation(YS[:, v, :], PS[:, 6 + v % 2, 0:D], ACT.Copy, scale=GATE[:, v:v + 1]).then_inc(y_ev, 1)

            def out_sqrt(n, u):
                act.wait_ge(c_var, n + 1)
                nc.scalar.activation(CW[:, u, 1:2], CW[:, u, 0:1], ACT.Sqrt).then_inc(c_sd, 1)

            def out_apply(n, u):
                act.wait_ge(c_rs, n + 1)
                if not (isinstance(n, int) and n < 4):
                    act.wait_ge(s_o[u], 16 * (n // 4) if isinstance(n, int) else (n - u) * 4)
                nc.scalar.activation(OF[:, u, :], SF[:, u, :], ACT.Identity, bias=CW[:, u, 7:8], scale=CW[:, u, 6:7]).then_inc(c_out, 1)

            for s in range(8):
                act_step(s, s % 4)
            with act.Fori(2, ST // 4 + 2) as i:
                for k in range(4):
                    act_step(i * 4 + k, k, pair=i * 2 + ((k - 3) // 2 + 1))

            def with_output(i, n, h, first=False):
                for k in range(4):
                    act_step(i * 4 + k, k, pair=i * 2 + ((k - 3) // 2 + 1))
                    if k == 0 and not first:
                        for v in range(2):
                            out_apply(n - 2 + v, (2 * h + 2 + v) % 4)
                    if k % 2 == 1:
                        out_sqrt(n + k // 2, 2 * h + k // 2)

            with_output(ST // 4 + 2, 0, 0, True)
            with_output(ST // 4 + 3, 2, 1)
            with act.Fori(1, NT // 4) as i:
                for h in range(2):
                    with_output(i * 2 + (ST // 4 + 2 + h), i * 4 + 2 * h, h)
            for v in range(2):
                out_apply(NT - 2 + v, 2 + v)
            for s in range(NS, NS + 3):
                act_step(s, s % 4)
            with act.Fori(NT // 4, 2 * NT // 4) as i:
                for h in range(2):
                    for v in range(2):
                        out_sqrt(i * 4 + (2 * h + v), 2 * h + v)
                    for v in range(2):
                        out_apply(i * 4 + (2 * h + v), 2 * h + v)

        @block.vector
        def _(dve):
            V = nc.vector

            def bc(ap, shape):
                return ap.broadcast_to(shape)

            nc.vector.memset(ONESB[:], 1.0)
            nc.vector.memset(ONES[:], 1.0)
            nc.vector.memset(LB[:, 0, :, :], 1.0)
            nc.vector.memset(X[:, :, D:D + 1], 1.0)
            nc.vector.memset(X[:, :, D + 1:D + 2], 0.0)
            dve.wait_ge(const_done, 1)
            V.tensor_copy(ID16[:], ID[:]).then_inc(setup_chain, 1)
            dve.wait_ge(set_mm, 1)
            V.tensor_copy(WQT[:, :, :], PS[:, 0, :].rearrange("p (c d) -> p c d", c=DC)).then_inc(set_ev, 1)
            dve.wait_ge(set_mm, 2)
            V.tensor_copy(WKR[:, :, 0:D], PS[:, 1, :].rearrange("p (c d) -> p c d", c=DC)).then_inc(set_ev, 1)
            dve.wait_ge(set_mm, 3)
            V.tensor_copy(WOT[:, :, 0:D], PS[:, 2, :].rearrange("p (c d) -> p c d", c=DC)).then_inc(set_ev, 1)
            dve.wait_ge(set_mm, 4)
            V.tensor_copy(WKR[:, :, D:DR], PS[:, 3, 0:DC * E].rearrange("p (c d) -> p c d", c=DC))
            V.tensor_copy(RT[:, :, :], PS[:, 3, 0:DC * E].rearrange("p (c d) -> p c d", c=DC)).then_inc(set_ev, 1)
            dve.wait_ge(s_bias, 32)
            V.tensor_copy(LB[:, 1, :, :], bc(BCOL[:, :].rearrange("p (c o) -> p c o", o=1), [P, DC, P])).then_inc(set_ev, 1)
            dve.wait_ge(set_mm, 5)
            V.tensor_copy(WOT[:, :, D:DR], PS[:, 4, 0:DC * E].rearrange("p (c d) -> p c d", c=DC)).then_inc(set_ev, 1)
            dve.wait_ge(set_mm, 6)
            V.tensor_copy(G[:, :, :], PS[:, 5:5 + DC, 0:DR]).then_inc(set_ev, 1)
            dve.wait_ge(set_mm, 7)
            V.tensor_copy(SRBR[:, :, :], PS[:, 7, 0:2 * E].rearrange("p (n e) -> p n e", n=2)).then_inc(set_ev, 1)

            def expert_max(e):
                for k in range(2):
                    dve.wait_ge(s_w[k], e * 16 + 16)
                    if k == 0 and not (isinstance(e, int) and e == 0):
                        dve.wait_ge(w_all, e)
                    V.tensor_reduce(AM[:, k:k + 1], STG[:, k, :], AX.X, ALU.max, apply_absolute_value=True).then_inc(w_max, 1)

            def expert_scale(e):
                dve.wait_ge(w_all, e + 1)
                p2 = P2[:, ds(e, 1), :].rearrange("p o k -> p (o k)")
                V.tensor_scalar(AMX[:, :], AMX[:, :], TINY, None, ALU.max).then_inc(w_step, 1)
                dve.wait_ge(w_step, e * 3 + 1)
                V.tensor_scalar(PW[:, :].bitcast(i32), AMX[:, :].bitcast(i32), 0x7F800000, None, ALU.bitwise_and).then_inc(w_step, 1)
                dve.wait_ge(w_step, e * 3 + 2)
                V.reciprocal(SG[:, 1, :], PW[:, :]).then_inc(w_step, 1)
                V.tensor_copy(p2, PW[:, :])
                dve.wait_ge(w_step, e * 3 + 3)
                if not (isinstance(e, int) and e == 0):
                    dve.wait_ge(w_hi, e * 2)
                V.tensor_scalar(SG[:, 0, :], SG[:, 1, :], 2.0 ** 14, None, ALU.mult).then_inc(w_scale, 1)

            def expert_low(e):
                dve.wait_ge(w_scale, e + 1)
                for k, (W, C) in enumerate(((W1, DC), (W2, HC))):
                    dve.wait_ge(w_hi, e * 2 + (k + 1))
                    V.scalar_tensor_tensor(
                        out=W[:, ds(e, 1), :, 1, :].rearrange("p o c h -> p (o c) h"),
                        in0=STG[:, k, :].rearrange("p (c h) -> p c h", c=C), scalar=SG[:, 0, k:k + 1],
                        in1=W[:, ds(e, 1), :, 0, :].rearrange("p o c h -> p (o c) h"),
                        op0=ALU.mult, op1=ALU.subtract).then_inc(w_lo, 1)

            def sums_part(gi, u, b):
                first = isinstance(gi, int) and gi < 2
                if b == 0:
                    expert_max(gi)
                for t in range(GT):
                    dve.wait_ge(k_mm, gi * GT + (t + 1))
                    if t == 0 and not first:
                        dve.wait_ge(kx_mm, gi - 1)
                    V.tensor_copy(XR[:, ds((gi - b * NG) * GT + t, 1), :].rearrange("p o e -> p (o e)"), PS[:, 2 + t % 2, D:DR])
                    V.tensor_scalar(KS[:, u, t, :], PS[:, 2 + t % 2, 0:D], 0.0, EPS, ALU.max, ALU.add).then_inc(k_ev, 1)
                if b == 0:
                    expert_scale(gi)
                for m in range(DC):
                    dve.wait_ge(q_mm, gi * 2 + (m + 1))
                    V.tensor_scalar(Q[:, m, ds((gi - b * NG) * (GT * P), GT * P)], PS[:, 4 + m, :], 0.0, EPS,
                                    ALU.max, ALU.add).then_inc(q_ev, 1)
                if b == 0:
                    expert_low(gi)
                dve.wait_ge(kx_mm, gi + 1)
                V.tensor_tensor(X[:, ds(gi * GT, GT), 0:D], X[:, ds(gi * GT, GT), 0:D],
                                bc(BB[:, :].rearrange("p (o d) -> p o d", o=1), [P, GT, D]), ALU.add).then_inc(b_add, 1)

            def make_m(b):
                dve.wait_ge(m_mm, 3 * b + 1)
                V.tensor_copy(KXS[:, :, :], PS[:, 6:6 + DC, 0:D + 2]).then_inc(m_ev, 1)
                dve.wait_ge(m_mm, 3 * b + 2)
                V.tensor_copy(KXT[:, :, :], PS[:, 0, :].rearrange("p (c d) -> p c d", c=DC)).then_inc(m_ev, 1)
                dve.wait_ge(m_mm, 3 * b + 3)
                V.tensor_copy(MQ[:, :, DEN:DEN + 1], KXS[:, :, D:D + 1])
                V.tensor_copy(MQ[:, :, 0:DR], PS[:, 1:1 + DC, 0:DR]).then_inc(m_ev, 1)

            def residual_stats(b, g):
                gi, u = b * NG + g, g % 2
                dve.wait_ge(u_mm, gi * GT + GT)
                V.tensor_scalar(ZT[:, u, :], PS[:, 4 * u:4 * u + GT, DEN:DEN + 1].rearrange("p t o -> p (t o)"), EPS, None,
                                ALU.add).then_inc(z_step, 1)
                dve.wait_ge(z_step, gi * 2 + 1)
                V.reciprocal(ZR[:, u, :], ZT[:, u, :]).then_inc(z_step, 1)
                dve.wait_ge(z_step, gi * 2 + 2)
                dve.wait_ge(b_add, gi + 1)
                V.tensor_tensor(LG[:, g * GT:(g + 1) * GT, :], PS[:, 4 * u:4 * u + GT, D:DR],
                                bc(ZR[:, u, :].rearrange("p (t o) -> p t o", o=1), [P, GT, E]), ALU.mult)
                for t in range(GT):
                    x = X[:, gi * GT + t, 0:D]
                    last = V.scalar_tensor_tensor(out=x, in0=PS[:, 4 * u + t, 0:D], scalar=ZR[:, u, t:t + 1], in1=x,
                                                  op0=ALU.mult, op1=ALU.add)
                last.then_inc(x2_done, 1)
                dve.wait_ge(x2_done, gi + 1)
                for t in range(GT):
                    last = V.bn_stats(ST6[:, u, t, :], X[:, gi * GT + t, 0:D])
                last.then_inc(st_step, 1)
                dve.wait_ge(st_step, gi * 2 + 1)
                for t in range(GT):
                    last = V.bn_aggr(MV[:, u, t, :], ST6[:, u, t, :])
                last.then_inc(st_step, 1)
                dve.wait_ge(st_step, gi * 2 + 2)
                V.tensor_scalar(VAR[:, g * GT:(g + 1) * GT], MV[:, u, :, 1:2].rearrange("p t o -> p (t o)"), EPS_LN, None,
                                ALU.add).then_inc(var_rdy, 1)

            def inverse_std(b, g):
                gi, u = b * NG + g, g % 2
                own = slice(g * GT, (g + 1) * GT)
                n = [gi * 5]

                def then(ins):
                    ins.then_inc(nw_step, 1)
                    n[0] += 1
                    dve.wait_ge(nw_step, n[0])

                dve.wait_ge(sd_rdy, gi + 1)
                then(V.reciprocal(NW[:, 0, :], SD[:, own]))
                then(V.tensor_tensor(NW[:, 1, :], NW[:, 0, :], NW[:, 0, :], ALU.mult))
                then(V.tensor_tensor(NW[:, 2, :], NW[:, 1, :], VAR[:, own], ALU.mult))
                then(V.tensor_scalar(NW[:, 3, :], NW[:, 2, :], -0.5, 1.5, ALU.mult, ALU.add))
                V.tensor_copy(MEAN[:, own], MV[:, u, :, 0:1].rearrange("p t o -> p (t o)"))
                V.tensor_tensor(RSTD[:, own], NW[:, 0, :], NW[:, 3, :], ALU.mult)
                then(V.scalar_tensor_tensor(out=RS2[:, u, :], in0=NW[:, 0, :], scalar=XS, in1=NW[:, 3, :],
                                            op0=ALU.mult, op1=ALU.mult))
                V.scalar_tensor_tensor(out=NB[:, u, :], in0=RS2[:, u, :], scalar=-1.0,
                                       in1=MV[:, u, :, 0:1].rearrange("p t o -> p (t o)"),
                                       op0=ALU.mult, op1=ALU.mult).then_inc(rs_rdy, 1)

            def low_part(b, g):
                gi, u = b * NG + g, g % 2
                dve.wait_ge(hi_rdy, gi + 1)
                own = slice(gi * GT, (gi + 1) * GT)
                V.tensor_tensor(XH[:, own, D:2 * D], KS[:, u, :, :], XH[:, own, 0:D], ALU.subtract).then_inc(lo_rdy, 1)

            R_STEPS = 49

            def route(b):
                n = [b * R_STEPS]

                def then(ins):
                    ins.then_inc(r_step, 1)
                    n[0] += 1
                    dve.wait_ge(r_step, n[0])

                TE = [P, NT, E]

                def over_t(row):
                    return bc(row.rearrange("p (o e) -> p o e", o=1), TE)

                def over_e(col):
                    return bc(col.rearrange("p (t o) -> p t o", o=1), TE)

                def flat(a):
                    return a.rearrange("p e t -> p (e t)")

                if b == 0:
                    dve.wait_ge(w_lo, 2 * E)
                    V.scalar_tensor_tensor(out=KAP[:, :], in0=P2[:, :, 0:1].rearrange("p e o -> p (e o)"), scalar=XS * 2.0 ** -10,
                                           in1=P2[:, :, 0:1].rearrange("p e o -> p (e o)"), op0=ALU.mult, op1=ALU.mult).then_inc(kap_step, 1)
                    dve.wait_ge(kap_step, 1)
                    V.tensor_tensor(KAP[:, :], KAP[:, :], P2[:, :, 1:2].rearrange("p e o -> p (e o)"), ALU.mult).then_inc(kap_step, 1)
                    dve.wait_ge(kap_step, 2)
                dve.wait_ge(rs_rdy, (b + 1) * NG)
                then(V.tensor_tensor(TA[:, :, :], LG[:, :, :], XR[:, :, :], ALU.add))
                then(V.tensor_tensor(TA[:, :, :], TA[:, :, :], over_t(SRBR[:, 1, :]), ALU.add))
                then(V.tensor_tensor(TB[:, :, :], over_e(MEAN[:, :]), over_t(SRBR[:, 0, :]), ALU.mult))
                then(V.tensor_tensor(TA[:, :, :], TA[:, :, :], TB[:, :, :], ALU.subtract))
                then(V.tensor_tensor(TA[:, :, :], TA[:, :, :], over_e(RSTD[:, :]), ALU.mult))
                for k in range(2):
                    then(V.tensor_reduce(MX[:, k, :], TA[:, :, :], AX.X, ALU.max))
                    then(V.tensor_tensor(TB[:, :, :], TA[:, :, :], over_e(MX[:, k, :]), ALU.is_equal))
                    then(V.tensor_tensor(TB[:, :, :], TB[:, :, :], over_t(REV[:, :]), ALU.mult))
                    then(V.tensor_reduce(CM[:, k, :], TB[:, :, :], AX.X, ALU.max))
                    then(V.tensor_tensor(OH[:, k, :, :], over_t(REV[:, :]), over_e(CM[:, k, :]), ALU.is_equal))
                    if k == 0:
                        then(V.scalar_tensor_tensor(out=TA[:, :, :], in0=OH[:, 0, :, :], scalar=-3.0e38, in1=TA[:, :, :],
                                                    op0=ALU.mult, op1=ALU.add))
                V.tensor_tensor(MK[:, :, :].rearrange("p e t -> p t e"), OH[:, 0, :, :], OH[:, 1, :, :], ALU.add).then_inc(mask_rdy, 1)
                V.tensor_tensor(GA[:, 0, :], MX[:, 1, :], MX[:, 0, :], ALU.subtract).then_inc(ex_in, 1)
                dve.wait_ge(cnt_mm, b + 1)
                then(V.tensor_tensor_scan(flat(SI[:, :, :]), ONES[:, :], PS[:, 1, 0:E * NT], 0.0, ALU.mult, ALU.add))
                then(V.tensor_tensor(flat(SX[:, :, :]), flat(SI[:, :, :]), PS[:, 1, 0:E * NT], ALU.subtract))
                start_e = SX[:, :, 0:1].rearrange("p e o -> p (e o)")
                then(V.tensor_tensor(CNT[:, :], SI[:, :, NT - 1:NT].rearrange("p e o -> p (e o)"), start_e, ALU.subtract))
                then(V.tensor_scalar(CI[:, :], CNT[:, :], float(P - 1), None, ALU.add))
                then(V.tensor_scalar(CI[:, :], CI[:, :], 7, None, ALU.arith_shift_right))
                then(V.tensor_copy(NTL[:, :], CI[:, :]))
                then(V.tensor_tensor_scan(TBI[:, :], ONES[:, 0:E], NTL[:, :], 0.0, ALU.mult, ALU.add))
                then(V.tensor_tensor(TBX[:, :], TBI[:, :], NTL[:, :], ALU.subtract))
                then(V.tensor_scalar(PD[:, 0, :], TBX[:, :], float(P), float(b * ST * P), ALU.mult, ALU.add))
                then(V.tensor_tensor(OFF[:, :], PD[:, 0, :], start_e, ALU.subtract))
                then(V.tensor_tensor(flat(SX[:, :, :]), flat(SX[:, :, :]), PS[:, 0, 0:E * NT], ALU.add))
                pos = SX[:, :, :].rearrange("p e t -> p t e")
                then(V.tensor_tensor(TB[:, :, :], pos, over_t(OFF[:, :]), ALU.add))
                for k in range(2):
                    then(V.tensor_tensor(TA[:, :, :], TB[:, :, :], OH[:, k, :, :], ALU.mult))
                    then(V.tensor_reduce(SL[:, k, :], TA[:, :, :], AX.X, ALU.add))
                V.tensor_copy(IDX[:, b, :, :], SL[:, :, :])
                then(V.tensor_tensor(PD[:, 1, :], CNT[:, :], PD[:, 0, :], ALU.add))
                then(V.tensor_scalar(PD[:, 1, :], PD[:, 1, :], PCOL[:, 0:1], None, ALU.add))
                then(V.scalar_tensor_tensor(out=PD[:, 2, :], in0=NTL[:, :], scalar=float(P), in1=PD[:, 0, :],
                                            op0=ALU.mult, op1=ALU.add))
                then(V.tensor_tensor(PD[:, 2, :], PD[:, 1, :], PD[:, 2, :], ALU.is_ge))
                V.scalar_tensor_tensor(out=PIDX[:, b, :], in0=PD[:, 2, :], scalar=FAR, in1=PD[:, 1, :], op0=ALU.mult, op1=ALU.add)
                then(V.tensor_tensor(CMP[:, :, :], bc(JROW[:, :].rearrange("p (j o) -> p j o", o=1), [P, ST, E]),
                                     bc(TBX[:, :].rearrange("p (o e) -> p o e", o=1), [P, ST, E]), ALU.is_ge))
                own = slice(b * ST, (b + 1) * ST)
                then(V.tensor_reduce(EIDF[:, own], CMP[:, :, :], AX.X, ALU.add))
                then(V.tensor_scalar(EIDF[:, own], EIDF[:, own], -1.0, None, ALU.add))
                then(V.tensor_copy(EID[:, own], EIDF[:, own]))
                dve.wait_ge(ex_out, b + 1)
                then(V.tensor_scalar(GA[:, 2, :], GA[:, 1, :], 1.0, None, ALU.add))
                then(V.reciprocal(GA[:, 3, :], GA[:, 2, :]))
                then(V.tensor_tensor(GA[:, 4, :], GA[:, 3, :], GA[:, 1, :], ALU.mult))
                for k in range(2):
                    then(V.tensor_tensor(TA[:, :, :], OH[:, k, :, :], over_t(KAP[:, :]), ALU.mult))
                    then(V.tensor_reduce(SL[:, k, :], TA[:, :, :], AX.X, ALU.add))
                    then(V.tensor_tensor(GA[:, 3 + k, :], GA[:, 3 + k, :], SL[:, k, :], ALU.mult))
                dve.wait_ge(lo_rdy, (b + 1) * NG)
                rows = slice(b * NT, (b + 1) * NT)

                def field(k):
                    return X[:, rows, D + k:D + k + 1].rearrange("p t o -> p (t o)")

                V.tensor_copy(field(0), TOK[:, rows])
                V.tensor_scalar(field(1), CM[:, 0, :], -1.0, float(E), ALU.mult, ALU.add)
                V.tensor_copy(field(2), GA[:, 3, :])
                V.tensor_tensor(field(3), GA[:, 4, :], GA[:, 3, :], ALU.subtract).then_inc(r_done, 1)
                assert n[0] == (b + 1) * R_STEPS

            def norm_part(b):
                for g in range(NG):
                    residual_stats(b, g)
                    if g >= 2:
                        low_part(b, g - 2)
                    if g >= 1:
                        inverse_std(b, g - 1)
                inverse_std(b, NG - 1)
                low_part(b, NG - 2)
                low_part(b, NG - 1)

            for b in range(B):
                each_group(dve, b, lambda gi, u: sums_part(gi, u, b))
                make_m(b)
                norm_part(b)
                route(b)

            def rows_out(j, v, first=False):
                dve.wait_ge(t_mm, j + 1)
                if not first:
                    dve.wait_ge(z_mm, j - 1)
                V.tensor_copy(XTF[:, v % 2, :], PS16[:, v % 2, 0:2 * D]).then_inc(t_ev, 1)

            def pair_meta(q, v, first=False):
                j = 2 * v
                if not first:
                    dve.wait_ge(y_ev, q * 2 - 2)
                    for w in range(2):
                        dve.wait_ge(s_y[j + w], 16 * (q // 2) if isinstance(q, int) else (q - v) * 8)
                V.tensor_tensor(MT[:, 0, :], XG[:, j:j + 2, D + 1:D + 2].rearrange("p j o -> p (j o)"), EIDF[:, ds(q * 2, 2)],
                                ALU.not_equal).then_inc(meta_step, 1)
                dve.wait_ge(meta_step, q * 2 + 1)
                V.scalar_tensor_tensor(out=YID[:, j:j + 2, :].rearrange("p j o -> p (j o)"), in0=MT[:, 0, :], scalar=float(B * T),
                                       in1=XG[:, j:j + 2, D:D + 1].rearrange("p j o -> p (j o)"), op0=ALU.mult, op1=ALU.add)
                V.tensor_tensor(MT[:, 1, :], MT[:, 0, :], XG[:, j:j + 2, D + 3:D + 4].rearrange("p j o -> p (j o)"),
                                ALU.mult).then_inc(meta_step, 1)
                dve.wait_ge(meta_step, q * 2 + 2)
                V.tensor_tensor(GATE[:, j:j + 2], MT[:, 1, :], XG[:, j:j + 2, D + 2:D + 3].rearrange("p j o -> p (j o)"),
                                ALU.add).then_inc(meta, 1)

            def split_h(j, v, first=False):
                dve.wait_ge(sq_ev, j + 1)
                if not first:
                    dve.wait_ge(y_mm, j - 1)
                V.tensor_copy(HHL[:, v % 2, 0, :], H32[:, v % 2, :]).then_inc(h_cp, 1)
                dve.wait_ge(h_cp, j + 1)
                V.tensor_tensor(HHL[:, v % 2, 1, :], H32[:, v % 2, :], HHL[:, v % 2, 0, :], ALU.subtract).then_inc(h_ev, 1)

            def dve_step(s, k, pair=None):
                known = isinstance(s, int)
                if not known or s < NS:
                    rows_out(s, k, first=known and s < 2)
                if not known or 0 <= s - 2 < NS:
                    split_h(s - 2, (k - 2) % 4, first=known and s - 2 < 2)
                if k % 2 == 0 and (not known or 2 <= s < NS + 2):
                    pair_meta((s - 2) // 2 if known else pair, 1 - k // 2, first=known and s < 6)

            C_STEPS = 5

            def sum_rows(n, u):
                row = ds(n, 1) if not isinstance(n, int) else slice(n, n + 1)
                dve.wait_ge(s_yg[u], 16 * (n // 4 + 1) if isinstance(n, int) else (n - u) * 4 + 16)
                if not (isinstance(n, int) and n < 4):
                    dve.wait_ge(c_out, n - 3)
                c = n * C_STEPS
                V.tensor_tensor(SF[:, u, :], XH[:, row, 0:D].rearrange("p o d -> p (o d)"),
                                XH[:, row, D:2 * D].rearrange("p o d -> p (o d)"), ALU.add).then_inc(c_step, 1)
                dve.wait_ge(c_step, c + 1)
                V.tensor_tensor(SF[:, u, :], SF[:, u, :], YG[:, u, 0, :], ALU.add).then_inc(c_step, 1)
                dve.wait_ge(c_step, c + 2)
                V.tensor_tensor(SF[:, u, :], SF[:, u, :], YG[:, u, 1, :], ALU.add).then_inc(c_step, 1)
                dve.wait_ge(c_step, c + 3)
                V.bn_stats(C6[:, u, :], SF[:, u, :]).then_inc(c_step, 1)
                dve.wait_ge(c_step, c + 4)
                V.tensor_copy(CW[:, u, 5:6], C6[:, u, 0:1])
                V.bn_aggr(CV[:, u, :], C6[:, u, :]).then_inc(c_step, 1)
                dve.wait_ge(c_step, c + 5)
                V.tensor_scalar(CW[:, u, 0:1], CV[:, u, 1:2], EPS_LN * XS * XS, None, ALU.add).then_inc(c_var, 1)

            def sum_scale(n, u):
                c = n * 5

                def w(k):
                    return CW[:, u, k:k + 1]

                dve.wait_ge(c_sd, n + 1)
                dve.wait_ge(c_var, n + 1)
                V.reciprocal(w(2), w(1)).then_inc(cn_step, 1)
                dve.wait_ge(cn_step, c + 1)
                V.tensor_tensor(w(3), w(2), w(2), ALU.mult).then_inc(cn_step, 1)
                dve.wait_ge(cn_step, c + 2)
                V.tensor_tensor(w(4), w(3), w(0), ALU.mult).then_inc(cn_step, 1)
                dve.wait_ge(cn_step, c + 3)
                V.tensor_scalar(w(5), w(4), -0.5, 1.5, ALU.mult, ALU.add).then_inc(cn_step, 1)
                dve.wait_ge(cn_step, c + 4)
                V.tensor_tensor(w(6), w(2), w(5), ALU.mult).then_inc(cn_step, 1)
                dve.wait_ge(cn_step, c + 5)
                V.scalar_tensor_tensor(out=w(7), in0=w(6), scalar=-1.0, in1=CV[:, u, 0:1], op0=ALU.mult, op1=ALU.mult).then_inc(c_rs, 1)

            for s in range(8):
                dve_step(s, s % 4, None)
            with dve.Fori(2, ST // 4 + 2) as i:
                for k in range(4):
                    dve_step(i * 4 + k, k, pair=i * 2 + (k // 2 - 1))

            def with_output(i, n, h, first=False):
                for k in range(4):
                    dve_step(i * 4 + k, k, pair=i * 2 + (k // 2 - 1))
                    if k == 0 and not first:
                        for v in range(2):
                            sum_scale(n - 2 + v, (2 * h + 2 + v) % 4)
                    if k % 2 == 1:
                        sum_rows(n + k // 2, 2 * h + k // 2)

            with_output(ST // 4 + 2, 0, 0, True)
            with_output(ST // 4 + 3, 2, 1)
            with dve.Fori(1, NT // 4) as i:
                for h in range(2):
                    with_output(i * 2 + (ST // 4 + 2 + h), i * 4 + 2 * h, h)
            for v in range(2):
                sum_scale(NT - 2 + v, 2 + v)
            for s in range(NS, NS + 3):
                dve_step(s, s % 4, None)
            with dve.Fori(NT // 4, 2 * NT // 4) as i:
                for h in range(2):
                    for v in range(2):
                        sum_rows(i * 4 + (2 * h + v), 2 * h + v)
                    for v in range(2):
                        sum_scale(i * 4 + (2 * h + v), 2 * h + v)


_INS = ["L0_attn_x", "L0_attn_W_qkv", "L0_attn_W_out", "L0_attn_b_out", "L0_ffn_router_w", "L0_ffn_w1", "L0_ffn_w2"]
_OUTS = [((2, 4096, 256), "float32")]


def kernel(**inputs):
    import numpy as _np
    import concourse.bacc as _bacc
    from concourse import mybir as _mybir
    from concourse.bass_utils import run_bass_kernel_spmd as _run

    nc = _bacc.Bacc("TRN2", target_bir_lowering=False, num_devices=1)
    arrays, args = {}, []
    for name in _INS:
        a = _np.ascontiguousarray(inputs[name])
        arrays[f"in_{name}_dram"] = a
        args.append(nc.dram_tensor(f"in_{name}_dram", a.shape, _mybir.dt.from_np(a.dtype), kind="ExternalInput").ap())
    for i, (shape, dtype) in enumerate(_OUTS):
        args.append(nc.dram_tensor(f"out_{i}_dram", shape, _mybir.dt.from_np(_np.dtype(dtype)), kind="ExternalOutput").ap())
    linear_attention_then_top2_experts(nc, *args)
    r = _run(nc, [arrays], core_ids=[0])
    return r.results[0]["out_0_dram"]
```

```python
import concourse.bass as bass
from concourse import mybir
from contextlib import ExitStack


def linear_attention_then_top2_experts(nc, x_in, w_qkv, w_out, b_out, router_w, w1_in, w2_in, out):
    f32, f16, bf16, i32 = mybir.dt.float32, mybir.dt.float16, mybir.dt.bfloat16, mybir.dt.int32
    ALU = mybir.AluOpType
    ACT = mybir.ActivationFunctionType
    AX = mybir.AxisListType
    ds = bass.ds

    P = 128
    B, T, D = x_in.shape
    E, _, H = w1_in.shape
    DC, HC = D // P, H // P
    NT = T // P
    GT = 4
    NG = NT // GT
    ST = 2 * NT + E
    NS = B * ST
    DR = D + E
    DEN = DR
    EW = DC * 2 * H
    ROW = D + 4
    EPS, EPS_LN = 1e-6, 1e-5
    XS = 2048.0
    R_SCALE = 2.0 ** -27
    TINY = 2.0 ** -100
    FAR = float(1 << 20)

    xf = x_in.rearrange("b (n p) d -> p (b n) d", p=P)
    of = out.rearrange("b (n p) d -> p (b n) d", p=P)
    x_slots = nc.dram_tensor("x_slots", (NS * P, ROW), f32, kind="Internal").ap()
    y_rows = nc.dram_tensor("y_rows", (2 * B * T, D), f32, kind="Internal").ap()
    xs_v = x_slots.rearrange("(j p) c -> p j c", p=P)
    yr_v = y_rows.rearrange("(k n p) d -> p k n d", k=2, p=P)

    ctx = ExitStack()
    with ctx:
        def sb(name, shape, dt):
            return ctx.enter_context(nc.sbuf_tensor(name, shape, dt))

        def sem(name):
            return ctx.enter_context(nc.semaphore(name))

        X = sb("X", [P, B * NT, ROW], f32)
        XH = X[:, :, :].bitcast(f16)
        W1 = sb("W1", [P, E, DC, 2, H], f16)
        W2 = sb("W2", [P, E, HC, 2, D], f16)
        W1f = W1[:, :, :, :, :].rearrange("p e c s h -> p (e c s h)")
        W2f = W2[:, :, :, :, :].rearrange("p e c s h -> p (e c s h)")
        STG = sb("STG", [P, 2, 1024], f32)
        Qb = sb("Qb", [P, DC * T], f32)
        Q = Qb[:, :].rearrange("p (c t) -> p c t", c=DC)
        RAW = Qb[:, 0:8 * D].rearrange("p (a d) -> p a d", a=8)
        XT = sb("XT", [P, 2, DC, GT * P], f32)
        KS = sb("KS", [P, 2, GT, D], f32)
        WKR = sb("WKR", [P, DC, DR], f32)
        WQT = sb("WQT", [P, DC, D], f32)
        WOT = Qb[:, 2048:2048 + DC * DR].rearrange("p (c d) -> p c d", c=DC)
        G = sb("G", [P, DC, DR], f32)
        RT = sb("RT", [P, DC, E], f32)
        RR = Qb[0:E, 2624:2624 + D]
        MQ = sb("MQ", [P, DC, DR + 2], f32)
        KXS = sb("KXS", [P, DC, D + 2], f32)
        KXT = KS[:, 0, 0:DC, :]
        ID = sb("ID", [P, P], f32)
        ID16 = sb("ID16", [P, P], f16)
        UPPER = sb("UPPER", [P, P], bf16)
        ONESB = sb("ONESB", [P, P], bf16)
        ZERO = sb("ZERO", [P, D + 2], f32)
        BB = sb("BB", [P, D], f32)
        BCOL = sb("BCOL", [P, DC], f32)
        LB = Qb[:, 3072:3072 + 2 * D].rearrange("p (n c k) -> p n c k", n=2, c=DC)
        SRBR = sb("SRBR", [P, 2, E], f32)
        PADROW = sb("PADROW", [P, ROW], f32)
        XR = sb("XR", [P, NT, E], f32)
        LG = sb("LG", [P, NT, E], f32)
        MEAN = sb("MEAN", [P, NT], f32)
        VAR = sb("VAR", [P, NT], f32)
        SD = sb("SD", [P, NT], f32)
        RSTD = sb("RSTD", [P, NT], f32)
        ZT = sb("ZT", [P, 2, GT], f32)
        ZR = sb("ZR", [P, 2, GT], f32)
        ST6 = sb("ST6", [P, 2, GT, 6], f32)
        MV = sb("MV", [P, 2, GT, 2], f32)
        NW = sb("NW", [P, 4, GT], f32)
        RS2 = sb("RS2", [P, 2, GT], f32)
        NB = sb("NB", [P, 2, GT], f32)
        AM = sb("AM", [P, 2], f32)
        AMX = sb("AMX", [P, 2], f32)
        P2 = sb("P2", [P, E, 2], f32)
        PW = sb("PW", [P, 2], f32)
        SG = sb("SG", [P, 2, 2], f32)
        KAP = sb("KAP", [P, E], f32)
        XTW = XT[:, :, :, :].rearrange("p u c t -> p (u c t)")
        TN = NT * E
        TA = XTW[:, 0:TN].rearrange("p (t e) -> p t e", e=E)
        TB = XTW[:, TN:2 * TN].rearrange("p (t e) -> p t e", e=E)
        OH = XTW[:, 2 * TN:4 * TN].rearrange("p (k t e) -> p k t e", k=2, e=E)
        MK = sb("MK", [P, E, NT], bf16)
        ONES = sb("ONES", [P, E * NT], f32)
        SI = XTW[:, 4 * TN:5 * TN].rearrange("p (e t) -> p e t", e=E)
        SX = XTW[:, 5 * TN:6 * TN].rearrange("p (e t) -> p e t", e=E)
        SMALL = XTW[:, 6 * TN:6 * TN + 12 * NT].rearrange("p (k t) -> p k t", t=NT)
        MX, CM, SL, GA = SMALL[:, 0:2, :], SMALL[:, 2:4, :], SMALL[:, 4:6, :], SMALL[:, 6:12, :]
        IDX = sb("IDX", [P, B, 2, NT], i32)
        CNT = sb("CNT", [P, E], f32)
        CI = sb("CI", [P, E], i32)
        NTL = sb("NTL", [P, E], f32)
        TBI = sb("TBI", [P, E], f32)
        TBX = sb("TBX", [P, E], f32)
        OFF = sb("OFF", [P, E], f32)
        PD = sb("PD", [P, 3, E], f32)
        PIDX = sb("PIDX", [P, B, E], i32)
        CMP = KS[:, :, :, :].rearrange("p u t d -> p (u t d)")[:, 0:ST * E].rearrange("p (j e) -> p j e", e=E)
        EIDF = sb("EIDF", [P, NS], f32)
        EID = sb("EID", [P, NS], i32)
        REV = sb("REV", [P, E], f32)
        TOK = sb("TOK", [P, B * NT], f32)
        JROW = sb("JROW", [P, ST], f32)
        PCOL = sb("PCOL", [P, 1], f32)
        MT = sb("MT", [P, 2, 2], f32)
        YID = sb("YID", [P, 8, 1], i32)
        GATE = sb("GATE", [P, 8], f32)
        cut = [0]

        def region(words):
            a = cut[0]
            cut[0] += words
            return Qb[:, a:a + words]

        XG = region(8 * ROW).rearrange("p (j c) -> p j c", j=8)
        XGH = XG.bitcast(f16)
        XTF = region(2 * DC * P).bitcast(f16).rearrange("p (u s) -> p u s", u=2)
        RL = region(2 * H).rearrange("p (u h) -> p u h", u=2)
        H32 = region(2 * H).rearrange("p (u h) -> p u h", u=2)
        HHL = region(2 * H).bitcast(f16).rearrange("p (u s h) -> p u s h", u=2, s=2)
        YS = region(4 * D).rearrange("p (j d) -> p j d", j=4)
        C6 = region(4 * 6).rearrange("p (u d) -> p u d", u=4)
        CV = region(4 * 2).rearrange("p (u d) -> p u d", u=4)
        CW = region(4 * 8).rearrange("p (u d) -> p u d", u=4)
        YG = KS[:, :, :, :].rearrange("p u t d -> p (u t d)").rearrange("p (u k d) -> p u k d", u=4, k=2)
        SF = XTW[:, 0:4 * D].rearrange("p (u d) -> p u d", u=4)
        OF = XTW[:, 4 * D:8 * D].rearrange("p (u d) -> p u d", u=4)
        assert cut[0] <= DC * T
        YW = [w.bitcast(f32).rearrange("p (g k t d) -> p g k t d", g=NG // 2, k=2, t=GT) for w in (W1f, W2f)]

        PS = ctx.enter_context(nc.psum_tensor("PS", [P, 8, 512], f32))
        PS16 = PS[:, :, :].bitcast(f16)

        s_raw, s_bias = sem("s_raw"), sem("s_bias")
        s_x = [sem(f"s_x{i}") for i in range(4)]
        s_w = [sem(f"s_w{i}") for i in range(2)]
        s_tail = sem("s_tail")
        const_done, pool_chain, setup_chain = sem("const_done"), sem("pool_chain"), sem("setup_chain")
        set_mm, set_ev = sem("set_mm"), sem("set_ev")
        xt_mm, xt_ev, k_mm, k_ev, q_mm, q_ev, kx_mm, b_add = (sem(n) for n in (
            "xt_mm", "xt_ev", "k_mm", "k_ev", "q_mm", "q_ev", "kx_mm", "b_add"))
        m_mm, m_ev = sem("m_mm"), sem("m_ev")
        w_max, w_all, w_scale, w_hi, w_lo, w_step = (sem(n) for n in ("w_max", "w_all", "w_scale", "w_hi", "w_lo", "w_step"))
        u_mm, z_step, x2_done, st_step, var_rdy, sd_rdy, nw_step, rs_rdy, x1_rdy, hi_rdy, lo_rdy = (sem(n) for n in (
            "u_mm", "z_step", "x2_done", "st_step", "var_rdy", "sd_rdy", "nw_step", "rs_rdy", "x1_rdy", "hi_rdy", "lo_rdy"))
        r_step, ex_in, ex_out, mask_rdy, cnt_mm, r_done = (sem(n) for n in (
            "r_step", "ex_in", "ex_out", "mask_rdy", "cnt_mm", "r_done"))
        s_scat = [sem(f"s_scat{b}") for b in range(B)]
        s_g = [sem(f"s_g{i}") for i in range(4)]
        t_mm, t_ev, z_mm, z_ev, rt_mm, sq_ev, h_cp, h_ev, y_mm, y_ev, meta, meta_step = (sem(n) for n in (
            "t_mm", "t_ev", "z_mm", "z_ev", "rt_mm", "sq_ev", "h_cp", "h_ev", "y_mm", "y_ev", "meta", "meta_step"))
        s_y = [sem(f"s_y{i}") for i in range(4)]
        s_yg = [sem(f"s_yg{i}") for i in range(4)]
        s_o = [sem(f"s_o{i}") for i in range(4)]
        c_step, c_var, c_sd, cn_step, c_rs, c_out = (sem(n) for n in ("c_step", "c_var", "c_sd", "cn_step", "c_rs", "c_out"))
        s_yt = [sem(f"s_yt{i}") for i in range(2)]
        s_ot = [sem(f"s_ot{i}") for i in range(2)]
        y_sum, o_mm = sem("y_sum"), sem("o_mm")
        kap_step = sem("kap_step")

        block = ctx.enter_context(nc.Block())

        def each_group(eng, b, body):
            first = 0
            if b == 0:
                body(0, 0)
                body(1, 1)
                first = 1
            with eng.Fori(first, NG // 2) as i:
                for u in range(2):
                    body(i * 2 + (b * NG + u), u)

        @block.sync
        def _(sp):
            sp.dma_start(RAW[:, 0:6, :], w_qkv.rearrange("(a p) d -> p a d", p=P)).then_inc(s_raw, 16)
            sp.dma_start(RAW[:, 6:8, :], w_out.rearrange("(a p) d -> p a d", p=P)).then_inc(s_raw, 16)
            sp.dma_start(RR[:, :], router_w).then_inc(s_raw, 16)
            for g in range(4):
                sp.dma_start(X[:, g * GT:(g + 1) * GT, 0:D], xf[:, g * GT:(g + 1) * GT, :]).then_inc(s_x[g], 16)
            sp.dma_start(BCOL[:, :], b_out.rearrange("(c p) -> p c", p=P), allow_slow_non_contiguous=True).then_inc(s_bias, 16)
            sp.dma_start(BB[:, :], b_out.rearrange("(o d) -> o d", o=1).broadcast_to([P, D])).then_inc(s_bias, 16)

            sp.wait_ge(const_done, 1)
            for b in range(B):
                for j in range(E):
                    sp.dma_start(xs_v[:, b * ST + 2 * NT + j, :], PADROW[:, :]).then_inc(s_tail, 16)

            def load_expert(e, first):
                if not first:
                    sp.wait_ge(w_lo, 2 * e - 1)
                    sp.wait_ge(w_hi, 2 * e - 1)
                sp.dma_start(STG[:, 0, :].rearrange("p (c h) -> p c h", c=DC),
                             w1_in[ds(e, 1), :, :].rearrange("o (c p) h -> p (o c) h", p=P)).then_inc(s_w[0], 16)
                if not first:
                    sp.wait_ge(w_lo, 2 * e)
                    sp.wait_ge(w_hi, 2 * e)
                sp.dma_start(STG[:, 1, :].rearrange("p (c h) -> p c h", c=HC),
                             w2_in[ds(e, 1), :, :].rearrange("o (c p) h -> p (o c) h", p=P)).then_inc(s_w[1], 16)

            load_expert(0, True)
            with sp.Fori(1, 4) as i:
                for k in range(4):
                    sp.wait_ge(s_x[k], i * 16)
                    gi = i * 4 + k
                    sp.dma_start(X[:, ds(gi * GT, GT), 0:D], xf[:, ds(gi * GT, GT), :]).then_inc(s_x[k], 16)
            with sp.Fori(1, E) as e:
                load_expert(e, False)

            sp.wait_ge(s_scat[0], 16 * (2 * NT + E))
            sp.wait_ge(u_mm, B * NT)

            def load_pair(q, v, wait=True):
                if wait:
                    sp.wait_ge(meta, q - 3)
                sp.dma_start(XG[:, 2 * v:2 * v + 2, :], xs_v[:, ds(q * 2, 2), :]).then_inc(s_g[v], 16)

            for v in range(4):
                load_pair(v, v, False)
            with sp.Fori(1, ST // 8) as i:
                for v in range(4):
                    load_pair(i * 4 + v, v)
            sp.wait_ge(s_scat[1], 16 * (2 * NT + E))

            def load_rows(n, u, wait=True):
                if wait:
                    sp.wait_ge(c_step, n * 5 - 17)
                sp.dma_start(YG[:, u, :, :], yr_v[:, :, ds(n, 1), :].rearrange("p k o d -> p k (o d)")).then_inc(s_yg[u], 16)

            def store_rows(n, u):
                sp.wait_ge(c_out, n + 1)
                sp.dma_start(of[:, ds(n, 1), :].rearrange("p o d -> p (o d)"), OF[:, u, :]).then_inc(s_o[u], 16)

            Q1 = ST // 2
            for v in range(7):
                load_pair(Q1 + v, (Q1 + v) % 4)
            for v in range(4):
                sp.wait_ge(s_y[v], 16 * ST // 4)
            for n in range(4):
                load_rows(n, n, False)
            load_pair(Q1 + 7, 3)
            with sp.Fori(1, NT // 4) as i:
                for v in range(4):
                    load_pair(i * 4 + (Q1 + 4 + v), v)
                    store_rows(i * 4 + (v - 4), v)
                    load_rows(i * 4 + v, v)
            for v in range(4):
                store_rows(NT - 4 + v, v)
            for v in range(4):
                sp.wait_ge(s_y[v], B * 16 * ST // 4)
            sp.wait_ge(y_mm, NS)

            def store_group(g):
                sp.wait_ge(x1_rdy, (B * NG + g) + 1)
                sp.dma_start(of[:, NT + g * GT:NT + (g + 1) * GT, :], KS[:, g % 2, :, :]).then_inc(s_ot[g % 2], 16)

            for g in range(NG):
                if g >= 2:
                    sp.wait_ge(s_yt[g % 2], 32 * (g // 2))
                for k in range(2):
                    sp.dma_start(YW[g // 4][:, g % 4, k, :, :],
                                 yr_v[:, k, NT + g * GT:NT + (g + 1) * GT, :]).then_inc(s_yt[g % 2], 16)
                if g >= 3:
                    store_group(g - 3)
            for g in range(NG - 3, NG):
                store_group(g)
            for v in range(4):
                sp.wait_ge(s_o[v], 16 * NT // 4)
            for v in range(2):
                sp.wait_ge(s_ot[v], 16 * NG // 2)

        @block.gpsimd
        def _(pool):
            nc.gpsimd.memset(ID[:], 0.0)
            nc.gpsimd.memset(ZERO[:], 0.0)
            nc.gpsimd.memset(UPPER[:], 1.0)
            nc.gpsimd.memset(PADROW[:], 0.0).then_inc(pool_chain, 1)
            pool.wait_ge(pool_chain, 1)
            nc.gpsimd.affine_select(out=ID[:], in_=ID[:], compare_op=ALU.not_equal, fill=1.0, base=0,
                                    pattern=[[-1, P]], channel_multiplier=1)
            nc.gpsimd.affine_select(out=UPPER[:], in_=UPPER[:], compare_op=ALU.is_gt, fill=0.0, base=0,
                                    pattern=[[1, P]], channel_multiplier=-1)
            nc.gpsimd.memset(PADROW[:, D:D + 1], FAR)
            nc.gpsimd.memset(PADROW[:, D + 1:D + 2], -1.0)
            nc.gpsimd.iota(REV[:], [[-1, E]], base=E, channel_multiplier=0, allow_small_or_imprecise_dtypes=True)
            nc.gpsimd.iota(TOK[:], [[P, B * NT]], base=0, channel_multiplier=1, allow_small_or_imprecise_dtypes=True)
            nc.gpsimd.iota(JROW[:], [[1, ST]], base=0, channel_multiplier=0, allow_small_or_imprecise_dtypes=True)
            nc.gpsimd.iota(PCOL[:], [[0, 1]], base=0, channel_multiplier=1,
                           allow_small_or_imprecise_dtypes=True).then_inc(const_done, 1)

            for e in range(E):
                pool.wait_ge(w_max, e * 2 + 2)
                nc.gpsimd.partition_all_reduce(AMX[:, :], AM[:, :], P, bass.bass_isa.ReduceOp.absmax).then_inc(w_all, 1)

            def scatter_tile(b, t, k):
                nc.gpsimd.indirect_dma_start(
                    out=x_slots, out_offset=bass.IndirectOffsetOnAxis(ap=IDX[:, b, k, t:t + 1], axis=0),
                    in_=X[:, t + b * NT, :], in_offset=None).then_inc(s_scat[b], 16)

            def scatter_padding(b):
                for e in range(E):
                    nc.gpsimd.indirect_dma_start(
                        out=x_slots, out_offset=bass.IndirectOffsetOnAxis(ap=PIDX[:, b, e:e + 1], axis=0),
                        in_=PADROW[:, :], in_offset=None, bounds_check=NS * P - 1, oob_is_err=False).then_inc(s_scat[b], 16)

            def scatter_result(j, v):
                pool.wait_ge(y_ev, j + 1)
                nc.gpsimd.indirect_dma_start(
                    out=y_rows, out_offset=bass.IndirectOffsetOnAxis(ap=YID[:, j % 8, :], axis=0),
                    in_=YS[:, v, :], in_offset=None, bounds_check=last_row, oob_is_err=False).then_inc(s_y[v], 16)

            last_row = pool.to_reg(2 * B * T - 1)
            pool.wait_ge(s_tail, B * E * 16)
            pool.wait_ge(r_done, 1)
            scatter_padding(0)
            for t in range(NT):
                for k in range(2):
                    scatter_tile(0, t, k)
            pool.wait_ge(r_done, 2)
            scatter_padding(1)
            for t in range(NT):
                for k in range(2):
                    scatter_tile(1, t, k)
                for k in range(2):
                    scatter_result(t * 2 + k, (t * 2 + k) % 4)
            for j in range(2 * NT, NS):
                scatter_result(j, j % 4)

        @block.tensor
        def _(pe):
            pe.wait_ge(const_done, 1)
            pe.wait_ge(s_raw, 48)
            for n, a0 in enumerate((0, 2, 6)):
                for a in range(2):
                    for c in range(DC):
                        last = nc.tensor.transpose(PS[:, n, c * D + a * P:c * D + (a + 1) * P],
                                                   RAW[:, a0 + a, c * P:(c + 1) * P], ID[:])
                last.then_inc(set_mm, 1)
            for c in range(DC):
                last = nc.tensor.transpose(PS[:, 3, c * E:(c + 1) * E], RR[:, c * P:(c + 1) * P], ID[0:E, 0:E])
            last.then_inc(set_mm, 1)
            pe.wait_ge(set_ev, 4)
            for e in range(DC):
                for f in range(DC):
                    last = nc.tensor.matmul(PS[:, 4, e * E:(e + 1) * E], RAW[:, 6 + f, e * P:(e + 1) * P], RT[:, f, :],
                                            start=(f == 0), stop=(f == DC - 1))
            last.then_inc(set_mm, 1)
            pe.wait_ge(set_ev, 6)
            for c in range(DC):
                for e in range(DC):
                    last = nc.tensor.matmul(PS[:, 5 + c, 0:DR], RAW[:, 4 + e, c * P:(c + 1) * P], WOT[:, e, :],
                                            start=(e == 0), stop=(e == DC - 1))
            last.then_inc(set_mm, 1)
            for n in range(2):
                for f in range(DC):
                    last = nc.tensor.matmul(PS[:, 7, n * E:(n + 1) * E], LB[:, n, f, :], RT[:, f, :],
                                            start=(f == 0), stop=(f == DC - 1))
            last.then_inc(set_mm, 1)
            pe.wait_ge(set_ev, 8)

            def transpose_x(gi, k, first=False):
                pe.wait_ge(s_x[k], 16 * (gi // 4 + 1) if isinstance(gi, int) else (gi - k) * 4 + 16)
                for c in range(DC):
                    if not first:
                        pe.wait_ge(xt_ev, gi * 2 - 1 + c)
                    for t in range(GT):
                        last = nc.tensor.transpose(PS[:, c, t * P:(t + 1) * P],
                                                   X[:, ds(gi * GT + t, 1), c * P:(c + 1) * P].rearrange("p o c -> p (o c)"), ID[:])
                    last.then_inc(xt_mm, 1)

            def project(gi, u, first=False):
                pe.wait_ge(xt_ev, gi * 2 + 2)
                for t in range(GT):
                    if not (first and t < 2):
                        pe.wait_ge(k_ev, gi * GT + (t - 1))
                    for c in range(DC):
                        last = nc.tensor.matmul(PS[:, 2 + t % 2, 0:DR], XT[:, u, c, t * P:(t + 1) * P], WKR[:, c, :],
                                                start=(c == 0), stop=(c == DC - 1))
                    last.then_inc(k_mm, 1)
                for m in range(DC):
                    if not first:
                        pe.wait_ge(q_ev, gi * 2 + (m - 1))
                    for c in range(DC):
                        last = nc.tensor.matmul(PS[:, 4 + m, :], WQT[:, c, m * P:(m + 1) * P], XT[:, u, c, :],
                                                start=(c == 0), stop=(c == DC - 1))
                    last.then_inc(q_mm, 1)
                for t in range(GT):
                    pe.wait_ge(k_ev, gi * GT + (t + 1))
                    for m in range(DC):
                        last = nc.tensor.matmul(PS[:, 6 + m, 0:D + 2], KS[:, u, t, m * P:(m + 1) * P],
                                                X[:, ds(gi * GT + t, 1), 0:D + 2].rearrange("p o c -> p (o c)"),
                                                start=False, stop=False, skip_group_check=True)
                last.then_inc(kx_mm, 1)

            def attention_sums(b):
                g0 = b * NG
                if b > 0:
                    pe.wait_ge(r_done, b)
                for m in range(DC):
                    nc.tensor.matmul(PS[:, 6 + m, 0:D + 2], ZERO[:, 0:P], ZERO[:, :], start=True, stop=False, skip_group_check=True)
                transpose_x(g0, 0, first=(b == 0))
                for g in range(g0, g0 + NG):
                    if g + 1 < g0 + NG:
                        transpose_x(g + 1, (g + 1) % 4)
                    project(g, g % 2, first=(g == 0))
                for m in range(DC):
                    last = nc.tensor.matmul(PS[:, 6 + m, 0:D + 2], ZERO[:, 0:P], ZERO[:, :], start=False, stop=True, skip_group_check=True)
                last.then_inc(m_mm, 1)
                pe.wait_ge(m_ev, 3 * b + 1)
                for m in range(DC):
                    for c in range(DC):
                        last = nc.tensor.transpose(PS[:, 0, c * D + m * P:c * D + (m + 1) * P], KXS[:, m, c * P:(c + 1) * P], ID[:])
                last.then_inc(m_mm, 1)
                pe.wait_ge(m_ev, 3 * b + 2)
                for m in range(DC):
                    for c in range(DC):
                        last = nc.tensor.matmul(PS[:, 1 + m, 0:DR], KXT[:, c, m * P:(m + 1) * P], G[:, c, :],
                                                start=(c == 0), stop=(c == DC - 1))
                last.then_inc(m_mm, 1)
                pe.wait_ge(m_ev, 3 * b + 3)

            def apply_m(b):
                for g in range(NG):
                    if g >= 2:
                        pe.wait_ge(x2_done, b * NG + g - 1)
                    for t in range(GT):
                        for m in range(DC):
                            last = nc.tensor.matmul(PS[:, 4 * (g % 2) + t, 0:DR + 1], Q[:, m, (g * GT + t) * P:(g * GT + t + 1) * P],
                                                    MQ[:, m, 0:DR + 1], start=(m == 0), stop=(m == DC - 1))
                        last.then_inc(u_mm, 1)

            def count_slots(b):
                pe.wait_ge(mask_rdy, b + 1)
                nc.tensor.matmul(PS[:, 0, 0:E * NT], UPPER[:], MK[:, :, :].rearrange("p e t -> p (e t)"), start=True, stop=True)
                nc.tensor.matmul(PS[:, 1, 0:E * NT], ONESB[:], MK[:, :, :].rearrange("p e t -> p (e t)"),
                                 start=True, stop=True).then_inc(cnt_mm, 1)

            attention_sums(0)
            apply_m(0)
            count_slots(0)
            attention_sums(1)
            apply_m(1)
            count_slots(1)
            pe.wait_ge(r_done, 2)

            def slots_transpose(j, v, first=False):
                if v % 2 == 0:
                    pe.wait_ge(s_g[v // 2], 16 * (j // 8 + 1) if isinstance(j, int) else (j - v) * 2 + 16)
                if not first:
                    pe.wait_ge(t_ev, j - 1)
                for c in range(DC):
                    for s in range(2):
                        last = nc.tensor.transpose(PS16[:, v % 2, (2 * c + s) * P:(2 * c + s + 1) * P],
                                                   XGH[:, v, s * D + c * P:s * D + (c + 1) * P], ID16[:])
                last.then_inc(t_mm, 1)

            THREE = ((0, 0), (0, 1), (1, 0))

            def first_product(j, v, w, first=False):
                pe.wait_ge(t_ev, j + 1)
                if not first:
                    pe.wait_ge(z_ev, j - 1)
                n = 0
                for c in range(DC):
                    for xp, wp in THREE:
                        last = nc.tensor.matmul(PS[:, 2 + v % 2, :], XTF[:, v % 2, (2 * c + xp) * P:(2 * c + xp + 1) * P],
                                                W1f[:, ds(w + (2 * c + wp) * H, H)],
                                                start=(n == 0), stop=(n == 3 * DC - 1))
                        n += 1
                last.then_inc(z_mm, 1)

            def relu_transpose(j, v, first=False):
                pe.wait_ge(z_ev, j + 1)
                if not first:
                    pe.wait_ge(sq_ev, j - 1)
                for c in range(HC):
                    last = nc.tensor.transpose(PS[:, 4 + v % 2, c * P:(c + 1) * P], RL[:, v % 2, c * P:(c + 1) * P], ID[:])
                last.then_inc(rt_mm, 1)

            def second_product(j, v, w, first=False):
                pe.wait_ge(h_ev, j + 1)
                if not first:
                    pe.wait_ge(y_ev, j - 1)
                n = 0
                for c in range(HC):
                    for hp, wp in THREE:
                        last = nc.tensor.matmul(PS[:, 6 + v % 2, 0:D], HHL[:, v % 2, hp, c * P:(c + 1) * P],
                                                W2f[:, ds(w + (2 * c + wp) * D, D)],
                                                start=(n == 0), stop=(n == 3 * HC - 1))
                        n += 1
                last.then_inc(y_mm, 1)

            def weights_of(first, n):
                return nc.values_load_multi_w_load_instructions(
                    EID[0:1, ds(first, n)], engines=[mybir.EngineType.PE], min_val=0, max_val=(E - 1) * EW,
                    skip_runtime_bounds_check_because="route() counts from 1 to E experts at or before each tile")[1]

            def step(s, k, w1, w2):
                known = isinstance(s, int)
                if not known or s < NS:
                    slots_transpose(s, k, first=known and s < 2)
                if not known or 0 <= s - 1 < NS:
                    first_product(s - 1, (k - 1) % 8, w1, first=known and s - 1 < 2)
                if not known or 0 <= s - 2 < NS:
                    relu_transpose(s - 2, (k - 2) % 8, first=known and s - 2 < 2)
                if not known or 0 <= s - 3 < NS:
                    second_product(s - 3, (k - 3) % 8, w2, first=known and s - 3 < 2)

            w = weights_of(0, 7)
            for s in range(8):
                step(s, s, w[max(s - 1, 0)], w[max(s - 3, 0)])
            with pe.Fori(1, NS // 8) as i:
                w = weights_of(i * 8 - 3, 10)
                for k in range(8):
                    step(i * 8 + k, k, w[k + 2], w[k])
            w = weights_of(NS - 3, 3)
            for k in range(3):
                step(NS + k, k, w[min(k + 2, 2)], w[k])

            pe.wait_ge(y_ev, NS)
            for g in range(NG):
                if g >= 2:
                    pe.wait_ge(x1_rdy, B * NG + g - 1)
                pe.wait_ge(y_sum, g + 1)
                for t in range(GT):
                    n, bank = NT + g * GT + t, PS[:, 4 * (g % 2) + t, 0:D]
                    nc.tensor.matmul(bank, ID16[:], XH[:, n, 0:D], start=True, stop=False)
                    nc.tensor.matmul(bank, ID16[:], XH[:, n, D:2 * D], start=False, stop=False)
                    nc.tensor.matmul(bank, ID[:], YW[g // 4][:, g % 4, 0, t, :], start=False, stop=True).then_inc(o_mm, 1)

        @block.scalar
        def _(act):
            def sums_part(gi, u):
                first = isinstance(gi, int) and gi < 2
                for c in range(DC):
                    act.wait_ge(xt_mm, gi * 2 + (c + 1))
                    if not first and c == 0:
                        act.wait_ge(q_mm, gi * 2 - 2)
                    nc.scalar.copy(XT[:, u, c, :], PS[:, c, :]).then_inc(xt_ev, 1)

            def expert_part(e):
                act.wait_ge(w_scale, e + 1)
                nc.scalar.activation(W1[:, ds(e, 1), :, 0, :].rearrange("p o c h -> p (o c) h"),
                                     STG[:, 0, :].rearrange("p (c h) -> p c h", c=DC), ACT.Copy,
                                     scale=SG[:, 0, 0:1]).then_inc(w_hi, 1)
                nc.scalar.activation(W2[:, ds(e, 1), :, 0, :].rearrange("p o c h -> p (o c) h"),
                                     STG[:, 1, :].rearrange("p (c h) -> p c h", c=HC), ACT.Copy,
                                     scale=SG[:, 0, 1:2]).then_inc(w_hi, 1)

            def both(gi, u):
                sums_part(gi, u)
                expert_part(gi)

            def norm_sqrt(gi, b):
                act.wait_ge(var_rdy, gi + 1)
                nc.scalar.activation(SD[:, ds((gi - b * NG) * GT, GT)], VAR[:, ds((gi - b * NG) * GT, GT)],
                                     ACT.Sqrt).then_inc(sd_rdy, 1)

            def norm_apply(gi, u, b):
                act.wait_ge(rs_rdy, gi + 1)
                for t in range(GT):
                    last = nc.scalar.activation(KS[:, u, t, :], X[:, ds(gi * GT + t, 1), 0:D].rearrange("p o c -> p (o c)"),
                                                ACT.Identity, bias=NB[:, u, t:t + 1], scale=RS2[:, u, t:t + 1])
                last.then_inc(x1_rdy, 1)
                act.wait_ge(x1_rdy, gi + 1)
                nc.scalar.copy(XH[:, ds(gi * GT, GT), 0:D], KS[:, u, :, :]).then_inc(hi_rdy, 1)

            def norm_part(b):
                g0 = b * NG
                norm_sqrt(g0, b)
                for g in range(1, NG):
                    norm_sqrt(g0 + g, b)
                    norm_apply(g0 + g - 1, (g - 1) % 2, b)
                norm_apply(g0 + NG - 1, (NG - 1) % 2, b)
                act.wait_ge(ex_in, b + 1)
                nc.scalar.activation(GA[:, 1, :], GA[:, 0, :], ACT.Exp).then_inc(ex_out, 1)

            each_group(act, 0, both)
            norm_part(0)
            each_group(act, 1, sums_part)
            norm_part(1)

            def act_relu(j, v):
                act.wait_ge(z_mm, j + 1)
                if not (isinstance(j, int) and j < 2):
                    act.wait_ge(rt_mm, j - 1)
                nc.scalar.activation(RL[:, v % 2, :], PS[:, 2 + v % 2, :], ACT.Relu, scale=R_SCALE).then_inc(z_ev, 1)

            def act_square(j, v):
                act.wait_ge(rt_mm, j + 1)
                if not (isinstance(j, int) and j < 2):
                    act.wait_ge(h_ev, j - 1)
                nc.scalar.activation(H32[:, v % 2, :], PS[:, 4 + v % 2, :], ACT.Square).then_inc(sq_ev, 1)

            def act_step(s, k, pair=None):
                known = isinstance(s, int)
                if not known or 0 <= s - 1 < NS:
                    act_relu(s - 1, (k - 1) % 8)
                if not known or 0 <= s - 2 < NS:
                    act_square(s - 2, (k - 2) % 8)
                if not known or 0 <= s - 3 < NS:
                    j, v = s - 3, (k - 3) % 8
                    act.wait_ge(y_mm, j + 1)
                    if v % 2 == 0:
                        act.wait_ge(meta, j // 2 + 1 if known else pair)
                    if not (known and j < 4):
                        act.wait_ge(s_y[v % 4], 16 * (j // 4) if known else (j - v % 4) * 4)
                    nc.scalar.activation(YS[:, v % 4, :], PS[:, 6 + v % 2, 0:D], ACT.Copy, scale=GATE[:, v:v + 1]).then_inc(y_ev, 1)

            def out_sqrt(n, u):
                act.wait_ge(c_var, n + 1)
                nc.scalar.activation(CW[:, u, 1:2], CW[:, u, 0:1], ACT.Sqrt).then_inc(c_sd, 1)

            def out_apply(n, u):
                act.wait_ge(c_rs, n + 1)
                if not (isinstance(n, int) and n < 4):
                    act.wait_ge(s_o[u], 16 * (n // 4) if isinstance(n, int) else (n - u) * 4)
                nc.scalar.activation(OF[:, u, :], SF[:, u, :], ACT.Identity, bias=CW[:, u, 7:8], scale=CW[:, u, 6:7]).then_inc(c_out, 1)

            for s in range(8):
                act_step(s, s)
            with act.Fori(1, ST // 8 + 1) as i:
                for k in range(8):
                    act_step(i * 8 + k, k, pair=i * 4 + ((k - 3) // 2 + 1))

            def with_output(i, n, first=False):
                for k in range(8):
                    act_step(i * 8 + k, k, pair=i * 4 + ((k - 3) // 2 + 1))
                    if k % 2 == 1:
                        out_sqrt(n + k // 2, k // 2)
                    elif not (first and k == 0):
                        out_apply(n + (k // 2 - 1), (k // 2 - 1) % 4)

            with_output(ST // 8 + 1, 0, True)
            with act.Fori(1, NT // 4) as i:
                with_output(i + (ST // 8 + 1), i * 4)
            out_apply(NT - 1, 3)
            for s in range(NS, NS + 3):
                act_step(s, s % 8)

            def out_group(g):
                u = g % 2
                act.wait_ge(rs_rdy, B * NG + g + 1)
                if g >= 2:
                    act.wait_ge(s_ot[u], 16 * (g // 2))
                for t in range(GT):
                    last = nc.scalar.activation(KS[:, u, t, :], PS[:, 4 * u + t, 0:D], ACT.Identity,
                                                bias=NB[:, u, t:t + 1], scale=RS2[:, u, t:t + 1])
                last.then_inc(x1_rdy, 1)

            norm_sqrt(B * NG, B)
            for g in range(1, NG):
                norm_sqrt(B * NG + g, B)
                out_group(g - 1)
            out_group(NG - 1)

        @block.vector
        def _(dve):
            V = nc.vector

            def bc(ap, shape):
                return ap.broadcast_to(shape)

            nc.vector.memset(ONESB[:], 1.0)
            nc.vector.memset(ONES[:], 1.0)
            nc.vector.memset(LB[:, 0, :, :], 1.0)
            nc.vector.memset(X[:, :, D:D + 1], 1.0)
            nc.vector.memset(X[:, :, D + 1:D + 2], 0.0)
            dve.wait_ge(const_done, 1)
            V.tensor_copy(ID16[:], ID[:]).then_inc(setup_chain, 1)
            dve.wait_ge(set_mm, 1)
            V.tensor_copy(WQT[:, :, :], PS[:, 0, :].rearrange("p (c d) -> p c d", c=DC)).then_inc(set_ev, 1)
            dve.wait_ge(set_mm, 2)
            V.tensor_copy(WKR[:, :, 0:D], PS[:, 1, :].rearrange("p (c d) -> p c d", c=DC)).then_inc(set_ev, 1)
            dve.wait_ge(set_mm, 3)
            V.tensor_copy(WOT[:, :, 0:D], PS[:, 2, :].rearrange("p (c d) -> p c d", c=DC)).then_inc(set_ev, 1)
            dve.wait_ge(set_mm, 4)
            V.tensor_copy(WKR[:, :, D:DR], PS[:, 3, 0:DC * E].rearrange("p (c d) -> p c d", c=DC))
            V.tensor_copy(RT[:, :, :], PS[:, 3, 0:DC * E].rearrange("p (c d) -> p c d", c=DC)).then_inc(set_ev, 1)
            dve.wait_ge(s_bias, 32)
            V.tensor_copy(LB[:, 1, :, :], bc(BCOL[:, :].rearrange("p (c o) -> p c o", o=1), [P, DC, P])).then_inc(set_ev, 1)
            dve.wait_ge(set_mm, 5)
            V.tensor_copy(WOT[:, :, D:DR], PS[:, 4, 0:DC * E].rearrange("p (c d) -> p c d", c=DC)).then_inc(set_ev, 1)
            dve.wait_ge(set_mm, 6)
            V.tensor_copy(G[:, :, :], PS[:, 5:5 + DC, 0:DR]).then_inc(set_ev, 1)
            dve.wait_ge(set_mm, 7)
            V.tensor_copy(SRBR[:, :, :], PS[:, 7, 0:2 * E].rearrange("p (n e) -> p n e", n=2)).then_inc(set_ev, 1)

            def expert_max(e):
                for k in range(2):
                    dve.wait_ge(s_w[k], e * 16 + 16)
                    if k == 0 and not (isinstance(e, int) and e == 0):
                        dve.wait_ge(w_all, e)
                    V.tensor_reduce(AM[:, k:k + 1], STG[:, k, :], AX.X, ALU.max, apply_absolute_value=True).then_inc(w_max, 1)

            def expert_scale(e):
                dve.wait_ge(w_all, e + 1)
                p2 = P2[:, ds(e, 1), :].rearrange("p o k -> p (o k)")
                V.tensor_scalar(AMX[:, :], AMX[:, :], TINY, None, ALU.max).then_inc(w_step, 1)
                dve.wait_ge(w_step, e * 3 + 1)
                V.tensor_scalar(PW[:, :].bitcast(i32), AMX[:, :].bitcast(i32), 0x7F800000, None, ALU.bitwise_and).then_inc(w_step, 1)
                dve.wait_ge(w_step, e * 3 + 2)
                V.reciprocal(SG[:, 1, :], PW[:, :]).then_inc(w_step, 1)
                V.tensor_copy(p2, PW[:, :])
                dve.wait_ge(w_step, e * 3 + 3)
                if not (isinstance(e, int) and e == 0):
                    dve.wait_ge(w_hi, e * 2)
                V.tensor_scalar(SG[:, 0, :], SG[:, 1, :], 2.0 ** 14, None, ALU.mult).then_inc(w_scale, 1)

            def expert_low(e):
                dve.wait_ge(w_scale, e + 1)
                for k, (W, C) in enumerate(((W1, DC), (W2, HC))):
                    dve.wait_ge(w_hi, e * 2 + (k + 1))
                    V.scalar_tensor_tensor(
                        out=W[:, ds(e, 1), :, 1, :].rearrange("p o c h -> p (o c) h"),
                        in0=STG[:, k, :].rearrange("p (c h) -> p c h", c=C), scalar=SG[:, 0, k:k + 1],
                        in1=W[:, ds(e, 1), :, 0, :].rearrange("p o c h -> p (o c) h"),
                        op0=ALU.mult, op1=ALU.subtract).then_inc(w_lo, 1)

            def sums_part(gi, u, b):
                first = isinstance(gi, int) and gi < 2
                if b == 0:
                    expert_max(gi)
                for t in range(GT):
                    dve.wait_ge(k_mm, gi * GT + (t + 1))
                    if t == 0 and not first:
                        dve.wait_ge(kx_mm, gi - 1)
                    V.tensor_copy(XR[:, ds((gi - b * NG) * GT + t, 1), :].rearrange("p o e -> p (o e)"), PS[:, 2 + t % 2, D:DR])
                    V.tensor_scalar(KS[:, u, t, :], PS[:, 2 + t % 2, 0:D], 0.0, EPS, ALU.max, ALU.add).then_inc(k_ev, 1)
                if b == 0:
                    expert_scale(gi)
                for m in range(DC):
                    dve.wait_ge(q_mm, gi * 2 + (m + 1))
                    V.tensor_scalar(Q[:, m, ds((gi - b * NG) * (GT * P), GT * P)], PS[:, 4 + m, :], 0.0, EPS,
                                    ALU.max, ALU.add).then_inc(q_ev, 1)
                if b == 0:
                    expert_low(gi)
                dve.wait_ge(kx_mm, gi + 1)
                V.tensor_tensor(X[:, ds(gi * GT, GT), 0:D], X[:, ds(gi * GT, GT), 0:D],
                                bc(BB[:, :].rearrange("p (o d) -> p o d", o=1), [P, GT, D]), ALU.add).then_inc(b_add, 1)

            def make_m(b):
                dve.wait_ge(m_mm, 3 * b + 1)
                V.tensor_copy(KXS[:, :, :], PS[:, 6:6 + DC, 0:D + 2]).then_inc(m_ev, 1)
                dve.wait_ge(m_mm, 3 * b + 2)
                V.tensor_copy(KXT[:, :, :], PS[:, 0, :].rearrange("p (c d) -> p c d", c=DC)).then_inc(m_ev, 1)
                dve.wait_ge(m_mm, 3 * b + 3)
                V.tensor_copy(MQ[:, :, DEN:DEN + 1], KXS[:, :, D:D + 1])
                V.tensor_copy(MQ[:, :, 0:DR], PS[:, 1:1 + DC, 0:DR]).then_inc(m_ev, 1)

            def residual_stats(b, g):
                gi, u = b * NG + g, g % 2
                dve.wait_ge(u_mm, gi * GT + GT)
                V.tensor_scalar(ZT[:, u, :], PS[:, 4 * u:4 * u + GT, DEN:DEN + 1].rearrange("p t o -> p (t o)"), EPS, None,
                                ALU.add).then_inc(z_step, 1)
                dve.wait_ge(z_step, gi * 2 + 1)
                V.reciprocal(ZR[:, u, :], ZT[:, u, :]).then_inc(z_step, 1)
                dve.wait_ge(z_step, gi * 2 + 2)
                dve.wait_ge(b_add, gi + 1)
                V.tensor_tensor(LG[:, g * GT:(g + 1) * GT, :], PS[:, 4 * u:4 * u + GT, D:DR],
                                bc(ZR[:, u, :].rearrange("p (t o) -> p t o", o=1), [P, GT, E]), ALU.mult)
                for t in range(GT):
                    x = X[:, gi * GT + t, 0:D]
                    last = V.scalar_tensor_tensor(out=x, in0=PS[:, 4 * u + t, 0:D], scalar=ZR[:, u, t:t + 1], in1=x,
                                                  op0=ALU.mult, op1=ALU.add)
                last.then_inc(x2_done, 1)
                dve.wait_ge(x2_done, gi + 1)
                for t in range(GT):
                    last = V.bn_stats(ST6[:, u, t, :], X[:, gi * GT + t, 0:D])
                last.then_inc(st_step, 1)
                dve.wait_ge(st_step, gi * 2 + 1)
                for t in range(GT):
                    last = V.bn_aggr(MV[:, u, t, :], ST6[:, u, t, :])
                last.then_inc(st_step, 1)
                dve.wait_ge(st_step, gi * 2 + 2)
                V.tensor_scalar(VAR[:, g * GT:(g + 1) * GT], MV[:, u, :, 1:2].rearrange("p t o -> p (t o)"), EPS_LN, None,
                                ALU.add).then_inc(var_rdy, 1)

            def inverse_std(b, g, scale=XS):
                gi, u = b * NG + g, g % 2
                own = slice(g * GT, (g + 1) * GT)
                n = [gi * 5]

                def then(ins):
                    ins.then_inc(nw_step, 1)
                    n[0] += 1
                    dve.wait_ge(nw_step, n[0])

                dve.wait_ge(sd_rdy, gi + 1)
                then(V.reciprocal(NW[:, 0, :], SD[:, own]))
                then(V.tensor_tensor(NW[:, 1, :], NW[:, 0, :], NW[:, 0, :], ALU.mult))
                then(V.tensor_tensor(NW[:, 2, :], NW[:, 1, :], VAR[:, own], ALU.mult))
                then(V.tensor_scalar(NW[:, 3, :], NW[:, 2, :], -0.5, 1.5, ALU.mult, ALU.add))
                if b < B:
                    V.tensor_copy(MEAN[:, own], MV[:, u, :, 0:1].rearrange("p t o -> p (t o)"))
                    V.tensor_tensor(RSTD[:, own], NW[:, 0, :], NW[:, 3, :], ALU.mult)
                then(V.scalar_tensor_tensor(out=RS2[:, u, :], in0=NW[:, 0, :], scalar=scale, in1=NW[:, 3, :],
                                            op0=ALU.mult, op1=ALU.mult))
                V.scalar_tensor_tensor(out=NB[:, u, :], in0=RS2[:, u, :], scalar=-1.0,
                                       in1=MV[:, u, :, 0:1].rearrange("p t o -> p (t o)"),
                                       op0=ALU.mult, op1=ALU.mult).then_inc(rs_rdy, 1)

            def low_part(b, g):
                gi, u = b * NG + g, g % 2
                dve.wait_ge(hi_rdy, gi + 1)
                own = slice(gi * GT, (gi + 1) * GT)
                V.tensor_tensor(XH[:, own, D:2 * D], KS[:, u, :, :], XH[:, own, 0:D], ALU.subtract).then_inc(lo_rdy, 1)

            R_STEPS = 49

            def route(b):
                n = [b * R_STEPS]

                def then(ins):
                    ins.then_inc(r_step, 1)
                    n[0] += 1
                    dve.wait_ge(r_step, n[0])

                TE = [P, NT, E]

                def over_t(row):
                    return bc(row.rearrange("p (o e) -> p o e", o=1), TE)

                def over_e(col):
                    return bc(col.rearrange("p (t o) -> p t o", o=1), TE)

                def flat(a):
                    return a.rearrange("p e t -> p (e t)")

                if b == 0:
                    dve.wait_ge(w_lo, 2 * E)
                    V.scalar_tensor_tensor(out=KAP[:, :], in0=P2[:, :, 0:1].rearrange("p e o -> p (e o)"), scalar=XS * 2.0 ** -10,
                                           in1=P2[:, :, 0:1].rearrange("p e o -> p (e o)"), op0=ALU.mult, op1=ALU.mult).then_inc(kap_step, 1)
                    dve.wait_ge(kap_step, 1)
                    V.tensor_tensor(KAP[:, :], KAP[:, :], P2[:, :, 1:2].rearrange("p e o -> p (e o)"), ALU.mult).then_inc(kap_step, 1)
                    dve.wait_ge(kap_step, 2)
                dve.wait_ge(rs_rdy, (b + 1) * NG)
                then(V.tensor_tensor(TA[:, :, :], LG[:, :, :], XR[:, :, :], ALU.add))
                then(V.tensor_tensor(TA[:, :, :], TA[:, :, :], over_t(SRBR[:, 1, :]), ALU.add))
                then(V.tensor_tensor(TB[:, :, :], over_e(MEAN[:, :]), over_t(SRBR[:, 0, :]), ALU.mult))
                then(V.tensor_tensor(TA[:, :, :], TA[:, :, :], TB[:, :, :], ALU.subtract))
                then(V.tensor_tensor(TA[:, :, :], TA[:, :, :], over_e(RSTD[:, :]), ALU.mult))
                for k in range(2):
                    then(V.tensor_reduce(MX[:, k, :], TA[:, :, :], AX.X, ALU.max))
                    then(V.tensor_tensor(TB[:, :, :], TA[:, :, :], over_e(MX[:, k, :]), ALU.is_equal))
                    then(V.tensor_tensor(TB[:, :, :], TB[:, :, :], over_t(REV[:, :]), ALU.mult))
                    then(V.tensor_reduce(CM[:, k, :], TB[:, :, :], AX.X, ALU.max))
                    then(V.tensor_tensor(OH[:, k, :, :], over_t(REV[:, :]), over_e(CM[:, k, :]), ALU.is_equal))
                    if k == 0:
                        then(V.scalar_tensor_tensor(out=TA[:, :, :], in0=OH[:, 0, :, :], scalar=-3.0e38, in1=TA[:, :, :],
                                                    op0=ALU.mult, op1=ALU.add))
                V.tensor_tensor(MK[:, :, :].rearrange("p e t -> p t e"), OH[:, 0, :, :], OH[:, 1, :, :], ALU.add).then_inc(mask_rdy, 1)
                V.tensor_tensor(GA[:, 0, :], MX[:, 1, :], MX[:, 0, :], ALU.subtract).then_inc(ex_in, 1)
                dve.wait_ge(cnt_mm, b + 1)
                then(V.tensor_tensor_scan(flat(SI[:, :, :]), ONES[:, :], PS[:, 1, 0:E * NT], 0.0, ALU.mult, ALU.add))
                then(V.tensor_tensor(flat(SX[:, :, :]), flat(SI[:, :, :]), PS[:, 1, 0:E * NT], ALU.subtract))
                start_e = SX[:, :, 0:1].rearrange("p e o -> p (e o)")
                then(V.tensor_tensor(CNT[:, :], SI[:, :, NT - 1:NT].rearrange("p e o -> p (e o)"), start_e, ALU.subtract))
                then(V.tensor_scalar(CI[:, :], CNT[:, :], float(P - 1), None, ALU.add))
                then(V.tensor_scalar(CI[:, :], CI[:, :], 7, None, ALU.arith_shift_right))
                then(V.tensor_copy(NTL[:, :], CI[:, :]))
                then(V.tensor_tensor_scan(TBI[:, :], ONES[:, 0:E], NTL[:, :], 0.0, ALU.mult, ALU.add))
                then(V.tensor_tensor(TBX[:, :], TBI[:, :], NTL[:, :], ALU.subtract))
                then(V.tensor_scalar(PD[:, 0, :], TBX[:, :], float(P), float(b * ST * P), ALU.mult, ALU.add))
                then(V.tensor_tensor(OFF[:, :], PD[:, 0, :], start_e, ALU.subtract))
                then(V.tensor_tensor(flat(SX[:, :, :]), flat(SX[:, :, :]), PS[:, 0, 0:E * NT], ALU.add))
                pos = SX[:, :, :].rearrange("p e t -> p t e")
                then(V.tensor_tensor(TB[:, :, :], pos, over_t(OFF[:, :]), ALU.add))
                for k in range(2):
                    then(V.tensor_tensor(TA[:, :, :], TB[:, :, :], OH[:, k, :, :], ALU.mult))
                    then(V.tensor_reduce(SL[:, k, :], TA[:, :, :], AX.X, ALU.add))
                V.tensor_copy(IDX[:, b, :, :], SL[:, :, :])
                then(V.tensor_tensor(PD[:, 1, :], CNT[:, :], PD[:, 0, :], ALU.add))
                then(V.tensor_scalar(PD[:, 1, :], PD[:, 1, :], PCOL[:, 0:1], None, ALU.add))
                then(V.scalar_tensor_tensor(out=PD[:, 2, :], in0=NTL[:, :], scalar=float(P), in1=PD[:, 0, :],
                                            op0=ALU.mult, op1=ALU.add))
                then(V.tensor_tensor(PD[:, 2, :], PD[:, 1, :], PD[:, 2, :], ALU.is_ge))
                V.scalar_tensor_tensor(out=PIDX[:, b, :], in0=PD[:, 2, :], scalar=FAR, in1=PD[:, 1, :], op0=ALU.mult, op1=ALU.add)
                then(V.tensor_tensor(CMP[:, :, :], bc(JROW[:, :].rearrange("p (j o) -> p j o", o=1), [P, ST, E]),
                                     bc(TBX[:, :].rearrange("p (o e) -> p o e", o=1), [P, ST, E]), ALU.is_ge))
                own = slice(b * ST, (b + 1) * ST)
                then(V.tensor_reduce(EIDF[:, own], CMP[:, :, :], AX.X, ALU.add))
                then(V.tensor_scalar(EIDF[:, own], EIDF[:, own], -1.0, None, ALU.add))
                then(V.tensor_scalar(EID[:, own], EIDF[:, own], float(EW), None, ALU.mult))
                dve.wait_ge(ex_out, b + 1)
                then(V.tensor_scalar(GA[:, 2, :], GA[:, 1, :], 1.0, None, ALU.add))
                then(V.reciprocal(GA[:, 3, :], GA[:, 2, :]))
                then(V.tensor_tensor(GA[:, 4, :], GA[:, 3, :], GA[:, 1, :], ALU.mult))
                for k in range(2):
                    then(V.tensor_tensor(TA[:, :, :], OH[:, k, :, :], over_t(KAP[:, :]), ALU.mult))
                    then(V.tensor_reduce(SL[:, k, :], TA[:, :, :], AX.X, ALU.add))
                    then(V.tensor_tensor(GA[:, 3 + k, :], GA[:, 3 + k, :], SL[:, k, :], ALU.mult))
                dve.wait_ge(lo_rdy, (b + 1) * NG)
                rows = slice(b * NT, (b + 1) * NT)

                def field(k):
                    return X[:, rows, D + k:D + k + 1].rearrange("p t o -> p (t o)")

                V.tensor_copy(field(0), TOK[:, rows])
                V.tensor_scalar(field(1), CM[:, 0, :], -1.0, float(E), ALU.mult, ALU.add)
                V.tensor_copy(field(2), GA[:, 3, :])
                V.tensor_tensor(field(3), GA[:, 4, :], GA[:, 3, :], ALU.subtract).then_inc(r_done, 1)
                assert n[0] == (b + 1) * R_STEPS

            def norm_part(b):
                for g in range(NG):
                    residual_stats(b, g)
                    if g >= 2:
                        low_part(b, g - 2)
                    if g >= 1:
                        inverse_std(b, g - 1)
                inverse_std(b, NG - 1)
                low_part(b, NG - 2)
                low_part(b, NG - 1)

            for b in range(B):
                each_group(dve, b, lambda gi, u: sums_part(gi, u, b))
                make_m(b)
                norm_part(b)
                route(b)

            def rows_out(j, v, first=False):
                dve.wait_ge(t_mm, j + 1)
                if not first:
                    dve.wait_ge(z_mm, j - 1)
                V.tensor_copy(XTF[:, v % 2, :], PS16[:, v % 2, 0:2 * D]).then_inc(t_ev, 1)

            def pair_meta(q, v):
                j = 2 * v
                if not (isinstance(q, int) and q < 4):
                    dve.wait_ge(y_ev, q * 2 - 2)
                V.tensor_tensor(MT[:, 0, :], XG[:, j:j + 2, D + 1:D + 2].rearrange("p j o -> p (j o)"), EIDF[:, ds(q * 2, 2)],
                                ALU.not_equal).then_inc(meta_step, 1)
                dve.wait_ge(meta_step, q * 2 + 1)
                V.scalar_tensor_tensor(out=YID[:, j:j + 2, :].rearrange("p j o -> p (j o)"), in0=MT[:, 0, :], scalar=float(B * T),
                                       in1=XG[:, j:j + 2, D:D + 1].rearrange("p j o -> p (j o)"), op0=ALU.mult, op1=ALU.add)
                V.tensor_tensor(MT[:, 1, :], MT[:, 0, :], XG[:, j:j + 2, D + 3:D + 4].rearrange("p j o -> p (j o)"),
                                ALU.mult).then_inc(meta_step, 1)
                dve.wait_ge(meta_step, q * 2 + 2)
                V.tensor_tensor(GATE[:, j:j + 2], MT[:, 1, :], XG[:, j:j + 2, D + 2:D + 3].rearrange("p j o -> p (j o)"),
                                ALU.add).then_inc(meta, 1)

            def split_h(j, v, first=False):
                dve.wait_ge(sq_ev, j + 1)
                if not first:
                    dve.wait_ge(y_mm, j - 1)
                V.tensor_copy(HHL[:, v % 2, 0, :], H32[:, v % 2, :]).then_inc(h_cp, 1)
                dve.wait_ge(h_cp, j + 1)
                V.tensor_tensor(HHL[:, v % 2, 1, :], H32[:, v % 2, :], HHL[:, v % 2, 0, :], ALU.subtract).then_inc(h_ev, 1)

            def dve_step(s, k, pair=None):
                known = isinstance(s, int)
                if not known or s < NS:
                    rows_out(s, k, first=known and s < 2)
                    if k % 2 == 1:
                        pair_meta(s // 2 if known else pair, k // 2)
                if not known or 0 <= s - 2 < NS:
                    split_h(s - 2, (k - 2) % 8, first=known and s - 2 < 2)

            C_STEPS = 5

            def sum_rows(n, u):
                row = ds(n, 1) if not isinstance(n, int) else slice(n, n + 1)
                dve.wait_ge(s_yg[u], 16 * (n // 4 + 1) if isinstance(n, int) else (n - u) * 4 + 16)
                if not (isinstance(n, int) and n < 4):
                    dve.wait_ge(c_out, n - 3)
                c = n * C_STEPS
                V.tensor_tensor(SF[:, u, :], XH[:, row, 0:D].rearrange("p o d -> p (o d)"),
                                XH[:, row, D:2 * D].rearrange("p o d -> p (o d)"), ALU.add).then_inc(c_step, 1)
                dve.wait_ge(c_step, c + 1)
                V.tensor_tensor(SF[:, u, :], SF[:, u, :], YG[:, u, 0, :], ALU.add).then_inc(c_step, 1)
                dve.wait_ge(c_step, c + 2)
                V.tensor_tensor(SF[:, u, :], SF[:, u, :], YG[:, u, 1, :], ALU.add).then_inc(c_step, 1)
                dve.wait_ge(c_step, c + 3)
                V.bn_stats(C6[:, u, :], SF[:, u, :]).then_inc(c_step, 1)
                dve.wait_ge(c_step, c + 4)
                V.tensor_copy(CW[:, u, 5:6], C6[:, u, 0:1])
                V.bn_aggr(CV[:, u, :], C6[:, u, :]).then_inc(c_step, 1)
                dve.wait_ge(c_step, c + 5)
                V.tensor_scalar(CW[:, u, 0:1], CV[:, u, 1:2], EPS_LN * XS * XS, None, ALU.add).then_inc(c_var, 1)

            def sum_scale(n, u):
                c = n * 5

                def w(k):
                    return CW[:, u, k:k + 1]

                dve.wait_ge(c_sd, n + 1)
                dve.wait_ge(c_var, n + 1)
                V.reciprocal(w(2), w(1)).then_inc(cn_step, 1)
                dve.wait_ge(cn_step, c + 1)
                V.tensor_tensor(w(3), w(2), w(2), ALU.mult).then_inc(cn_step, 1)
                dve.wait_ge(cn_step, c + 2)
                V.tensor_tensor(w(4), w(3), w(0), ALU.mult).then_inc(cn_step, 1)
                dve.wait_ge(cn_step, c + 3)
                V.tensor_scalar(w(5), w(4), -0.5, 1.5, ALU.mult, ALU.add).then_inc(cn_step, 1)
                dve.wait_ge(cn_step, c + 4)
                V.tensor_tensor(w(6), w(2), w(5), ALU.mult).then_inc(cn_step, 1)
                dve.wait_ge(cn_step, c + 5)
                V.scalar_tensor_tensor(out=w(7), in0=w(6), scalar=-1.0, in1=CV[:, u, 0:1], op0=ALU.mult, op1=ALU.mult).then_inc(c_rs, 1)

            for s in range(8):
                dve_step(s, s)
            with dve.Fori(1, ST // 8 + 1) as i:
                for k in range(8):
                    dve_step(i * 8 + k, k, pair=i * 4 + k // 2)

            def with_output(i, n):
                for k in range(8):
                    dve_step(i * 8 + k, k, pair=i * 4 + k // 2)
                    (sum_rows if k % 2 == 0 else sum_scale)(n + k // 2, k // 2)

            with_output(ST // 8 + 1, 0)
            with dve.Fori(1, NT // 4) as i:
                with_output(i + (ST // 8 + 1), i * 4)
            for s in range(NS, NS + 3):
                dve_step(s, s % 8)

            def sum_results(g):
                y = YW[g // 4][:, g % 4, :, :, :]
                dve.wait_ge(s_yt[g % 2], 32 * (g // 2 + 1))
                V.tensor_tensor(y[:, 0, :, :], y[:, 0, :, :], y[:, 1, :, :], ALU.add).then_inc(y_sum, 1)

            def out_stats(g):
                gi, u = B * NG + g, g % 2
                for t in range(GT):
                    dve.wait_ge(o_mm, g * GT + t + 1)
                    last = V.bn_stats(ST6[:, u, t, :], PS[:, 4 * u + t, 0:D])
                last.then_inc(st_step, 1)
                dve.wait_ge(st_step, gi * 2 + 1)
                for t in range(GT):
                    last = V.bn_aggr(MV[:, u, t, :], ST6[:, u, t, :])
                last.then_inc(st_step, 1)
                dve.wait_ge(st_step, gi * 2 + 2)
                V.tensor_scalar(VAR[:, g * GT:(g + 1) * GT], MV[:, u, :, 1:2].rearrange("p t o -> p (t o)"), EPS_LN * XS * XS, None,
                                ALU.add).then_inc(var_rdy, 1)

            sum_results(0)
            for g in range(NG):
                if g + 1 < NG:
                    sum_results(g + 1)
                out_stats(g)
                if g >= 1:
                    inverse_std(B, g - 1, 1.0)
            inverse_std(B, NG - 1, 1.0)


_INS = ["L0_attn_x", "L0_attn_W_qkv", "L0_attn_W_out", "L0_attn_b_out", "L0_ffn_router_w", "L0_ffn_w1", "L0_ffn_w2"]
_OUTS = [((2, 4096, 256), "float32")]


def kernel(**inputs):
    import numpy as _np
    import concourse.bacc as _bacc
    from concourse import mybir as _mybir
    from concourse.bass_utils import run_bass_kernel_spmd as _run

    nc = _bacc.Bacc("TRN2", target_bir_lowering=False, num_devices=1)
    arrays, args = {}, []
    for name in _INS:
        a = _np.ascontiguousarray(inputs[name])
        arrays[f"in_{name}_dram"] = a
        args.append(nc.dram_tensor(f"in_{name}_dram", a.shape, _mybir.dt.from_np(a.dtype), kind="ExternalInput").ap())
    for i, (shape, dtype) in enumerate(_OUTS):
        args.append(nc.dram_tensor(f"out_{i}_dram", shape, _mybir.dt.from_np(_np.dtype(dtype)), kind="ExternalOutput").ap())
    linear_attention_then_top2_experts(nc, *args)
    r = _run(nc, [arrays], core_ids=[0])
    return r.results[0]["out_0_dram"]
```

```python
import concourse.bass as bass
from concourse import mybir
from contextlib import ExitStack


def linear_attention_then_top2_experts(nc, x_in, w_qkv, w_out, b_out, router_w, w1_in, w2_in, out):
    f32, f32r, f16, bf16, i32 = mybir.dt.float32, mybir.dt.float32r, mybir.dt.float16, mybir.dt.bfloat16, mybir.dt.int32
    ALU = mybir.AluOpType
    ACT = mybir.ActivationFunctionType
    AX = mybir.AxisListType
    ds = bass.ds

    P = 128
    B, T, D = x_in.shape
    E, _, H = w1_in.shape
    DC, HC = D // P, H // P
    NT = T // P
    GT = 4
    NG = NT // GT
    ST = 2 * NT + E - 1
    NS = B * ST
    DR = D + E
    DEN = DR
    EW = DC * 2 * H
    ROW = D + 4
    EPS, EPS_LN = 1e-6, 1e-5
    XS = 2048.0
    R_SCALE = 2.0 ** -27
    TINY = 2.0 ** -100
    FAR = float(1 << 20)

    xf = x_in.rearrange("b (n p) d -> p (b n) d", p=P)
    of = out.rearrange("b (n p) d -> p (b n) d", p=P)
    x_slots = nc.dram_tensor("x_slots", (NS * P, ROW), f32, kind="Internal").ap()
    y_rows = nc.dram_tensor("y_rows", (2 * B * T, D), f32, kind="Internal").ap()
    xs_v = x_slots.rearrange("(j p) c -> p j c", p=P)
    yr_v = y_rows.rearrange("(k n p) d -> p k n d", k=2, p=P)

    ctx = ExitStack()
    with ctx:
        def sb(name, shape, dt):
            return ctx.enter_context(nc.sbuf_tensor(name, shape, dt))

        def sem(name):
            return ctx.enter_context(nc.semaphore(name))

        X = sb("X", [P, B * NT, ROW], f32)
        XH = X[:, :, :].bitcast(f16)
        W1 = sb("W1", [P, E, DC, 2, H], f16)
        W2 = sb("W2", [P, E, HC, 2, D], f16)
        W1f = W1[:, :, :, :, :].rearrange("p e c s h -> p (e c s h)")
        W2f = W2[:, :, :, :, :].rearrange("p e c s h -> p (e c s h)")
        STG = sb("STG", [P, 2, 1024], f32)
        ST2 = [STG[:, :, :].rearrange("p k (a d) -> p (k a) d", d=D), X[:, (B * NG - 2) * GT:B * NG * GT, 0:D]]
        X1 = STG[:, :, :].rearrange("p u (t d) -> p u t d", t=GT)
        Qb = sb("Qb", [P, DC * T], f32)
        Q = Qb[:, :].rearrange("p (c t) -> p c t", c=DC)
        RQK = Qb[:, T // 2:T // 2 + 4 * D].rearrange("p (a d) -> p a d", a=4)
        RR = Qb[0:E, 3 * T // 4:3 * T // 4 + D]
        W1w, W2w = W1f.bitcast(f32), W2f.bitcast(f32)
        EWw = W1w.shape[1] // E
        RVO = W1w[:, (E - 1) * EWw:E * EWw].rearrange("p (a d) -> p a d", a=4)
        XT = sb("XT", [P, 2, DC, GT * P], f32r)
        KS = sb("KS", [P, 2, GT, D], f32)
        WKR = sb("WKR", [P, 2, DC, DR], f32r)
        WQT = sb("WQT", [P, 2, DC, D], f32r)
        WOT = W2w[:, (E - 1) * EWw:(E - 1) * EWw + DC * DR].rearrange("p (c d) -> p c d", c=DC)
        G = sb("G", [P, DC, DR], f32)
        RT = sb("RT", [P, DC, E], f32)
        MQ = sb("MQ", [P, DC, DR + 2], f32)
        KXS = STG[:, :, :].rearrange("p k w -> p (k w)")[:, 0:DC * (D + 2)].rearrange("p (c d) -> p c d", c=DC)
        KXT = KS[:, 0, 0:DC, :]
        ID = sb("ID", [P, P], f32)
        ID16 = sb("ID16", [P, P], f16)
        UPPER = sb("UPPER", [P, P], bf16)
        ONESB = sb("ONESB", [P, P], bf16)
        BB = sb("BB", [P, D], f32)
        BCOL = sb("BCOL", [P, DC], f32)
        LB = W2w[:, (E - 2) * EWw:(E - 2) * EWw + 2 * D].rearrange("p (n c k) -> p n c k", n=2, c=DC)
        SRBR = sb("SRBR", [P, 2, E], f32)
        PADROW = sb("PADROW", [P, ROW], f32)
        XR = sb("XR", [P, B, NT, E], f32)
        ZL = sb("ZL", [P, GT, E], f32)
        MEAN = sb("MEAN", [P, NT], f32)
        VAR = sb("VAR", [P, NT], f32)
        SD = sb("SD", [P, NT], f32)
        RSTD = sb("RSTD", [P, NT], f32)
        ZT = sb("ZT", [P, 2, GT], f32)
        ZR = sb("ZR", [P, 2, GT], f32)
        ST6 = sb("ST6", [P, 2, GT, 6], f32)
        MV = sb("MV", [P, 2, GT, 2], f32)
        NW = sb("NW", [P, 4, GT], f32)
        RS2 = sb("RS2", [P, 2, GT], f32)
        NB = sb("NB", [P, 2, GT], f32)
        AM = sb("AM", [P, 2], f32)
        AMX = sb("AMX", [P, 2], f32)
        P2 = sb("P2", [P, E, 2], f32)
        PW = sb("PW", [P, 2], f32)
        SG = sb("SG", [P, 2, 2], f32)
        KAP = sb("KAP", [P, E], f32)
        STW = STG[:, :, :].rearrange("p k w -> p (k w)")
        TN = NT * E
        SMALL = STW[:, 0:12 * NT].rearrange("p (k t) -> p k t", t=NT)
        MX, CM, SL, GA = SMALL[:, 0:2, :], SMALL[:, 2:4, :], SMALL[:, 4:6, :], SMALL[:, 6:12, :]
        AT = 12 * NT
        TA = STW[:, AT:AT + TN].rearrange("p (t e) -> p t e", e=E)
        TB = STW[:, AT + TN:AT + 2 * TN].rearrange("p (t e) -> p t e", e=E)
        CMP = STW[:, AT:AT + ST * E].rearrange("p (j e) -> p j e", e=E)
        assert AT + max(2 * TN, ST * E) <= GT * D
        OH = STW[:, 4 * TN:6 * TN].rearrange("p (k t e) -> p k t e", k=2, e=E)
        SI = STW[:, 6 * TN:7 * TN].rearrange("p (e t) -> p e t", e=E)
        SX = STW[:, 7 * TN:8 * TN].rearrange("p (e t) -> p e t", e=E)
        MK = sb("MK", [P, E, NT], bf16)
        ONE = sb("ONE", [P, 1], f32)
        IDX = sb("IDX", [P, B, 2, NT], i32)
        CNT = sb("CNT", [P, E], f32)
        CI = sb("CI", [P, E], i32)
        NTL = sb("NTL", [P, E], f32)
        TBI = sb("TBI", [P, E], f32)
        TBX = sb("TBX", [P, E], f32)
        OFF = sb("OFF", [P, E], f32)
        PD = sb("PD", [P, 3, E], f32)
        PIDX = sb("PIDX", [P, B, E], i32)
        SE = sb("SE", [P, E], f32)
        EIDF = sb("EIDF", [P, NS], f32)
        EID = sb("EID", [P, NS], i32)
        REV = sb("REV", [P, E], f32)
        TOK = sb("TOK", [P, B * NT], f32)
        JROW = sb("JROW", [P, ST], f32)
        PCOL = sb("PCOL", [P, 1], f32)
        MT = sb("MT", [P, 2, 2], f32)
        YID = sb("YID", [P, 8, 1], i32)
        GATE = sb("GATE", [P, 8], f32)
        cut = [0]

        def region(words):
            a = cut[0]
            cut[0] += words
            return Qb[:, a:a + words]

        XG = region(8 * ROW).rearrange("p (j c) -> p j c", j=8)
        XGH = XG.bitcast(f16)
        XTF = region(2 * DC * P).bitcast(f16).rearrange("p (u s) -> p u s", u=2)
        RL = region(2 * H).rearrange("p (u h) -> p u h", u=2)
        H32 = region(2 * H).rearrange("p (u h) -> p u h", u=2)
        HHL = region(2 * H).bitcast(f16).rearrange("p (u s h) -> p u s h", u=2, s=2)
        YS = region(4 * D).rearrange("p (j d) -> p j d", j=4)
        C6 = region(4 * 6).rearrange("p (u d) -> p u d", u=4)
        CV = region(4 * 2).rearrange("p (u d) -> p u d", u=4)
        CW = region(4 * 8).rearrange("p (u d) -> p u d", u=4)
        YG = KS[:, :, :, :].rearrange("p u t d -> p (u t d)").rearrange("p (u k d) -> p u k d", u=4, k=2)
        SF = STW[:, 0:4 * D].rearrange("p (u d) -> p u d", u=4)
        OF = STW[:, 4 * D:8 * D].rearrange("p (u d) -> p u d", u=4)
        assert cut[0] <= DC * T
        YW = [w.bitcast(f32).rearrange("p (g k t d) -> p g k t d", g=NG // 2, k=2, t=GT) for w in (W1f, W2f)]

        PEEL = 24
        COUNT_STEP = 8
        OUT_ROUND = ST // 8 + 2
        assert 8 * OUT_ROUND >= ST + 8 and NS // 8 == OUT_ROUND + NT // 4 - 1

        PS = ctx.enter_context(nc.psum_tensor("PS", [P, 8, 512], f32))
        PS16 = PS[:, :, :].bitcast(f16)
        COUNTS = slice(512 - E * NT, 512)

        s_raw, s_late, s_bias = sem("s_raw"), sem("s_late"), sem("s_bias")
        s_x = [sem(f"s_x{i}") for i in range(4)]
        s_w = [[sem(f"s_w{u}{k}") for k in range(2)] for u in range(2)]
        s_tail = sem("s_tail")
        const_done, pool_chain, setup_chain = sem("const_done"), sem("pool_chain"), sem("setup_chain")
        set_mm, set_ev = sem("set_mm"), sem("set_ev")
        xt_mm, xt_ev, xl_ev, k_mm, k_ev, q_mm, q_ev, kx_mm, b_add = (sem(n) for n in (
            "xt_mm", "xt_ev", "xl_ev", "k_mm", "k_ev", "q_mm", "q_ev", "kx_mm", "b_add"))
        m_mm, m_ev = sem("m_mm"), sem("m_ev")
        w_max, w_all, w_scale, w_scaled, w_hi, w_lo, w_step = (sem(n) for n in ("w_max", "w_all", "w_scale", "w_scaled", "w_hi", "w_lo", "w_step"))
        u_mm, z_step, x2_pair, x2_done, st_done, mv_done, var_rdy, sd_rdy, nw_step, rs_rdy, x1_rdy, hi_rdy, lo_rdy = (sem(n) for n in (
            "u_mm", "z_step", "x2_pair", "x2_done", "st_done", "mv_done", "var_rdy", "sd_rdy", "nw_step", "rs_rdy", "x1_rdy", "hi_rdy", "lo_rdy"))
        r_step, ex_in, ex_out, mask_rdy, cnt_mm, cnt_used, r_done = (sem(n) for n in (
            "r_step", "ex_in", "ex_out", "mask_rdy", "cnt_mm", "cnt_used", "r_done"))
        s_scat = [sem(f"s_scat{b}") for b in range(B)]
        s_g = [sem(f"s_g{i}") for i in range(4)]
        t_mm, t_ev, z_mm, z_ev, rt_mm, sq_ev, h_cp, h_ev, y_mm, y_ev, meta, meta_step = (sem(n) for n in (
            "t_mm", "t_ev", "z_mm", "z_ev", "rt_mm", "sq_ev", "h_cp", "h_ev", "y_mm", "y_ev", "meta", "meta_step"))
        s_y = [sem(f"s_y{i}") for i in range(4)]
        s_yg = [sem(f"s_yg{i}") for i in range(4)]
        s_o = [sem(f"s_o{i}") for i in range(4)]
        c_step, c_var, c_sd, cn_step, c_rs, c_out = (sem(n) for n in ("c_step", "c_var", "c_sd", "cn_step", "c_rs", "c_out"))
        s_yt = [sem(f"s_yt{i}") for i in range(2)]
        s_ot = [sem(f"s_ot{i}") for i in range(2)]
        yg_step, y_sum, o_mm = sem("yg_step"), sem("y_sum"), sem("o_mm")
        kap_step, b_own, zl_step, xr_done = sem("kap_step"), sem("b_own"), sem("zl_step"), sem("xr_done")
        pad_rdy, eid_rdy, y_sum0 = sem("pad_rdy"), sem("eid_rdy"), sem("y_sum0")

        block = ctx.enter_context(nc.Block())

        PAIRS = NT // 2
        GAPS = 5
        GAP_K2 = 5
        MIX = PAIRS // GAPS
        assert PAIRS == GAPS * MIX + 1

        def mixed(gi):
            return isinstance(gi, int) and NG <= gi < NG + MIX

        def pairs_of(g):
            return range(min(GAPS * g, PAIRS), min(GAPS * (g + 1), PAIRS))

        def parts_of(e, u, k):
            W, C = ((W1, DC), (W2, HC))[k]
            staged = ST2[u][:, 4 * k:4 * k + 4, :].rearrange("p (c a) d -> p c a d", c=C)
            return staged, *(W[:, ds(e, 1), :, s, :].rearrange("p o c (a d) -> p (o c) a d", d=D) for s in range(2))

        def each_group(eng, body):
            body(0, 0)
            body(1, 1)
            with eng.Fori(1, NG // 2) as i:
                for u in range(2):
                    body(i * 2 + u, u)

        @block.sync
        def _(sp):
            sp.dma_start(RQK[:, :, :], w_qkv[0:2 * D, :].rearrange("(a p) d -> p a d", p=P)).then_inc(s_raw, 16)
            sp.dma_start(RR[:, :], router_w).then_inc(s_raw, 16)
            for g in range(2):
                sp.dma_start(X[:, g * GT:(g + 1) * GT, 0:D], xf[:, g * GT:(g + 1) * GT, :]).then_inc(s_x[g], 16)
            sp.dma_start(BCOL[:, :], b_out.rearrange("(c p) -> p c", p=P), allow_slow_non_contiguous=True).then_inc(s_bias, 16)
            sp.dma_start(BB[:, :], b_out.rearrange("(o d) -> o d", o=1).broadcast_to([P, D])).then_inc(s_bias, 16)

            def load_expert(e, u, wait=True):
                if wait:
                    sp.wait_ge(w_lo, 2 * e - 2)
                for c in range(DC):
                    sp.dma_start(ST2[u][:, 2 * c:2 * c + 2, :],
                                 w1_in[ds(e, 1), c * P:(c + 1) * P, :].rearrange("o p (a d) -> p (o a) d", d=D)).then_inc(s_w[u][0], 16)
                sp.dma_start(ST2[u][:, HC:2 * HC, :],
                             w2_in[ds(e, 1), :, :].rearrange("o (c p) h -> p (o c) h", p=P)).then_inc(s_w[u][1], 16)

            load_expert(0, 0, False)
            load_expert(1, 1, False)
            sp.dma_start(RVO[:, 0:2, :], w_qkv[2 * D:3 * D, :].rearrange("(a p) d -> p a d", p=P)).then_inc(s_late, 16)
            sp.dma_start(RVO[:, 2:4, :], w_out.rearrange("(a p) d -> p a d", p=P)).then_inc(s_late, 16)
            for g in range(2, 4):
                sp.dma_start(X[:, g * GT:(g + 1) * GT, 0:D], xf[:, g * GT:(g + 1) * GT, :]).then_inc(s_x[g], 16)

            def load_x(gi):
                k = gi % 4
                sp.wait_ge(s_x[k], gi // 4 * 16)
                sp.dma_start(X[:, gi * GT:(gi + 1) * GT, 0:D], xf[:, gi * GT:(gi + 1) * GT, :]).then_inc(s_x[k], 16)

            for gi in range(4, B * NG - 2):
                load_x(gi)
            with sp.Fori(1, E // 2) as i:
                for u in range(2):
                    load_expert(i * 2 + u, u)
            sp.wait_ge(w_lo, 2 * E)
            for gi in range(B * NG - 2, B * NG):
                load_x(gi)

            sp.wait_ge(const_done, 1)
            for b in range(B):
                for j in range(E - 1):
                    sp.dma_start(xs_v[:, b * ST + 2 * NT + j, :], PADROW[:, :]).then_inc(s_tail, 16)

            sp.wait_ge(s_scat[0], 16 * (2 * NT + E))
            sp.wait_ge(u_mm, B * NT)

            def results(n, v):
                return 16 * len(range(v, n, 4))

            def load_pair(q, v, wait=True):
                if wait:
                    sp.wait_ge(meta, q - 3)
                sp.dma_start(XG[:, 2 * v:2 * v + 2, :], xs_v[:, ds(q * 2, 2), :]).then_inc(s_g[v], 16)

            for v in range(4):
                load_pair(v, v, False)
            with sp.Fori(1, ST // 8) as i:
                for v in range(4):
                    load_pair(i * 4 + v, v)
            for q in range(ST // 8 * 4, ST // 2):
                load_pair(q, q % 4)
            sp.wait_ge(s_scat[1], 16 * (2 * NT + E))

            def load_rows(n, u, wait=True):
                if wait:
                    sp.wait_ge(c_step, n * 3 - 11)
                sp.dma_start(YG[:, u, :, :], yr_v[:, :, ds(n, 1), :].rearrange("p k o d -> p k (o d)")).then_inc(s_yg[u], 16)

            def store_rows(n, u):
                sp.wait_ge(c_out, n + 1)
                sp.dma_start(of[:, ds(n, 1), :].rearrange("p o d -> p (o d)"), OF[:, u, :]).then_inc(s_o[u], 16)

            OUT_PAIR = OUT_ROUND * 4
            for q in range(ST // 2, OUT_PAIR + 3):
                load_pair(q, q % 4)
            for v in range(4):
                sp.wait_ge(s_y[v], results(ST, v))
            for n in range(4):
                load_rows(n, n, False)
            load_pair(OUT_PAIR + 3, 3)

            def output_round(i):
                for v in range(4):
                    q = i * 4 + (OUT_PAIR + v)
                    if not isinstance(i, int) or q < NS // 2:
                        load_pair(q, v)
                    store_rows(i * 4 + (v - 4), v)
                    load_rows(i * 4 + v, v)

            with sp.Fori(1, NT // 4 - 1) as i:
                output_round(i)
            output_round(NT // 4 - 1)
            for v in range(4):
                store_rows(NT - 4 + v, v)
            for v in range(4):
                sp.wait_ge(s_y[v], results(NS, v))
            sp.wait_ge(y_mm, NS)

            def store_group(g):
                sp.wait_ge(x1_rdy, (B * NG + g) + 1)
                sp.dma_start(of[:, NT + g * GT:NT + (g + 1) * GT, :], KS[:, g % 2, :, :]).then_inc(s_ot[g % 2], 16)

            for g in range(NG):
                if g >= 2:
                    sp.wait_ge(s_yt[g % 2], 32 * (g // 2))
                for k in range(2):
                    sp.dma_start(YW[g // 4][:, g % 4, k, :, :],
                                 yr_v[:, k, NT + g * GT:NT + (g + 1) * GT, :]).then_inc(s_yt[g % 2], 16)
                if g >= 3:
                    store_group(g - 3)
            for g in range(NG - 3, NG):
                store_group(g)
            for v in range(4):
                sp.wait_ge(s_o[v], 16 * NT // 4)
            for v in range(2):
                sp.wait_ge(s_ot[v], 16 * NG // 2)

        @block.gpsimd
        def _(pool):
            nc.gpsimd.memset(ID[:], 0.0)
            nc.gpsimd.memset(UPPER[:], 1.0)
            nc.gpsimd.memset(PADROW[:], 0.0).then_inc(pool_chain, 1)
            pool.wait_ge(pool_chain, 1)
            nc.gpsimd.affine_select(out=ID[:], in_=ID[:], compare_op=ALU.not_equal, fill=1.0, base=0,
                                    pattern=[[-1, P]], channel_multiplier=1)
            nc.gpsimd.affine_select(out=UPPER[:], in_=UPPER[:], compare_op=ALU.is_gt, fill=0.0, base=0,
                                    pattern=[[1, P]], channel_multiplier=-1)
            nc.gpsimd.memset(PADROW[:, D:D + 1], FAR)
            nc.gpsimd.memset(PADROW[:, D + 1:D + 2], -1.0)
            nc.gpsimd.iota(REV[:], [[-1, E]], base=E, channel_multiplier=0, allow_small_or_imprecise_dtypes=True)
            nc.gpsimd.iota(TOK[:], [[P, B * NT]], base=0, channel_multiplier=1, allow_small_or_imprecise_dtypes=True)
            nc.gpsimd.iota(JROW[:], [[1, ST]], base=0, channel_multiplier=0, allow_small_or_imprecise_dtypes=True)
            nc.gpsimd.iota(PCOL[:], [[0, 1]], base=0, channel_multiplier=1,
                           allow_small_or_imprecise_dtypes=True).then_inc(const_done, 1)

            def add_bias(gi):
                pool.wait_ge(kx_mm, gi + 1)
                nc.gpsimd.tensor_tensor(X[:, gi * GT:(gi + 1) * GT, 0:D], X[:, gi * GT:(gi + 1) * GT, 0:D],
                                        BB[:, :].rearrange("p (o d) -> p o d", o=1).broadcast_to([P, GT, D]), ALU.add).then_inc(b_add, 1)

            for e in range(E):
                pool.wait_ge(w_max, e * 2 + 2)
                nc.gpsimd.partition_all_reduce(AMX[:, :], AM[:, :], P, bass.bass_isa.ReduceOp.absmax).then_inc(w_all, 1)
                if e >= 1:
                    add_bias(e - 1)
                for k in range(2):
                    staged, high, low = parts_of(e, e % 2, k)
                    pool.wait_ge(w_hi, 2 * e + k + 1)
                    nc.gpsimd.tensor_tensor(low, staged, high, ALU.subtract).then_inc(w_lo, 1)
            add_bias(NG - 1)

            def low_part(g):
                pool.wait_ge(hi_rdy, g + 1)
                nc.gpsimd.tensor_tensor(XH[:, g * GT:(g + 1) * GT, D:2 * D], X1[:, g % 2, :, :],
                                        XH[:, g * GT:(g + 1) * GT, 0:D], ALU.subtract).then_inc(lo_rdy, 1)

            for g in range(MIX + 1):
                for p in pairs_of(g):
                    if p % 2 == 0 and p >= 2:
                        low_part(p // 2 - 1)
                if g == MIX:
                    low_part(NG - 1)
                add_bias(NG + g)

            def scatter_tile(b, t, k):
                nc.gpsimd.indirect_dma_start(
                    out=x_slots, out_offset=bass.IndirectOffsetOnAxis(ap=IDX[:, b, k, t:t + 1], axis=0),
                    in_=X[:, t + b * NT, :], in_offset=None).then_inc(s_scat[b], 16)

            def scatter_padding(b):
                pool.wait_ge(pad_rdy, b + 1)
                for e in range(E):
                    nc.gpsimd.indirect_dma_start(
                        out=x_slots, out_offset=bass.IndirectOffsetOnAxis(ap=PIDX[:, b, e:e + 1], axis=0),
                        in_=PADROW[:, :], in_offset=None, bounds_check=NS * P - 1, oob_is_err=False).then_inc(s_scat[b], 16)

            def scatter_result(j, v):
                pool.wait_ge(y_ev, j + 1)
                nc.gpsimd.indirect_dma_start(
                    out=y_rows, out_offset=bass.IndirectOffsetOnAxis(ap=YID[:, j % 8, :], axis=0),
                    in_=YS[:, v, :], in_offset=None, bounds_check=last_row, oob_is_err=False).then_inc(s_y[v], 16)

            last_row = pool.to_reg(2 * B * T - 1)
            pool.wait_ge(s_tail, B * (E - 1) * 16)
            pool.wait_ge(r_done, 1)
            for t in range(NT):
                for k in range(2):
                    scatter_tile(0, t, k)
            scatter_padding(0)
            EARLY = 14
            for j in range(EARLY):
                scatter_result(j, j % 4)
            pool.wait_ge(r_done, 2)
            scatter_padding(1)
            j = EARLY
            for t in range(NT):
                for k in range(2):
                    scatter_tile(1, t, k)
                for k in range(2 if t % 4 == 3 else 1):
                    scatter_result(j, j % 4)
                    j += 1
            for j in range(j, NS):
                scatter_result(j, j % 4)
                n = (j - (8 * OUT_ROUND - 4)) // 2
                if j % 2 == 0 and 0 <= n < NT:
                    u = n % 4
                    pool.wait_ge(s_yg[u], 16 * (n // 4 + 1))
                    nc.gpsimd.tensor_tensor(YG[:, u, 0, :], YG[:, u, 0, :], YG[:, u, 1, :], ALU.add).then_inc(yg_step, 1)
                    pool.wait_ge(yg_step, 2 * n + 1)
                    nc.gpsimd.tensor_tensor(YG[:, u, 1, :], XH[:, n, 0:D], XH[:, n, D:2 * D], ALU.add).then_inc(yg_step, 1)
            for g in range(1, NG):
                y = YW[g // 4][:, g % 4, :, :, :]
                pool.wait_ge(s_yt[g % 2], 32 * (g // 2 + 1))
                nc.gpsimd.tensor_tensor(y[:, 0, :, :], y[:, 0, :, :], y[:, 1, :, :], ALU.add).then_inc(y_sum, 1)

        @block.tensor
        def _(pe):
            def transpose_rows(bank, rows):
                for a in range(2):
                    for c in range(DC):
                        last = nc.tensor.transpose(PS[:, bank, c * D + a * P:c * D + (a + 1) * P], rows[:, a, c * P:(c + 1) * P], ID[:])
                last.then_inc(set_mm, 1)

            pe.wait_ge(const_done, 1)
            pe.wait_ge(s_raw, 32)
            transpose_rows(6, RQK[:, 2:4, :])
            for c in range(DC):
                last = nc.tensor.transpose(PS[:, 5, c * E:(c + 1) * E], RR[:, c * P:(c + 1) * P], ID[0:E, 0:E])
            last.then_inc(set_mm, 1)
            transpose_rows(7, RQK[:, 0:2, :])

            def setup_after_0():
                pe.wait_ge(s_late, 32)
                pe.wait_ge(set_ev, 4)
                pe.wait_ge(q_ev, 2)
                for n in range(2):
                    for f in range(DC):
                        nc.tensor.matmul(PS[:, 5, n * E:(n + 1) * E], LB[:, n, f, :], RT[:, f, :],
                                         start=(f == 0), stop=(f == DC - 1))
                transpose_rows(4, RVO[:, 2:4, :])

            def setup_after_1():
                pe.wait_ge(q_ev, 4)
                for e in range(DC):
                    for f in range(DC):
                        last = nc.tensor.matmul(PS[:, 4, e * E:(e + 1) * E], RVO[:, 2 + f, e * P:(e + 1) * P], RT[:, f, :],
                                                start=(f == 0), stop=(f == DC - 1))
                last.then_inc(set_mm, 1)
                pe.wait_ge(set_ev, 6)
                for c in range(DC):
                    for e in range(DC):
                        last = nc.tensor.matmul(PS[:, 4 + c, 0:DR], RVO[:, e, c * P:(c + 1) * P], WOT[:, e, :],
                                                start=(e == 0), stop=(e == DC - 1))
                last.then_inc(set_mm, 1)

            def transpose_x(gi, k):
                pe.wait_ge(s_x[k], 16 * (gi // 4 + 1) if isinstance(gi, int) else (gi - k) * 4 + 16)
                for c in range(DC):
                    for t in range(GT):
                        last = nc.tensor.transpose(PS[:, c, t * P:(t + 1) * P],
                                                   X[:, ds(gi * GT + t, 1), c * P:(c + 1) * P].rearrange("p o c -> p (o c)"), ID[:])
                    last.then_inc(xt_mm, 1)

            THREE = ((0, 0), (0, 1), (1, 0))

            def apply_pair(p):
                if p >= 1:
                    pe.wait_ge(x2_pair, p)
                if p % GAPS == GAPS - 1:
                    pe.wait_ge(xt_ev, (NG + p // GAPS) * 2 + 4)
                    pe.wait_ge(xl_ev, (NG + p // GAPS) * 2 + 4)
                for k in range(2):
                    t = p * 2 + k
                    for m in range(DC):
                        last = nc.tensor.matmul(PS[:, k, 0:DR + 1], Q[:, m, t * P:(t + 1) * P], MQ[:, m, 0:DR + 1],
                                                start=(m == 0), stop=(m == DC - 1))
                    last.then_inc(u_mm, 1)

            def project(gi, u, gap=lambda k: None):
                g, first = gi % NG, gi == 0
                pe.wait_ge(xt_ev, gi * 2 + 2)
                pe.wait_ge(xl_ev, gi * 2 + 2)
                for t in range(GT):
                    if not (first and t < 2):
                        pe.wait_ge(k_ev, gi * GT + (t - 1))
                    n = 0
                    for c in range(DC):
                        for xp, wp in THREE:
                            last = nc.tensor.matmul(PS[:, 2 + t % 2, 0:DR], XT[:, xp, c, t * P:(t + 1) * P], WKR[:, wp, c, :],
                                                    start=(n == 0), stop=(n == 3 * DC - 1))
                            n += 1
                    last.then_inc(k_mm, 1)
                    if t % 2 == 1:
                        gap(t // 2)
                for m in range(DC):
                    if not first:
                        pe.wait_ge(q_ev, gi * 2 + (m - 1))
                    if gi in (1, 2) and m == 0:
                        pe.wait_ge(set_ev, 3 + 2 * gi)
                    n = 0
                    for c in range(DC):
                        for wp, xp in THREE:
                            last = nc.tensor.matmul(PS[:, 4 + m, :], WQT[:, wp, c, m * P:(m + 1) * P], XT[:, xp, c, :],
                                                    start=(n == 0), stop=(n == 3 * DC - 1))
                            n += 1
                    last.then_inc(q_mm, 1)
                    gap(2 + m)
                if not mixed(gi) and gi + 1 < B * NG:
                    if gi == NG + MIX:
                        pe.wait_ge(x2_pair, PAIRS)
                    if gi == NG + MIX + 1:
                        pe.wait_ge(cnt_used, 1)
                    transpose_x(gi + 1, (gi + 1) % 4)
                for t in range(GT):
                    pe.wait_ge(k_ev, gi * GT + (t + 1))
                    for m in range(DC):
                        last = nc.tensor.matmul(PS[:, 6 + m, 0:D + 2], KS[:, u, t, m * P:(m + 1) * P], X[:, gi * GT + t, 0:D + 2],
                                                start=(g == 0 and t == 0), stop=(g == NG - 1 and t == GT - 1), skip_group_check=True)
                    if t == 1 and mixed(gi):
                        pe.wait_ge(x2_pair, GAPS * (g + 1) - 1)
                        transpose_x(gi + 1, (gi + 1) % 4)
                last.then_inc(kx_mm, 1)
                gap(4)

            def attention_sums(b):
                g0 = b * NG
                if b == 0:
                    transpose_x(0, 0)
                    pe.wait_ge(set_ev, 3)
                for g in range(g0, g0 + NG):
                    if b == 1 and g - g0 <= MIX:
                        own = pairs_of(g - g0)
                        project(g, g % 2, gap=lambda k: apply_pair(own[k]) if k < len(own) else None)
                    elif b == 1 and g - g0 == MIX + 1:
                        project(g, g % 2, gap=lambda k: count_slots(0) if k == 1 else None)
                    else:
                        project(g, g % 2)
                        if g == 0:
                            setup_after_0()
                        if g == 1:
                            setup_after_1()
                pe.wait_ge(m_ev, 3 * b + 1)
                for m in range(DC):
                    for c in range(DC):
                        last = nc.tensor.transpose(PS[:, 0, c * D + m * P:c * D + (m + 1) * P], KXS[:, m, c * P:(c + 1) * P], ID[:])
                last.then_inc(m_mm, 1)
                pe.wait_ge(m_ev, 3 * b + 2)
                for m in range(DC):
                    for c in range(DC):
                        last = nc.tensor.matmul(PS[:, 1 + m, 0:DR], KXT[:, c, m * P:(m + 1) * P], G[:, c, :],
                                                start=(c == 0), stop=(c == DC - 1))
                last.then_inc(m_mm, 1)
                pe.wait_ge(m_ev, 3 * b + 3)

            def apply_m(b):
                for g in range(NG):
                    if g >= 2:
                        pe.wait_ge(x2_done, g - 1)
                    for t in range(GT):
                        for m in range(DC):
                            last = nc.tensor.matmul(PS[:, 4 * (g % 2) + t, 0:DR + 1], Q[:, m, (g * GT + t) * P:(g * GT + t + 1) * P],
                                                    MQ[:, m, 0:DR + 1], start=(m == 0), stop=(m == DC - 1))
                        last.then_inc(u_mm, 1)

            def count_slots(b):
                pe.wait_ge(mask_rdy, b + 1)
                nc.tensor.matmul(PS[:, 0, COUNTS], UPPER[:], MK[:, :, :].rearrange("p e t -> p (e t)"), start=True, stop=True)
                nc.tensor.matmul(PS[:, 1, COUNTS], ONESB[:], MK[:, :, :].rearrange("p e t -> p (e t)"),
                                 start=True, stop=True).then_inc(cnt_mm, 1)

            attention_sums(0)
            attention_sums(1)
            apply_m(1)
            pe.wait_ge(x2_done, NG)

            pe.wait_ge(eid_rdy, 1)
            pe.wait_ge(w_lo, 2 * E)
            pe.wait_ge(w_hi, 2 * E)

            def slots_transpose(j, v, first=False):
                if v % 2 == 0:
                    pe.wait_ge(s_g[v // 2], 16 * (j // 8 + 1) if isinstance(j, int) else (j - v) * 2 + 16)
                if not first:
                    pe.wait_ge(t_ev, j - 1)
                for c in range(DC):
                    for s in range(2):
                        last = nc.tensor.transpose(PS16[:, v % 2, (2 * c + s) * P:(2 * c + s + 1) * P],
                                                   XGH[:, v, s * D + c * P:s * D + (c + 1) * P], ID16[:])
                last.then_inc(t_mm, 1)

            def first_product(j, v, w, first=False):
                pe.wait_ge(t_ev, j + 1)
                if not first:
                    pe.wait_ge(z_ev, j - 1)
                n = 0
                for c in range(DC):
                    for xp, wp in THREE:
                        last = nc.tensor.matmul(PS[:, 2 + v % 2, :], XTF[:, v % 2, (2 * c + xp) * P:(2 * c + xp + 1) * P],
                                                W1f[:, ds(w + (2 * c + wp) * H, H)],
                                                start=(n == 0), stop=(n == 3 * DC - 1))
                        n += 1
                last.then_inc(z_mm, 1)

            def relu_transpose(j, v, first=False):
                pe.wait_ge(z_ev, j + 1)
                if not first:
                    pe.wait_ge(sq_ev, j - 1)
                for c in range(HC):
                    last = nc.tensor.transpose(PS[:, 4 + v % 2, c * P:(c + 1) * P], RL[:, v % 2, c * P:(c + 1) * P], ID[:])
                last.then_inc(rt_mm, 1)

            def second_product(j, v, w, first=False):
                pe.wait_ge(h_ev, j + 1)
                if not first:
                    pe.wait_ge(y_ev, j - 1)
                n = 0
                for c in range(HC):
                    for hp, wp in THREE:
                        last = nc.tensor.matmul(PS[:, 6 + v % 2, 0:D], HHL[:, v % 2, hp, c * P:(c + 1) * P],
                                                W2f[:, ds(w + (2 * c + wp) * D, D)],
                                                start=(n == 0), stop=(n == 3 * HC - 1))
                        n += 1
                last.then_inc(y_mm, 1)

            def weights_of(first, n):
                return nc.values_load_multi_w_load_instructions(
                    EID[0:1, ds(first, n)], engines=[mybir.EngineType.PE], min_val=0, max_val=(E - 1) * EW,
                    skip_runtime_bounds_check_because="route() counts from 1 to E experts at or before each tile")[1]

            def step(s, k, w1, w2):
                known = isinstance(s, int)
                if known and s == COUNT_STEP + 1:
                    pe.wait_ge(cnt_used, 2)
                if not known or s < NS:
                    slots_transpose(s, k, first=known and s < 2)
                if not known or 0 <= s - 1 < NS:
                    first_product(s - 1, (k - 1) % 8, w1, first=known and s - 1 < 2)
                if not known or 0 <= s - 2 < NS:
                    relu_transpose(s - 2, (k - 2) % 8, first=known and s - 2 < 2)
                if known and s == COUNT_STEP:
                    pe.wait_ge(t_ev, s + 1)
                    count_slots(1)
                if not known or 0 <= s - 3 < NS:
                    second_product(s - 3, (k - 3) % 8, w2, first=known and s - 3 < 2)

            for i in range(PEEL // 8):
                first = max(8 * i - 3, 0)
                w = weights_of(first, 8 * i + 7 - first)
                for s in range(8 * i, 8 * i + 8):
                    step(s, s % 8, w[max(s - 1, 0) - first], w[max(s - 3, 0) - first])
            ROUNDS = NS // 8
            with pe.Fori(PEEL // 8, ROUNDS) as i:
                w = weights_of(i * 8 - 3, 10)
                for k in range(8):
                    step(i * 8 + k, k, w[k + 2], w[k])
            first = ROUNDS * 8 - 3
            w = weights_of(first, NS - first)
            for s in range(ROUNDS * 8, NS + 3):
                step(s, s % 8, w[min(s - 1, NS - 1) - first], w[s - 3 - first])

            pe.wait_ge(y_ev, NS)
            for g in range(NG):
                if g >= 2:
                    pe.wait_ge(x1_rdy, B * NG + g - 1)
                if g == 0:
                    pe.wait_ge(y_sum0, 1)
                else:
                    pe.wait_ge(y_sum, g)
                for t in range(GT):
                    n, bank = NT + g * GT + t, PS[:, 4 * (g % 2) + t, 0:D]
                    nc.tensor.matmul(bank, ID16[:], XH[:, n, 0:D], start=True, stop=False)
                    nc.tensor.matmul(bank, ID16[:], XH[:, n, D:2 * D], start=False, stop=False)
                    nc.tensor.matmul(bank, ID[:], YW[g // 4][:, g % 4, 0, t, :], start=False, stop=True).then_inc(o_mm, 1)

        @block.scalar
        def _(act):
            def sums_part(gi):
                for c in range(DC):
                    act.wait_ge(xt_mm, gi * 2 + (c + 1))
                    nc.scalar.copy(XT[:, 0, c, :], PS[:, c, :]).then_inc(xt_ev, 1)

            def expert_part(e, u, k):
                act.wait_ge(w_scale, e + 1)
                staged, high, low = parts_of(e, u, k)
                nc.scalar.activation(staged, staged, ACT.Copy, scale=SG[:, 0, k:k + 1]).then_inc(w_scaled, 1)
                act.wait_ge(w_scaled, e * 2 + (k + 1))
                nc.scalar.copy(high, staged).then_inc(w_hi, 1)

            def norm_sqrt(gi):
                act.wait_ge(var_rdy, gi + 1)
                own = slice(gi % NG * GT, (gi % NG + 1) * GT)
                nc.scalar.activation(SD[:, own], VAR[:, own], ACT.Sqrt).then_inc(sd_rdy, 1)

            def norm_x1(gi):
                u = gi % 2
                act.wait_ge(rs_rdy, gi + 1)
                if gi >= 2:
                    act.wait_ge(lo_rdy, gi - 1)
                for t in range(GT):
                    last = nc.scalar.activation(X1[:, u, t, :], X[:, gi * GT + t, 0:D],
                                                ACT.Identity, bias=NB[:, u, t:t + 1], scale=RS2[:, u, t:t + 1])
                last.then_inc(x1_rdy, 1)

            def norm_high(gi):
                act.wait_ge(x1_rdy, gi + 1)
                nc.scalar.copy(XH[:, gi * GT:(gi + 1) * GT, 0:D], X1[:, gi % 2, :, :]).then_inc(hi_rdy, 1)

            def norm_apply(gi):
                norm_x1(gi)
                norm_high(gi)

            def gate_exp(b):
                act.wait_ge(ex_in, b + 1)
                nc.scalar.activation(GA[:, 1, :], GA[:, 0, :], ACT.Exp).then_inc(ex_out, 1)

            sums_part(0)
            with act.Fori(0, NG // 2) as i:
                for u in range(2):
                    expert_part(i * 2 + u, u, 0)
                    sums_part(i * 2 + (u + 1))
                    expert_part(i * 2 + u, u, 1)

            def norm_beside(pairs):
                for p in pairs:
                    if p >= PAIRS:
                        continue
                    if p % 2 == 1:
                        norm_sqrt(p // 2)
                    elif p >= 2:
                        norm_apply(p // 2 - 1)

            for g in range(NG):
                norm_beside(range(GAPS * g, GAPS * g + 3))
                if g == MIX:
                    norm_x1(NG - 1)
                if g + 1 < NG:
                    sums_part(NG + g + 1)
                if g == MIX:
                    norm_high(NG - 1)
                norm_beside(range(GAPS * g + 3, GAPS * g + 5))
                if g == MIX + 1:
                    gate_exp(0)
            norm_sqrt(NG)
            for g in range(1, NG):
                norm_sqrt(NG + g)
                norm_apply(NG + g - 1)
            norm_apply(2 * NG - 1)

            def act_relu(j, v):
                act.wait_ge(z_mm, j + 1)
                if not (isinstance(j, int) and j < 2):
                    act.wait_ge(rt_mm, j - 1)
                nc.scalar.activation(RL[:, v % 2, :], PS[:, 2 + v % 2, :], ACT.Relu, scale=R_SCALE).then_inc(z_ev, 1)

            def act_square(j, v):
                act.wait_ge(rt_mm, j + 1)
                if not (isinstance(j, int) and j < 2):
                    act.wait_ge(h_ev, j - 1)
                nc.scalar.activation(H32[:, v % 2, :], PS[:, 4 + v % 2, :], ACT.Square).then_inc(sq_ev, 1)

            def act_step(s, k, pair=None):
                known = isinstance(s, int)
                if not known or 0 <= s - 1 < NS:
                    act_relu(s - 1, (k - 1) % 8)
                if not known or 0 <= s - 2 < NS:
                    act_square(s - 2, (k - 2) % 8)
                if not known or 0 <= s - 3 < NS:
                    j, v = s - 3, (k - 3) % 8
                    act.wait_ge(y_mm, j + 1)
                    if v % 2 == 0:
                        act.wait_ge(meta, j // 2 + 1 if known else pair)
                    if not (known and j < 4):
                        act.wait_ge(s_y[v % 4], 16 * (j // 4) if known else (j - v % 4) * 4)
                    nc.scalar.activation(YS[:, v % 4, :], PS[:, 6 + v % 2, 0:D], ACT.Copy, scale=GATE[:, v:v + 1]).then_inc(y_ev, 1)

            def out_sqrt(n, u):
                act.wait_ge(c_var, n + 1)
                nc.scalar.activation(CW[:, u, 1:2], CW[:, u, 0:1], ACT.Sqrt).then_inc(c_sd, 1)

            def out_apply(n, u):
                act.wait_ge(c_rs, n + 1)
                if not (isinstance(n, int) and n < 4):
                    act.wait_ge(s_o[u], 16 * (n // 4) if isinstance(n, int) else (n - u) * 4)
                nc.scalar.activation(OF[:, u, :], SF[:, u, :], ACT.Identity, bias=CW[:, u, 7:8], scale=CW[:, u, 6:7]).then_inc(c_out, 1)

            for s in range(PEEL):
                act_step(s, s % 8)
                if s == COUNT_STEP:
                    gate_exp(1)
            with act.Fori(PEEL // 8, OUT_ROUND) as i:
                for k in range(8):
                    act_step(i * 8 + k, k, pair=i * 4 + ((k - 3) // 2 + 1))

            def with_output(i, n, first=False):
                for k in range(8):
                    act_step(i * 8 + k, k, pair=i * 4 + ((k - 3) // 2 + 1))
                    if k % 2 == 1:
                        out_sqrt(n + k // 2, k // 2)
                    elif not (first and k == 0):
                        out_apply(n + (k // 2 - 1), (k // 2 - 1) % 4)

            with_output(OUT_ROUND, 0, True)
            with act.Fori(1, NT // 4 - 1) as i:
                with_output(i + OUT_ROUND, i * 4)
            with_output(NT // 4 - 1 + OUT_ROUND, NT - 4)
            out_apply(NT - 1, 3)
            for s in range(8 * OUT_ROUND + 2 * NT, NS + 3):
                act_step(s, s % 8)

            def out_group(g):
                u = g % 2
                act.wait_ge(rs_rdy, B * NG + g + 1)
                if g >= 2:
                    act.wait_ge(s_ot[u], 16 * (g // 2))
                for t in range(GT):
                    last = nc.scalar.activation(KS[:, u, t, :], PS[:, 4 * u + t, 0:D], ACT.Identity,
                                                bias=NB[:, u, t:t + 1], scale=RS2[:, u, t:t + 1])
                last.then_inc(x1_rdy, 1)

            for g in range(NG):
                norm_sqrt(B * NG + g)
                out_group(g)

        @block.vector
        def _(dve):
            V = nc.vector

            def bc(ap, shape):
                return ap.broadcast_to(shape)

            nc.vector.memset(ONESB[:], 1.0)
            nc.vector.memset(ONE[:], 1.0)
            nc.vector.memset(X[:, :, D:D + 1], 1.0)
            nc.vector.memset(X[:, :, D + 1:D + 2], 0.0)
            dve.wait_ge(const_done, 1)
            V.tensor_copy(ID16[:], ID[:]).then_inc(setup_chain, 1)

            def two(bank):
                return PS[:, bank, :].rearrange("p (c d) -> p c d", c=DC)

            def router_part(bank):
                return PS[:, bank, 0:DC * E].rearrange("p (c d) -> p c d", c=DC)

            dve.wait_ge(set_mm, 1)
            V.tensor_copy(WKR[:, 0, :, 0:D], two(6)).then_inc(setup_chain, 1)
            dve.wait_ge(setup_chain, 2)
            V.tensor_tensor(WKR[:, 1, :, 0:D], two(6), WKR[:, 0, :, 0:D], ALU.subtract).then_inc(set_ev, 1)
            dve.wait_ge(set_mm, 2)
            V.tensor_copy(WKR[:, 0, :, D:DR], router_part(5)).then_inc(setup_chain, 1)
            dve.wait_ge(setup_chain, 3)
            V.tensor_tensor(WKR[:, 1, :, D:DR], router_part(5), WKR[:, 0, :, D:DR], ALU.subtract)
            V.tensor_copy(RT[:, :, :], router_part(5)).then_inc(set_ev, 1)
            dve.wait_ge(set_mm, 3)
            V.tensor_copy(WQT[:, 0, :, :], two(7)).then_inc(setup_chain, 1)
            dve.wait_ge(setup_chain, 4)
            V.tensor_tensor(WQT[:, 1, :, :], two(7), WQT[:, 0, :, :], ALU.subtract).then_inc(set_ev, 1)
            nc.vector.memset(LB[:, 0, :, :], 1.0)
            dve.wait_ge(s_bias, 32)
            V.tensor_copy(LB[:, 1, :, :], bc(BCOL[:, :].rearrange("p (c o) -> p c o", o=1), [P, DC, P])).then_inc(set_ev, 1)

            def setup_after_0():
                dve.wait_ge(set_mm, 4)
                V.tensor_copy(SRBR[:, :, :], PS[:, 5, 0:2 * E].rearrange("p (n e) -> p n e", n=2))
                V.tensor_copy(WOT[:, :, 0:D], two(4)).then_inc(set_ev, 1)

            def setup_after_1():
                dve.wait_ge(set_mm, 5)
                V.tensor_copy(WOT[:, :, D:DR], router_part(4)).then_inc(set_ev, 1)
                dve.wait_ge(set_mm, 6)
                V.tensor_copy(G[:, :, :], PS[:, 4:4 + DC, 0:DR]).then_inc(set_ev, 1)

            def expert_max(e, u, k):
                n = (32, 16)[k]
                dve.wait_ge(s_w[u][k], n * (e // 2 + 1) if isinstance(e, int) else (e - u) * (n // 2) + n)
                if k == 0 and not (isinstance(e, int) and e == 0):
                    dve.wait_ge(w_all, e)
                V.tensor_reduce(AM[:, k:k + 1], ST2[u][:, 4 * k:4 * k + 4, :], AX.XY, ALU.max, apply_absolute_value=True).then_inc(w_max, 1)

            def expert_scale(e):
                dve.wait_ge(w_all, e + 1)
                p2 = P2[:, ds(e, 1), :].rearrange("p o k -> p (o k)")
                V.tensor_scalar(AMX[:, :], AMX[:, :], TINY, None, ALU.max).then_inc(w_step, 1)
                dve.wait_ge(w_step, e * 3 + 1)
                V.tensor_scalar(PW[:, :].bitcast(i32), AMX[:, :].bitcast(i32), 0x7F800000, None, ALU.bitwise_and).then_inc(w_step, 1)
                dve.wait_ge(w_step, e * 3 + 2)
                V.reciprocal(SG[:, 1, :], PW[:, :]).then_inc(w_step, 1)
                V.tensor_copy(p2, PW[:, :])
                dve.wait_ge(w_step, e * 3 + 3)
                if not (isinstance(e, int) and e == 0):
                    dve.wait_ge(w_hi, e * 2)
                V.tensor_scalar(SG[:, 0, :], SG[:, 1, :], 2.0 ** 14, None, ALU.mult).then_inc(w_scale, 1)

            def expert_gap(gi, u, k):
                if k == 0:
                    expert_max(gi, u, 0)
                if k == GAP_K2:
                    expert_max(gi, u, 1)
                if k == 1:
                    expert_scale(gi)
                if k == 4 and isinstance(gi, int):
                    (setup_after_0, setup_after_1)[gi]()

            def low_x(gi):
                for c in range(DC):
                    dve.wait_ge(xt_ev, gi * 2 + (c + 1))
                    V.tensor_tensor(XT[:, 1, c, :], PS[:, c, :], XT[:, 0, c, :], ALU.subtract).then_inc(xl_ev, 1)

            low_x(0)

            def sums_part(gi, u, b, gap):
                first = isinstance(gi, int) and gi < 2
                for t in range(GT):
                    dve.wait_ge(k_mm, gi * GT + (t + 1))
                    if t == 0 and not first:
                        dve.wait_ge(kx_mm, gi - 1)
                    V.tensor_copy(XR[:, b, ds((gi - b * NG) * GT + t, 1), :].rearrange("p o e -> p (o e)"), PS[:, 2 + t % 2, D:DR])
                    V.tensor_scalar(KS[:, u, t, :], PS[:, 2 + t % 2, 0:D], 0.0, EPS, ALU.max, ALU.add).then_inc(k_ev, 1)
                    if t >= 1:
                        gap(gi, GAP_K2 if t == 2 else t // 2)
                for m in range(DC):
                    dve.wait_ge(q_mm, gi * 2 + (m + 1))
                    V.tensor_scalar(Q[:, m, ds((gi - b * NG) * (GT * P), GT * P)], PS[:, 4 + m, :], 0.0, EPS,
                                    ALU.max, ALU.add).then_inc(q_ev, 1)
                    if m == 0 or mixed(gi):
                        gap(gi, 2 + m)
                if not (isinstance(gi, int) and gi == B * NG - 1):
                    low_x(gi + 1)
                if not mixed(gi):
                    gap(gi, 3)
                gap(gi, 4)

            def make_m(b):
                dve.wait_ge(kx_mm, (b + 1) * NG)
                if b == 0:
                    dve.wait_ge(w_lo, 2 * E - 2)
                else:
                    dve.wait_ge(r_done, 1)
                    dve.wait_ge(eid_rdy, 1)
                V.tensor_copy(KXS[:, :, :], PS[:, 6:6 + DC, 0:D + 2]).then_inc(m_ev, 1)
                dve.wait_ge(m_mm, 2 * b + 1)
                V.tensor_copy(KXT[:, :, :], PS[:, 0, :].rearrange("p (c d) -> p c d", c=DC)).then_inc(m_ev, 1)
                dve.wait_ge(m_mm, 2 * b + 2)
                V.tensor_copy(MQ[:, :, DEN:DEN + 1], KXS[:, :, D:D + 1])
                V.tensor_copy(MQ[:, :, 0:DR], PS[:, 1:1 + DC, 0:DR]).then_inc(m_ev, 1)

            def own_of(g):
                return slice(g * GT, (g + 1) * GT)

            def mean_var(gi, eps=EPS_LN):
                g, u = gi % NG, gi % 2
                dve.wait_ge(st_done, gi + 1)
                for t in range(GT):
                    last = V.bn_aggr(MV[:, u, t, :], ST6[:, u, t, :])
                last.then_inc(mv_done, 1)
                dve.wait_ge(mv_done, gi + 1)
                V.tensor_scalar(VAR[:, own_of(g)], MV[:, u, :, 1:2].rearrange("p t o -> p (t o)"), eps, None,
                                ALU.add).then_inc(var_rdy, 1)

            def pair_stats(p):
                dve.wait_ge(x2_pair, p + 1)
                for t in (2 * p, 2 * p + 1):
                    last = V.bn_stats(ST6[:, p // 2 % 2, t % GT, :], X[:, t, 0:D])
                if p % 2 == 1:
                    last.then_inc(st_done, 1)

            def residual_pair(p):
                v = p % 2
                dve.wait_ge(u_mm, 2 * p + 2)
                V.tensor_scalar(ZT[:, v, 0:2], PS[:, 0:2, DEN:DEN + 1].rearrange("p t o -> p (t o)"), EPS, None, ALU.add).then_inc(z_step, 1)
                dve.wait_ge(z_step, 2 * p + 1)
                V.reciprocal(ZR[:, v, 0:2], ZT[:, v, 0:2]).then_inc(z_step, 1)
                dve.wait_ge(z_step, 2 * p + 2)
                dve.wait_ge(b_add, p // 2 + 1)
                V.tensor_tensor(ZL[:, 0:2, :], PS[:, 0:2, D:DR],
                                bc(ZR[:, v, 0:2].rearrange("p (t o) -> p t o", o=1), [P, 2, E]), ALU.mult).then_inc(zl_step, 1)
                for k in range(2):
                    x = X[:, 2 * p + k, 0:D]
                    last = V.scalar_tensor_tensor(out=x, in0=PS[:, k, 0:D], scalar=ZR[:, v, k:k + 1], in1=x,
                                                  op0=ALU.mult, op1=ALU.add)
                last.then_inc(x2_pair, 1)
                dve.wait_ge(zl_step, p + 1)
                V.tensor_tensor(XR[:, 0, 2 * p:2 * p + 2, :], XR[:, 0, 2 * p:2 * p + 2, :], ZL[:, 0:2, :], ALU.add).then_inc(xr_done, 1)
                if v == 0 and p >= 2:
                    inverse_std(0, p // 2 - 1, beside=lambda t: pair_stats(p) if t == 0 else None)
                else:
                    pair_stats(p)
                if v == 1:
                    mean_var(p // 2)

            def residual_group(g):
                gi, u = NG + g, g % 2
                dve.wait_ge(u_mm, gi * GT + GT)
                V.tensor_scalar(ZT[:, u, :], PS[:, 4 * u:4 * u + GT, DEN:DEN + 1].rearrange("p t o -> p (t o)"), EPS, None,
                                ALU.add).then_inc(z_step, 1)
                if g >= 3:
                    low_part(gi - 3)
                dve.wait_ge(z_step, 2 * PAIRS + g * 2 + 1)
                V.reciprocal(ZR[:, u, :], ZT[:, u, :]).then_inc(z_step, 1)
                dve.wait_ge(z_step, 2 * PAIRS + g * 2 + 2)
                if gi <= NG + MIX:
                    dve.wait_ge(b_add, gi + 1)
                else:
                    dve.wait_ge(b_own, gi - NG - MIX)
                V.tensor_tensor(ZL[:, :, :], PS[:, 4 * u:4 * u + GT, D:DR],
                                bc(ZR[:, u, :].rearrange("p (t o) -> p t o", o=1), [P, GT, E]), ALU.mult).then_inc(zl_step, 1)
                for t in range(GT):
                    x = X[:, gi * GT + t, 0:D]
                    last = V.scalar_tensor_tensor(out=x, in0=PS[:, 4 * u + t, 0:D], scalar=ZR[:, u, t:t + 1], in1=x,
                                                  op0=ALU.mult, op1=ALU.add)
                last.then_inc(x2_done, 1)
                dve.wait_ge(zl_step, PAIRS + g + 1)
                V.tensor_tensor(XR[:, 1, own_of(g), :], XR[:, 1, own_of(g), :], ZL[:, :, :], ALU.add).then_inc(xr_done, 1)

                def stats(t):
                    dve.wait_ge(x2_done, g + 1)
                    last = V.bn_stats(ST6[:, u, t, :], X[:, gi * GT + t, 0:D])
                    if t == GT - 1:
                        last.then_inc(st_done, 1)

                if g == 0:
                    for t in range(GT):
                        stats(t)
                else:
                    inverse_std(1, g - 1, beside=stats)
                mean_var(gi)

            def inverse_std(b, g, scale=XS, beside=lambda t: None):
                gi, u = b * NG + g, g % 2
                own = own_of(g)
                n = [gi * 5]

                def then(ins, t=None):
                    ins.then_inc(nw_step, 1)
                    n[0] += 1
                    if t is not None:
                        beside(t)
                    dve.wait_ge(nw_step, n[0])

                dve.wait_ge(sd_rdy, gi + 1)
                then(V.reciprocal(NW[:, 0, :], SD[:, own]), 0)
                then(V.tensor_tensor(NW[:, 1, :], NW[:, 0, :], NW[:, 0, :], ALU.mult), 1)
                then(V.tensor_tensor(NW[:, 2, :], NW[:, 1, :], VAR[:, own], ALU.mult), 2)
                then(V.tensor_scalar(NW[:, 3, :], NW[:, 2, :], -0.5, 1.5, ALU.mult, ALU.add), 3)
                if b < B:
                    V.tensor_copy(MEAN[:, own], MV[:, u, :, 0:1].rearrange("p t o -> p (t o)"))
                    V.tensor_tensor(RSTD[:, own], NW[:, 0, :], NW[:, 3, :], ALU.mult)
                then(V.scalar_tensor_tensor(out=RS2[:, u, :], in0=NW[:, 0, :], scalar=scale, in1=NW[:, 3, :],
                                            op0=ALU.mult, op1=ALU.mult))
                V.scalar_tensor_tensor(out=NB[:, u, :], in0=RS2[:, u, :], scalar=-1.0,
                                       in1=MV[:, u, :, 0:1].rearrange("p t o -> p (t o)"),
                                       op0=ALU.mult, op1=ALU.mult).then_inc(rs_rdy, 1)

            def low_part(gi):
                dve.wait_ge(hi_rdy, gi + 1)
                own = slice(gi * GT, (gi + 1) * GT)
                V.tensor_tensor(XH[:, own, D:2 * D], X1[:, gi % 2, :, :], XH[:, own, 0:D], ALU.subtract).then_inc(lo_rdy, 1)

            TE = [P, NT, E]
            r_n = [0]

            def then(ins):
                ins.then_inc(r_step, 1)
                r_n[0] += 1
                dve.wait_ge(r_step, r_n[0])

            def over_t(row):
                return bc(row.rearrange("p (o e) -> p o e", o=1), TE)

            def over_e(col):
                return bc(col.rearrange("p (t o) -> p t o", o=1), TE)

            def flat(a):
                return a.rearrange("p e t -> p (e t)")

            def gate_scales():
                V.scalar_tensor_tensor(out=KAP[:, :], in0=P2[:, :, 0:1].rearrange("p e o -> p (e o)"), scalar=XS * 2.0 ** -10,
                                       in1=P2[:, :, 0:1].rearrange("p e o -> p (e o)"), op0=ALU.mult, op1=ALU.mult).then_inc(kap_step, 1)
                dve.wait_ge(kap_step, 1)
                V.tensor_tensor(KAP[:, :], KAP[:, :], P2[:, :, 1:2].rearrange("p e o -> p (e o)"), ALU.mult).then_inc(kap_step, 1)
                dve.wait_ge(kap_step, 2)

            def route_logits_a(b):
                dve.wait_ge(rs_rdy, (b + 1) * NG)
                dve.wait_ge(lo_rdy, (b + 1) * NG - 1)
                dve.wait_ge(xr_done, PAIRS + b * NG)
                then(V.tensor_tensor(TA[:, :, :], XR[:, b, :, :], over_t(SRBR[:, 1, :]), ALU.add))

            def route_logits_b(b):
                then(V.tensor_tensor(TB[:, :, :], over_e(MEAN[:, :]), over_t(SRBR[:, 0, :]), ALU.mult))
                then(V.tensor_tensor(TA[:, :, :], TA[:, :, :], TB[:, :, :], ALU.subtract))
                then(V.tensor_tensor(TA[:, :, :], TA[:, :, :], over_e(RSTD[:, :]), ALU.mult))

            def route_choice_a(k):
                then(V.tensor_reduce(MX[:, k, :], TA[:, :, :], AX.X, ALU.max))
                then(V.tensor_tensor(TB[:, :, :], TA[:, :, :], over_e(MX[:, k, :]), ALU.is_equal))
                then(V.tensor_tensor(TB[:, :, :], TB[:, :, :], over_t(REV[:, :]), ALU.mult))

            def route_choice_b(b, k):
                if k == 0:
                    dve.wait_ge(lo_rdy, (b + 1) * NG)
                then(V.tensor_reduce(CM[:, k, :], TB[:, :, :], AX.X, ALU.max))
                then(V.tensor_tensor(OH[:, k, :, :], over_t(REV[:, :]), over_e(CM[:, k, :]), ALU.is_equal))
                if k == 0:
                    then(V.scalar_tensor_tensor(out=TA[:, :, :], in0=OH[:, 0, :, :], scalar=-3.0e38, in1=TA[:, :, :],
                                                op0=ALU.mult, op1=ALU.add))
                else:
                    V.tensor_tensor(MK[:, :, :].rearrange("p e t -> p t e"), OH[:, 0, :, :], OH[:, 1, :, :], ALU.add).then_inc(mask_rdy, 1)
                    V.tensor_tensor(GA[:, 0, :], MX[:, 1, :], MX[:, 0, :], ALU.subtract).then_inc(ex_in, 1)

            start_e = SX[:, :, 0:1].rearrange("p e o -> p (e o)")

            def route_counts(b):
                dve.wait_ge(cnt_mm, b + 1)
                then(V.tensor_tensor_scan(flat(SI[:, :, :]), ONE[:, 0:1].broadcast_to([P, E * NT]), PS[:, 1, COUNTS], 0.0, ALU.mult, ALU.add))
                then(V.tensor_tensor(flat(SX[:, :, :]), flat(SI[:, :, :]), PS[:, 1, COUNTS], ALU.subtract))
                V.tensor_copy(SE[:, :], start_e)
                then(V.tensor_tensor(CNT[:, :], SI[:, :, NT - 1:NT].rearrange("p e o -> p (e o)"), start_e, ALU.subtract))
                V.tensor_tensor(flat(SX[:, :, :]), flat(SX[:, :, :]), PS[:, 0, COUNTS], ALU.add).then_inc(cnt_used, 1)

            def route_slots_a(b):
                then(V.tensor_scalar(CI[:, :], CNT[:, :], float(P - 1), None, ALU.add))
                then(V.tensor_scalar(CI[:, :], CI[:, :], 7, None, ALU.arith_shift_right))
                then(V.tensor_copy(NTL[:, :], CI[:, :]))
                then(V.tensor_tensor_scan(TBI[:, :], ONE[:, 0:1].broadcast_to([P, E]), NTL[:, :], 0.0, ALU.mult, ALU.add))
                then(V.tensor_tensor(TBX[:, :], TBI[:, :], NTL[:, :], ALU.subtract))
                then(V.tensor_scalar(PD[:, 0, :], TBX[:, :], float(P), float(b * ST * P), ALU.mult, ALU.add))
                then(V.tensor_tensor(OFF[:, :], PD[:, 0, :], SE[:, :], ALU.subtract))
                dve.wait_ge(cnt_used, b + 1)

            def route_slots_b(b):
                then(V.tensor_tensor(TB[:, :, :], SX[:, :, :].rearrange("p e t -> p t e"), over_t(OFF[:, :]), ALU.add))
                then(V.tensor_tensor(TA[:, :, :], TB[:, :, :], OH[:, 0, :, :], ALU.mult))
                then(V.tensor_reduce(SL[:, 0, :], TA[:, :, :], AX.X, ALU.add))

            def route_slots_c(b):
                then(V.tensor_tensor(TA[:, :, :], TB[:, :, :], OH[:, 1, :, :], ALU.mult))
                then(V.tensor_reduce(SL[:, 1, :], TA[:, :, :], AX.X, ALU.add))
                V.tensor_copy(IDX[:, b, :, :], SL[:, :, :])

            def route_tables_a(b):
                then(V.tensor_tensor(PD[:, 1, :], CNT[:, :], PD[:, 0, :], ALU.add))
                then(V.tensor_scalar(PD[:, 1, :], PD[:, 1, :], PCOL[:, 0:1], None, ALU.add))
                then(V.scalar_tensor_tensor(out=PD[:, 2, :], in0=NTL[:, :], scalar=float(P), in1=PD[:, 0, :],
                                            op0=ALU.mult, op1=ALU.add))
                then(V.tensor_tensor(PD[:, 2, :], PD[:, 1, :], PD[:, 2, :], ALU.is_ge))
                V.scalar_tensor_tensor(out=PIDX[:, b, :], in0=PD[:, 2, :], scalar=FAR, in1=PD[:, 1, :], op0=ALU.mult, op1=ALU.add).then_inc(pad_rdy, 1)

            def route_tables_b(b):
                then(V.tensor_tensor(CMP[:, :, :], bc(JROW[:, :].rearrange("p (j o) -> p j o", o=1), [P, ST, E]),
                                     bc(TBX[:, :].rearrange("p (o e) -> p o e", o=1), [P, ST, E]), ALU.is_ge))
                own = slice(b * ST, (b + 1) * ST)
                then(V.tensor_reduce(EIDF[:, own], CMP[:, :, :], AX.X, ALU.add))
                then(V.tensor_scalar(EIDF[:, own], EIDF[:, own], -1.0, None, ALU.add))
                V.tensor_scalar(EID[:, own], EIDF[:, own], float(EW), None, ALU.mult).then_inc(eid_rdy, 1)

            def route_gates_a(b):
                dve.wait_ge(ex_out, b + 1)
                then(V.tensor_scalar(GA[:, 2, :], GA[:, 1, :], 1.0, None, ALU.add))
                then(V.reciprocal(GA[:, 3, :], GA[:, 2, :]))
                then(V.tensor_tensor(GA[:, 4, :], GA[:, 3, :], GA[:, 1, :], ALU.mult))

            def route_gates_b(k):
                then(V.tensor_tensor(TA[:, :, :], OH[:, k, :, :], over_t(KAP[:, :]), ALU.mult))
                then(V.tensor_reduce(SL[:, k, :], TA[:, :, :], AX.X, ALU.add))
                then(V.tensor_tensor(GA[:, 3 + k, :], GA[:, 3 + k, :], SL[:, k, :], ALU.mult))

            def route_rows(b):
                rows = slice(b * NT, (b + 1) * NT)

                def field(k):
                    return X[:, rows, D + k:D + k + 1].rearrange("p t o -> p (t o)")

                V.tensor_copy(field(0), TOK[:, rows])
                V.tensor_scalar(field(1), CM[:, 0, :], -1.0, float(E), ALU.mult, ALU.add)
                V.tensor_copy(field(2), GA[:, 3, :])
                V.tensor_tensor(field(3), GA[:, 4, :], GA[:, 3, :], ALU.subtract).then_inc(r_done, 1)

            def add_bias(gi):
                dve.wait_ge(kx_mm, gi + 1)
                own = slice(gi * GT, (gi + 1) * GT)
                V.tensor_tensor(X[:, own, 0:D], X[:, own, 0:D],
                                bc(BB[:, :].rearrange("p (o d) -> p o d", o=1), [P, GT, D]), ALU.add).then_inc(b_own, 1)

            each_group(dve, lambda gi, u: sums_part(gi, u, 0, lambda gi, k: expert_gap(gi, u, k)))
            make_m(0)

            def beside_sums(gi, k):
                g = gi - NG
                if k == GAP_K2:
                    return
                if g <= MIX and k < len(pairs_of(g)):
                    residual_pair(pairs_of(g)[k])
                elif g == MIX and k == 1:
                    gate_scales()
                    inverse_std(0, NG - 1)
                    route_logits_a(0)
                    route_logits_b(0)
                elif g == MIX and k == 2:
                    route_choice_a(0)
                elif g == MIX and k == 3:
                    route_choice_b(0, 0)
                    route_choice_a(1)
                elif g == MIX + 1 and k == 0:
                    route_choice_b(0, 1)
                elif g == MIX + 1 and k == 1:
                    route_counts(0)
                    route_slots_a(0)
                    route_slots_b(0)
                elif g == MIX + 1 and k == 2:
                    route_slots_c(0)
                    route_gates_a(0)
                elif g == MIX + 1 and k == 3:
                    route_gates_b(0)
                    route_gates_b(1)
                    route_rows(0)
                elif g == MIX + 2 and k in (1, 3):
                    (route_tables_a if k == 1 else route_tables_b)(0)
                elif g > MIX + 1 and k == 2:
                    add_bias(gi - 1)

            for g in range(NG):
                sums_part(NG + g, g % 2, 1, beside_sums)
            make_m(1)
            add_bias(2 * NG - 1)
            for g in range(NG):
                residual_group(g)
            low_part(2 * NG - 3)
            inverse_std(1, NG - 1)

            def rows_out(j, v, first=False):
                dve.wait_ge(t_mm, j + 1)
                if not first:
                    dve.wait_ge(z_mm, j - 1)
                V.tensor_copy(XTF[:, v % 2, :], PS16[:, v % 2, 0:2 * D]).then_inc(t_ev, 1)

            def pair_meta(q, v):
                j = 2 * v
                if not (isinstance(q, int) and q < 4):
                    dve.wait_ge(y_ev, q * 2 - 2)
                V.tensor_tensor(MT[:, 0, :], XG[:, j:j + 2, D + 1:D + 2].rearrange("p j o -> p (j o)"), EIDF[:, ds(q * 2, 2)],
                                ALU.not_equal).then_inc(meta_step, 1)
                dve.wait_ge(meta_step, q * 2 + 1)
                V.scalar_tensor_tensor(out=YID[:, j:j + 2, :].rearrange("p j o -> p (j o)"), in0=MT[:, 0, :], scalar=float(B * T),
                                       in1=XG[:, j:j + 2, D:D + 1].rearrange("p j o -> p (j o)"), op0=ALU.mult, op1=ALU.add)
                V.tensor_tensor(MT[:, 1, :], MT[:, 0, :], XG[:, j:j + 2, D + 3:D + 4].rearrange("p j o -> p (j o)"),
                                ALU.mult).then_inc(meta_step, 1)
                dve.wait_ge(meta_step, q * 2 + 2)
                V.tensor_tensor(GATE[:, j:j + 2], MT[:, 1, :], XG[:, j:j + 2, D + 2:D + 3].rearrange("p j o -> p (j o)"),
                                ALU.add).then_inc(meta, 1)

            def split_h(j, v, first=False):
                dve.wait_ge(sq_ev, j + 1)
                if not first:
                    dve.wait_ge(y_mm, j - 1)
                V.tensor_copy(HHL[:, v % 2, 0, :], H32[:, v % 2, :]).then_inc(h_cp, 1)
                dve.wait_ge(h_cp, j + 1)
                V.tensor_tensor(HHL[:, v % 2, 1, :], H32[:, v % 2, :], HHL[:, v % 2, 0, :], ALU.subtract).then_inc(h_ev, 1)

            def dve_step(s, k, pair=None):
                known = isinstance(s, int)
                if not known or s < NS:
                    rows_out(s, k, first=known and s < 2)
                    if k % 2 == 1:
                        pair_meta(s // 2 if known else pair, k // 2)
                if not known or 0 <= s - 2 < NS:
                    split_h(s - 2, (k - 2) % 8, first=known and s - 2 < 2)

            C_STEPS = 3

            def sum_rows(n, u):
                dve.wait_ge(yg_step, n * 2 + 2)
                if not (isinstance(n, int) and n < 4):
                    dve.wait_ge(c_out, n - 3)
                c = n * C_STEPS
                V.tensor_tensor(SF[:, u, :], YG[:, u, 0, :], YG[:, u, 1, :], ALU.add).then_inc(c_step, 1)
                dve.wait_ge(c_step, c + 1)
                V.bn_stats(C6[:, u, :], SF[:, u, :]).then_inc(c_step, 1)
                dve.wait_ge(c_step, c + 2)
                V.tensor_copy(CW[:, u, 5:6], C6[:, u, 0:1])
                V.bn_aggr(CV[:, u, :], C6[:, u, :]).then_inc(c_step, 1)
                dve.wait_ge(c_step, c + 3)
                V.tensor_scalar(CW[:, u, 0:1], CV[:, u, 1:2], EPS_LN * XS * XS, None, ALU.add).then_inc(c_var, 1)

            def sum_scale(n, u):
                c = n * 5

                def w(k):
                    return CW[:, u, k:k + 1]

                dve.wait_ge(c_sd, n + 1)
                dve.wait_ge(c_var, n + 1)
                V.reciprocal(w(2), w(1)).then_inc(cn_step, 1)
                dve.wait_ge(cn_step, c + 1)
                V.tensor_tensor(w(3), w(2), w(2), ALU.mult).then_inc(cn_step, 1)
                dve.wait_ge(cn_step, c + 2)
                V.tensor_tensor(w(4), w(3), w(0), ALU.mult).then_inc(cn_step, 1)
                dve.wait_ge(cn_step, c + 3)
                V.tensor_scalar(w(5), w(4), -0.5, 1.5, ALU.mult, ALU.add).then_inc(cn_step, 1)
                dve.wait_ge(cn_step, c + 4)
                V.tensor_tensor(w(6), w(2), w(5), ALU.mult).then_inc(cn_step, 1)
                dve.wait_ge(cn_step, c + 5)
                V.scalar_tensor_tensor(out=w(7), in0=w(6), scalar=-1.0, in1=CV[:, u, 0:1], op0=ALU.mult, op1=ALU.mult).then_inc(c_rs, 1)

            for s in range(PEEL):
                dve_step(s, s % 8)
                if s in (0, 1):
                    low_part(2 * NG - 2 + s)
                elif s == 2:
                    route_logits_a(1)
                elif s == 3:
                    route_logits_b(1)
                elif s in (4, 6):
                    route_choice_a(s // 2 - 2)
                elif s in (5, 7):
                    route_choice_b(1, s // 2 - 2)
                elif s == COUNT_STEP:
                    route_counts(1)
                elif s == COUNT_STEP + 1:
                    route_slots_a(1)
                elif s == COUNT_STEP + 2:
                    route_slots_b(1)
                elif s == COUNT_STEP + 3:
                    route_slots_c(1)
                elif s == COUNT_STEP + 4:
                    route_tables_a(1)
                elif s == COUNT_STEP + 5:
                    route_tables_b(1)
                elif s == COUNT_STEP + 6:
                    route_gates_a(1)
                elif s in (COUNT_STEP + 7, COUNT_STEP + 8):
                    route_gates_b(s - (COUNT_STEP + 7))
                    if s == COUNT_STEP + 8:
                        route_rows(1)
            with dve.Fori(PEEL // 8, OUT_ROUND) as i:
                for k in range(8):
                    dve_step(i * 8 + k, k, pair=i * 4 + k // 2)

            def with_output(i, n):
                for k in range(8):
                    dve_step(i * 8 + k, k, pair=i * 4 + k // 2)
                    (sum_rows if k % 2 == 0 else sum_scale)(n + k // 2, k // 2)

            with_output(OUT_ROUND, 0)
            with dve.Fori(1, NT // 4 - 1) as i:
                with_output(i + OUT_ROUND, i * 4)
            with_output(NT // 4 - 1 + OUT_ROUND, NT - 4)
            for s in range(8 * OUT_ROUND + 2 * NT, NS + 3):
                dve_step(s, s % 8)

            def out_stats(g):
                gi, u = B * NG + g, g % 2
                for t in range(GT):
                    dve.wait_ge(o_mm, g * GT + t + 1)
                    last = V.bn_stats(ST6[:, u, t, :], PS[:, 4 * u + t, 0:D])
                last.then_inc(st_done, 1)
                mean_var(gi, EPS_LN * XS * XS)

            dve.wait_ge(s_yt[0], 32)
            V.tensor_tensor(YW[0][:, 0, 0, :, :], YW[0][:, 0, 0, :, :], YW[0][:, 0, 1, :, :], ALU.add).then_inc(y_sum0, 1)
            for g in range(NG):
                out_stats(g)
                inverse_std(B, g, 1.0)


_INS = ["L0_attn_x", "L0_attn_W_qkv", "L0_attn_W_out", "L0_attn_b_out", "L0_ffn_router_w", "L0_ffn_w1", "L0_ffn_w2"]
_OUTS = [((2, 4096, 256), "float32")]


def kernel(**inputs):
    import numpy as _np
    import concourse.bacc as _bacc
    from concourse import mybir as _mybir
    from concourse.bass_utils import run_bass_kernel_spmd as _run

    nc = _bacc.Bacc("TRN2", target_bir_lowering=False, num_devices=1)
    arrays, args = {}, []
    for name in _INS:
        a = _np.ascontiguousarray(inputs[name])
        arrays[f"in_{name}_dram"] = a
        args.append(nc.dram_tensor(f"in_{name}_dram", a.shape, _mybir.dt.from_np(a.dtype), kind="ExternalInput").ap())
    for i, (shape, dtype) in enumerate(_OUTS):
        args.append(nc.dram_tensor(f"out_{i}_dram", shape, _mybir.dt.from_np(_np.dtype(dtype)), kind="ExternalOutput").ap())
    linear_attention_then_top2_experts(nc, *args)
    r = _run(nc, [arrays], core_ids=[0])
    return r.results[0]["out_0_dram"]
```
